# Optimizing a Trainium2 kernel written in Bass

```python
import numpy as np
import jax
import jax.numpy as jnp

def _softmax(x, axis=-1):
    return jax.nn.softmax(x, axis=axis)

def _gelu(x):
    return jax.nn.gelu(x, approximate=True)

def _silu(x):
    return jax.nn.silu(x)

def _sigmoid(x):
    return jax.nn.sigmoid(x)

def _layernorm(x, axis=-1, eps=1e-05):
    m = jnp.mean(x, axis=axis, keepdims=True)
    v = jnp.var(x, axis=axis, keepdims=True)
    return (x - m) / jnp.sqrt(v + eps)

def _scatter_add(tgt, idx, src, axis=0):
    return tgt.at[idx].add(src)

def _segment_sum(src, seg, n):
    return jax.ops.segment_sum(src, seg, n)
kernel_name = 'mk_xattn_ffn_d2_seqx_r8_2cb4d1'

def setup_inputs(seed: int=0):
    np.random.seed(seed)
    _w = jnp.asarray

    def _rec_inputs():
        import jax
        import jax.numpy as jnp
        _rk = jax.random.key(seed)
        x = 7.22e-05 + 1 * jax.random.normal(jax.random.fold_in(_rk, 1), (128, 64, 128), jnp.float32)
        _lenS = 64 - jax.random.randint(jax.random.fold_in(_rk, 7), (128,), 0, max(1, 64 // 4) + 1, jnp.int32)
        _lenS2 = 64 - jax.random.randint(jax.random.fold_in(_rk, 8), (128,), 0, max(1, 64 // 4) + 1, jnp.int32)
        _ctx_768P = jax.random.normal(jax.random.fold_in(_rk, 11), (128, 16, 96), jnp.float32)
        _ctx_768c = jax.random.dirichlet(jax.random.fold_in(_rk, 511), 0.3 * jnp.ones((16,), jnp.float32), (128, 64))
        _ctx_768t = jnp.einsum('bsk,bkd->bsd', _ctx_768c, _ctx_768P)
        _ctx_768t = _ctx_768t * jax.lax.rsqrt(jnp.mean(jnp.square(_ctx_768t)) + 1e-12) * 0.953939
        ctx_768 = 2.09791e-05 + 1.00001 * (_ctx_768t + 0.3 * jax.random.normal(jax.random.fold_in(_rk, 611), (128, 64, 96), jnp.float32))
        return (x, ctx_768)
    x, ctx_768 = _rec_inputs()

    def _L0_xattn_setup():
        import jax, jax.numpy as jnp
        import numpy as np
        NUM_HEADS = 16
        key = jax.random.key(seed)
        ks = jax.random.split(key, 8)
        dim, cond_dim = (128, 96)
        B, N, condN = (4, 256, 128)
        s = lambda k, shp, fan: jax.random.normal(k, shp, dtype=jnp.float32) * fan ** (-0.5)
        return {'x': jax.random.normal(ks[0], (B, N, dim), dtype=jnp.float32), 'cond': jax.random.normal(ks[1], (B, condN, cond_dim), dtype=jnp.float32), 'q_w': s(ks[2], (dim, dim), dim), 'q_b': jnp.zeros((dim,), jnp.float32), 'kv_w': s(ks[3], (cond_dim, 2 * dim), cond_dim), 'kv_b': jnp.zeros((2 * dim,), jnp.float32), 'proj_w': s(ks[4], (dim, dim), dim), 'proj_b': jnp.zeros((dim,), jnp.float32)}
    _L0_xattn_all = _L0_xattn_setup()
    _L0_xattn_in = {k: v for k, v in _L0_xattn_all.items() if k in ('q_w', 'q_b', 'kv_w', 'kv_b', 'proj_w', 'proj_b')}
    del _L0_xattn_all

    def _L0_ffn_setup():
        import jax, jax.numpy as jnp
        import numpy as np
        D_IN, D_HID = (128, 512)

        def _ternary(key, shape):
            return jax.random.randint(key, shape, -1, 2).astype(jnp.float32)

        def _tlin(x, w, s):
            return jnp.einsum('bsi,oi->bso', x, w) * s
        key = jax.random.key(seed)
        ks = jax.random.split(key, 12)
        inv = lambda fan: 1.0 / np.sqrt(fan).astype(np.float32)
        return {'x': jax.random.normal(ks[0], (4, 256, D_IN), dtype=jnp.float32), 'w1_w': _ternary(ks[1], (D_HID, D_IN)), 'w1_s': jax.random.uniform(ks[2], (D_HID,), dtype=jnp.float32) * inv(D_IN), 'w2_w': _ternary(ks[3], (D_HID, D_IN)), 'w2_s': jax.random.uniform(ks[4], (D_HID,), dtype=jnp.float32) * inv(D_IN), 'h1_w': _ternary(ks[5], (D_HID, D_HID)), 'h1_s': jax.random.uniform(ks[6], (D_HID,), dtype=jnp.float32) * inv(D_HID), 'h2_w': _ternary(ks[7], (D_HID, D_HID)), 'h2_s': jax.random.uniform(ks[8], (D_HID,), dtype=jnp.float32) * inv(D_HID), 'w3_w': _ternary(ks[9], (D_IN, D_HID)), 'w3_s': jax.random.uniform(ks[10], (D_IN,), dtype=jnp.float32) * inv(D_HID)}
    _L0_ffn_all = _L0_ffn_setup()
    _L0_ffn_in = {k: v for k, v in _L0_ffn_all.items() if k in ('w1_w', 'w1_s', 'w2_w', 'w2_s', 'h1_w', 'h1_s', 'h2_w', 'h2_s', 'w3_w', 'w3_s')}
    del _L0_ffn_all

    def _L1_xattn_setup():
        import jax, jax.numpy as jnp
        import numpy as np
        N_HEADS = 16
        D_HEAD = 64
        key = jax.random.key(seed)
        ks = jax.random.split(key, 7)
        B, SQ, SKV = (2, 256, 256)
        D_MODEL, D_COND, D_ATTN = (128, 96, N_HEADS * D_HEAD)
        return {'x': jax.random.normal(ks[0], (B, SQ, D_MODEL), jnp.float32), 'cond': jax.random.normal(ks[1], (B, SKV, D_COND), jnp.float32), 'w_q': jax.random.normal(ks[2], (D_MODEL, D_ATTN), jnp.float32) * D_MODEL ** (-0.5), 'w_k': jax.random.normal(ks[3], (D_COND, D_ATTN), jnp.float32) * D_COND ** (-0.5), 'w_v': jax.random.normal(ks[4], (D_COND, D_ATTN), jnp.float32) * D_COND ** (-0.5), 'w_out': jax.random.normal(ks[5], (D_ATTN, D_MODEL), jnp.float32) * D_ATTN ** (-0.5), 'b_out': jnp.zeros((D_MODEL,), jnp.float32)}
    _L1_xattn_all = _L1_xattn_setup()
    _L1_xattn_in = {k: v for k, v in _L1_xattn_all.items() if k in ('w_q', 'w_k', 'w_v', 'w_out', 'b_out')}
    del _L1_xattn_all

    def _L1_ffn_setup():
        import jax, jax.numpy as jnp
        import numpy as np
        B, S, D, F, E = (2, 256, 128, 512, 8)
        LN_EPS = 1e-05

        def _xavier(key, shape, fan_in, fan_out):
            a = np.sqrt(6.0 / (fan_in + fan_out))
            return jax.random.uniform(key, shape, jnp.float32, -a, a)
        key = jax.random.key(seed)
        ks = jax.random.split(key, 8)
        tgt = jax.random.normal(ks[0], (B, S, D), jnp.float32)
        router_w = _xavier(ks[1], (E, D), D, E)
        router_b = jnp.zeros((E,), jnp.float32)
        w1 = _xavier(ks[2], (E, D, F), D, F)
        b1 = jnp.zeros((E, F), jnp.float32)
        w2 = _xavier(ks[3], (E, F, D), F, D)
        b2 = jnp.zeros((E, D), jnp.float32)
        gamma = jnp.ones((D,), jnp.float32)
        beta = jnp.zeros((D,), jnp.float32)
        return {'tgt': tgt, 'router_w': router_w, 'router_b': router_b, 'w1': w1, 'b1': b1, 'w2': w2, 'b2': b2, 'gamma': gamma, 'beta': beta}
    _L1_ffn_all = _L1_ffn_setup()
    _L1_ffn_in = {k: v for k, v in _L1_ffn_all.items() if k in ('router_w', 'router_b', 'w1', 'b1', 'w2', 'b2', 'gamma', 'beta')}
    del _L1_ffn_all
    return {'x': x, 'ctx_768': ctx_768, 'L0_xattn_q_w': _L0_xattn_in['q_w'], 'L0_xattn_q_b': _L0_xattn_in['q_b'], 'L0_xattn_kv_w': _L0_xattn_in['kv_w'], 'L0_xattn_kv_b': _L0_xattn_in['kv_b'], 'L0_xattn_proj_w': _L0_xattn_in['proj_w'], 'L0_xattn_proj_b': _L0_xattn_in['proj_b'], 'L0_ffn_w1_w': _L0_ffn_in['w1_w'], 'L0_ffn_w1_s': _L0_ffn_in['w1_s'], 'L0_ffn_w2_w': _L0_ffn_in['w2_w'], 'L0_ffn_w2_s': _L0_ffn_in['w2_s'], 'L0_ffn_h1_w': _L0_ffn_in['h1_w'], 'L0_ffn_h1_s': _L0_ffn_in['h1_s'], 'L0_ffn_h2_w': _L0_ffn_in['h2_w'], 'L0_ffn_h2_s': _L0_ffn_in['h2_s'], 'L0_ffn_w3_w': _L0_ffn_in['w3_w'], 'L0_ffn_w3_s': _L0_ffn_in['w3_s'], 'L1_xattn_w_q': _L1_xattn_in['w_q'], 'L1_xattn_w_k': _L1_xattn_in['w_k'], 'L1_xattn_w_v': _L1_xattn_in['w_v'], 'L1_xattn_w_out': _L1_xattn_in['w_out'], 'L1_xattn_b_out': _L1_xattn_in['b_out'], 'L1_ffn_router_w': _L1_ffn_in['router_w'], 'L1_ffn_router_b': _L1_ffn_in['router_b'], 'L1_ffn_w1': _L1_ffn_in['w1'], 'L1_ffn_b1': _L1_ffn_in['b1'], 'L1_ffn_w2': _L1_ffn_in['w2'], 'L1_ffn_b2': _L1_ffn_in['b2'], 'L1_ffn_gamma': _L1_ffn_in['gamma'], 'L1_ffn_beta': _L1_ffn_in['beta']}

def reference(x, ctx_768, L0_xattn_q_w, L0_xattn_q_b, L0_xattn_kv_w, L0_xattn_kv_b, L0_xattn_proj_w, L0_xattn_proj_b, L0_ffn_w1_w, L0_ffn_w1_s, L0_ffn_w2_w, L0_ffn_w2_s, L0_ffn_h1_w, L0_ffn_h1_s, L0_ffn_h2_w, L0_ffn_h2_s, L0_ffn_w3_w, L0_ffn_w3_s, L1_xattn_w_q, L1_xattn_w_k, L1_xattn_w_v, L1_xattn_w_out, L1_xattn_b_out, L1_ffn_router_w, L1_ffn_router_b, L1_ffn_w1, L1_ffn_b1, L1_ffn_w2, L1_ffn_b2, L1_ffn_gamma, L1_ffn_beta):
    import jax
    import jax.numpy as jnp

    def _L0_xattn_ref(x, cond, q_w, q_b, kv_w, kv_b, proj_w, proj_b):
        import jax, jax.numpy as jnp
        import numpy as np
        NUM_HEADS = 16
        B, N, C = x.shape
        condN = cond.shape[1]
        H = NUM_HEADS
        hd = C // H
        scale = hd ** (-0.5)
        q = (x @ q_w + q_b).reshape(B, N, H, hd).transpose(0, 2, 1, 3)
        kv = (cond @ kv_w + kv_b).reshape(B, condN, 2, H, hd)
        k = kv[:, :, 0].transpose(0, 2, 1, 3)
        v = kv[:, :, 1].transpose(0, 2, 1, 3)
        attn = jnp.einsum('bhnd,bhmd->bhnm', q * scale, k)
        attn = jax.nn.softmax(attn, axis=-1)
        out = jnp.einsum('bhnm,bhmd->bhnd', attn, v)
        out = out.transpose(0, 2, 1, 3).reshape(B, N, C)
        return out @ proj_w + proj_b

    def _L0_ffn_ref(x, w1_w, w1_s, w2_w, w2_s, h1_w, h1_s, h2_w, h2_s, w3_w, w3_s):
        import jax, jax.numpy as jnp
        import numpy as np
        D_IN, D_HID = (128, 512)

        def _ternary(key, shape):
            return jax.random.randint(key, shape, -1, 2).astype(jnp.float32)

        def _tlin(x, w, s):
            return jnp.einsum('bsi,oi->bso', x, w) * s
        h = jax.nn.silu(_tlin(x, w1_w, w1_s)) * _tlin(x, w2_w, w2_s)
        h = jax.nn.gelu(_tlin(h, h1_w, h1_s), approximate=False)
        h = jax.nn.gelu(_tlin(h, h2_w, h2_s), approximate=False)
        return _tlin(h, w3_w, w3_s)

    def _L1_xattn_ref(x, cond, w_q, w_k, w_v, w_out, b_out):
        import jax, jax.numpy as jnp
        import numpy as np
        N_HEADS = 16
        D_HEAD = 64
        B, SQ, _ = x.shape
        SKV = cond.shape[1]
        scale = D_HEAD ** (-0.5)
        q = (x @ w_q).reshape(B, SQ, N_HEADS, D_HEAD)
        k = (cond @ w_k).reshape(B, SKV, N_HEADS, D_HEAD)
        v = (cond @ w_v).reshape(B, SKV, N_HEADS, D_HEAD)
        attn = jnp.einsum('bqhd,bkhd->bhqk', q, k) * scale
        attn = jax.nn.softmax(attn, axis=-1)
        out = jnp.einsum('bhqk,bkhd->bqhd', attn, v).reshape(B, SQ, N_HEADS * D_HEAD)
        return out @ w_out + b_out

    def _L1_ffn_ref(tgt, router_w, router_b, w1, b1, w2, b2, gamma, beta):
        import jax, jax.numpy as jnp
        import numpy as np
        B, S, D, F, E = (2, 256, 128, 512, 8)
        LN_EPS = 1e-05

        def _xavier(key, shape, fan_in, fan_out):
            a = np.sqrt(6.0 / (fan_in + fan_out))
            return jax.random.uniform(key, shape, jnp.float32, -a, a)
        logits = jnp.einsum('bsd,ed->bse', tgt, router_w) + router_b
        rw = jax.nn.softmax(logits, axis=-1)
        rw = jnp.zeros_like(rw).at[..., 0].set(1.0)
        h = jax.nn.relu(jnp.einsum('bsd,edf->besf', tgt, w1) + b1[None, :, None, :])
        eo = jnp.einsum('besf,efd->besd', h, w2) + b2[None, :, None, :]
        tgt2 = jnp.einsum('besd,bse->bsd', eo, rw)
        x = tgt + tgt2
        mean = jnp.mean(x, axis=-1, keepdims=True)
        var = jnp.mean(jnp.square(x - mean), axis=-1, keepdims=True)
        return (x - mean) * jax.lax.rsqrt(var + LN_EPS) * gamma + beta
    x = x + _L0_xattn_ref(_layernorm(x, axis=-1), ctx_768, L0_xattn_q_w, L0_xattn_q_b, L0_xattn_kv_w, L0_xattn_kv_b, L0_xattn_proj_w, L0_xattn_proj_b)
    x = x + _L0_ffn_ref(_layernorm(x, axis=-1), L0_ffn_w1_w, L0_ffn_w1_s, L0_ffn_w2_w, L0_ffn_w2_s, L0_ffn_h1_w, L0_ffn_h1_s, L0_ffn_h2_w, L0_ffn_h2_s, L0_ffn_w3_w, L0_ffn_w3_s)
    x = x + _L1_xattn_ref(_layernorm(x, axis=-1), ctx_768, L1_xattn_w_q, L1_xattn_w_k, L1_xattn_w_v, L1_xattn_w_out, L1_xattn_b_out)
    x = x + _L1_ffn_ref(_layernorm(x, axis=-1), L1_ffn_router_w, L1_ffn_router_b, L1_ffn_w1, L1_ffn_b1, L1_ffn_w2, L1_ffn_b2, L1_ffn_gamma, L1_ffn_beta)
    return x

_drawn_inputs = setup_inputs


def setup_inputs(seed=0):
    import zlib

    import numpy as np

    out = dict(_drawn_inputs(seed))
    spreads = {'L0_xattn_q_b': (0.0, 0.1),
     'L0_xattn_kv_b': (0.0, 0.1),
     'L0_xattn_proj_b': (0.0, 0.1),
     'L1_xattn_b_out': (0.0, 0.1),
     'L1_ffn_router_b': (0.0, 0.1),
     'L1_ffn_b1': (0.0, 0.1),
     'L1_ffn_b2': (0.0, 0.1),
     'L1_ffn_gamma': (1.0, 0.2),
     'L1_ffn_beta': (0.0, 0.1)}
    factors = {}
    for name, (base, spread) in spreads.items():
        noise = np.random.default_rng([zlib.crc32(name.encode()), seed]).standard_normal(out[name].shape)
        drawn = base * np.exp(spread * noise) if base else spread * noise
        out[name] = jnp.asarray(drawn.astype(out[name].dtype))
    for name, factor in factors.items():
        out[name] = (out[name] * factor).astype(out[name].dtype)
    return out
```

```python
from contextlib import ExitStack

import concourse.bass as bass
from concourse import mybir

ALU = mybir.AluOpType
ACT = mybir.ActivationFunctionType
AX = mybir.AxisListType
F32 = mybir.dt.float32
F32R = mybir.dt.float32r

P = 128
D = 128
TOK = 512
TT = TOK // P
EPS = 1e-5
PARTS = ((0, 0), (1, 0), (0, 1))


class Stream:

    def __init__(self, nc, ctx, tokens):
        def sb(name, shape):
            return ctx.enter_context(nc.sbuf_tensor(name, shape, F32))
        self.nc, self.ctx = nc, ctx
        self.tiles = tokens // P
        self.x = sb("x", [P, self.tiles, D])
        self.moments = sb("moments", [P, self.tiles, 2])
        self.rstd = sb("rstd", [P, self.tiles])
        self.shift = sb("shift", [P, self.tiles])
        self.ident = sb("ident", [P, P])
        self.power = sb("power", [P, self.tiles])


    def sem(self, name):
        return self.ctx.enter_context(self.nc.semaphore(name))


def rows(vec, n):
    return vec.rearrange("(a n) -> a n", a=1).broadcast_to([P, n])


def at(i, n=1):
    return slice(i, i + n) if isinstance(i, int) else bass.ds(i, n)


def norm_factors(pool, s, done):
    pool.tensor_scalar(s.rstd[:], s.moments[:, :, 1], EPS, 1.0, ALU.add, ALU.mult).then_inc(done, 1)
    pool.wait_ge(done, 1)
    pool.tensor_tensor(s.rstd[:], s.rstd[:], s.power[:], ALU.pow).then_inc(done, 1)
    pool.wait_ge(done, 2)
    pool.tensor_tensor(s.shift[:], s.moments[:, :, 0], s.rstd[:], ALU.mult).then_inc(done, 1)
    pool.wait_ge(done, 3)
    pool.tensor_scalar(s.shift[:], s.shift[:], -1.0, 0.0, ALU.mult, ALU.add).then_inc(done, 1)
    pool.wait_ge(done, 4)


def normalise(dve, s, xn, first_tile, tiles, normed):
    for t in range(tiles):
        i = first_tile + t
        dve.tensor_scalar(xn[:, t, :], s.x[:, at(i), :], s.rstd[:, at(i)], s.shift[:, at(i)],
                           ALU.mult, ALU.add).then_inc(normed, 1)


class Update:

    def __init__(self, s, sb, prefix, tiles):
        self.s, self.tiles = s, tiles
        self.fresh, self.stats = sb("fresh", [P, tiles, D]), sb("stats", [P, tiles, 6])
        self.pair = sb("pair", [P, tiles, 2])
        self.read, self.added, self.measured, self.stored, self.gathered, self.done = (
            s.sem(prefix + n) for n in ("x_got_read", "x_added", "x_measured", "x_stored", "x_gathered", "x_done"))

    def take(self, dve, got, other, n):
        if not (isinstance(n, int) and n == 1):
            dve.wait_ge(self.stored, n - 1)
        dve.tensor_tensor(self.fresh[:], got, other, ALU.add).then_inc(self.read, 1)

    def finish(self, dve, first_tile, n, add_x=True):
        s, x = self.s, self.s.x[:, at(first_tile, self.tiles), :]
        dve.wait_ge(self.read, n)
        if add_x:
            dve.tensor_tensor(self.fresh[:], self.fresh[:], x, ALU.add).then_inc(self.added, 1)
            dve.wait_ge(self.added, n)
        for t in range(self.tiles):
            ins = dve.bn_stats(self.stats[:, t, :], self.fresh[:, t, :])
        ins.then_inc(self.measured, 1)
        dve.wait_ge(self.measured, n)
        dve.tensor_scalar(x, self.fresh[:], 1.0, None, ALU.mult).then_inc(self.stored, 1)
        for t in range(self.tiles):
            ins = dve.bn_aggr(self.pair[:, t, :], self.stats[:, t, :])
        ins.then_inc(self.gathered, 1)
        dve.wait_ge(self.gathered, n)
        dve.tensor_scalar(s.moments[:, at(first_tile, self.tiles), :], self.pair[:], 1.0, None,
                          ALU.mult).then_inc(self.done, 1)

    def run(self, dve, got, bias, first_tile, n):
        x = self.s.x[:, at(first_tile, self.tiles), :]
        self.take(dve, got, x if bias is None else bias, n)
        self.finish(dve, first_tile, n, bias is not None)


def load_stream(nc, s, x_dram):
    with ExitStack() as ctx:
        sem = s.sem
        x_in = [sem(f"x_in{c}") for c in range(4)]
        stats_done, zeroed, made = sem("stats_done"), sem("ident_zeroed"), sem("constants_made")
        moments_done = sem("moments_done")
        stats = ctx.enter_context(nc.sbuf_tensor("load_stats", [P, s.tiles, 6], F32))
        xv = x_dram.rearrange("(t p) d -> p t d", p=P)
        n = s.tiles // 4
        block = ctx.enter_context(nc.Block())

        @block.sync
        def _(sp):
            for c in range(4):
                sp.dma_start(s.x[:, c * n:(c + 1) * n, :], xv[:, c * n:(c + 1) * n, :]).then_inc(x_in[c], 16)

        @block.gpsimd
        def _(pool):
            pool.memset(s.ident[:], 0.0).then_inc(zeroed, 1)
            pool.memset(s.power[:], -0.5).then_inc(made, 1)
            pool.wait_ge(zeroed, 1)
            pool.affine_select(out=s.ident[:], in_=s.ident[:], compare_op=ALU.not_equal, fill=1.0, base=0,
                               pattern=[[-1, P]], channel_multiplier=1).then_inc(made, 1)
            pool.wait_ge(made, 2)

        @block.vector
        def _(dve):
            for c in range(4):
                dve.wait_ge(x_in[c], 16)
                for t in range(c * n, (c + 1) * n):
                    dve.bn_stats(stats[:, t, :], s.x[:, t, :]).then_inc(stats_done, 1)
            for t in range(s.tiles):
                dve.wait_ge(stats_done, t + 1)
                dve.bn_aggr(s.moments[:, t, :], stats[:, t, :]).then_inc(moments_done, 1)
            dve.wait_ge(moments_done, s.tiles)


class Chain:

    def __init__(self, eng, sem):
        self.eng, self.sem, self.base = eng, sem, 0

    def start(self, base):
        self.base = base

    def then(self, ins):
        ins.then_inc(self.sem, 1)
        self.base = self.base + 1
        self.eng.wait_ge(self.sem, self.base)


def split(dve, hi, lo, src, hi_sem, hi_count, lo_sem):
    dve.tensor_copy(hi, src).then_inc(hi_sem, 1)
    dve.wait_ge(hi_sem, hi_count)
    dve.tensor_tensor(lo, src, hi.bitcast(F32), ALU.subtract).then_inc(lo_sem, 1)


def xattn_small(nc, s, cT_dram, w):
    NH, HD, B = 16, D // 16, 64
    HP = NH // 2
    CD = cT_dram.shape[0]
    SCALE = float(HD) ** -0.5
    ROWS = 4 * HD
    NB = TOK // B
    STEPS = s.tiles // TT
    V1 = HD + 1
    with ExitStack() as ctx:
        def sb(n, shape, dt=F32):
            return ctx.enter_context(nc.sbuf_tensor("a_" + n, shape, dt))

        def ps(n, shape):
            return ctx.enter_context(nc.psum_tensor("a_" + n, shape, F32))

        def sem(n):
            return s.sem("a_" + n)

        raw_q, raw_kv = sb("raw_q", [P, D]), sb("raw_kv", [CD, 2 * D])
        wq, wk = [sb(f"wq_{i}", [P, D], F32R) for i in "01"], [sb(f"wk_{i}", [CD, D], F32R) for i in "01"]
        wo, qb, kb = sb("wo", [P, D]), sb("qb", [P, 1]), sb("kb", [P, 1])
        qbs = sb("qb_scaled", [P, 1])
        vb, ob = sb("vb", [P, D]), sb("ob", [P, D])
        xn = sb("xn", [P, TT, D])
        xT = [sb(f"xT_{i}", [P, TOK], F32R) for i in "01"]
        cT = [sb(f"cT{b}", [CD, NB, 2, B]) for b in "01"]
        cp = [sb(f"c_{i}", [CD, TOK], F32R) for i in "01"]
        qf, kf = sb("qf", [P, TOK]), sb("kf", [P, TOK])
        kp = [sb(f"k_{i}", [P, TOK]) for i in "01"]
        qz = [[sb(f"qz{b}_{i}", [P, NH // 4, TT, 3 * B], F32R) for i in "01"] for b in "01"]
        zero = sb("zero", [P, 1])
        kz = [[sb(f"kz{b}_{i}", [P, 4, TOK], F32R) for i in "01"] for b in "01"]
        vz = [sb(f"vz{b}", [P, TT, HP, 2, 2 * V1]) for b in "01"]
        head_rows, mask = sb("head_rows", [P, NH]), sb("mask", [P, 4])
        top = sb("top", [P, 2, NH])
        e = [sb(f"e{u}", [P, NH, B]) for u in "01"]
        eT = sb("eT", [P, HP, P])
        inv = sb("inv", [P, 2, HP, 2])
        o = sb("o", [P, TT, D])
        oT = sb("oT", [P, TOK])
        update = Update(s, sb, "a_", TT)
        scores = [ps(f"scores{u}", [P, NH, B]) for u in "01"]
        turned_e, att, misc = ps("turned_e", [P, HP, P]), ps("att", [P, HP, 2, 2, V1]), ps("misc", [P, TOK])

        w_in, vec_in = sem("weights_in"), sem("vectors_in")
        c_in = [sem("ctx_in0"), sem("ctx_in1")]
        w_hi, w_split = sem("weights_hi"), sem("weights_split")
        made, mask_made = sem("constants_made"), sem("mask_made")
        factors, normed = sem("norm_factors"), sem("normed")
        turned, x_hi, x_split = sem("xn_turned"), sem("x_hi"), sem("x_split")
        c_hi, c_split = sem("c_hi"), sem("c_split")
        q_prod, q_out, q_hi, q_split = sem("q_product"), sem("q_out"), sem("q_hi"), sem("q_split")
        k_prod, k_out, k_hi, k_split, k_masked = (sem(n) for n in ("k_product", "k_out", "k_hi", "k_split",
                                                                  "k_masked"))
        v_prod, v_out = sem("v_product"), sem("v_out")
        o_turned, o_out, proj_done = sem("o_turned"), sem("o_out"), sem("projected")
        scored, top_done, shifted, exped = sem("scored"), sem("top_done"), sem("shifted"), sem("exped")
        e_turned = sem("e_turned")
        eT_act, eT_dve = sem("eT_by_act"), sem("eT_by_dve")
        attended, inv_done, normal = sem("attended"), sem("inv_done"), sem("o_normalised")
        block = ctx.enter_context(nc.Block())

        def exists(g):
            return not isinstance(g, int) or 0 <= g < STEPS

        def bodies(eng, body):
            body(0, 0)
            body(1, 1)
            with eng.Fori(1, STEPS // 2 - 1) as i:
                body(2 * i, 0)
                body(2 * i + 1, 1)
            body(STEPS - 2, 0)
            body(STEPS - 1, 1)
            body(STEPS, 0)

        def by_batch(t):
            return t[:].rearrange("c (b k) -> c b k", k=B)

        def is0(g):
            return isinstance(g, int) and g == 0

        @block.sync
        def _(sp):
            def fetch(sp, g, b):
                for copy in (0, 1):
                    sp.dma_start(cT[b][:, :, copy, :], cT_dram[:, at(g * TOK, TOK)].rearrange(
                        "c (b k) -> c b k", k=B)).then_inc(c_in[b], 16)

            sp.dma_start(raw_q[:], w["q"]).then_inc(w_in, 16)
            sp.dma_start(raw_kv[:], w["kv"]).then_inc(w_in, 16)
            fetch(sp, 0, 0)
            sp.dma_start(qb[:], w["qb"]).then_inc(vec_in, 16)
            sp.dma_start(kb[:], w["kb"]).then_inc(vec_in, 16)
            sp.dma_start(vb[:], rows(w["vb"], D)).then_inc(vec_in, 16)
            sp.dma_start(ob[:], rows(w["ob"], D)).then_inc(vec_in, 16)
            sp.dma_start(wo[:], w["o"]).then_inc(vec_in, 16)

            def body(g, b):
                after = exists(g + 1)
                if after:
                    if not is0(g):
                        sp.wait_ge(v_prod, 2 * g)
                    fetch(sp, g + 1, 1 - b)
            bodies(sp, body)

        @block.gpsimd
        def _(pool):
            for b in (0, 1):
                for i in (0, 1):
                    pool.memset(qz[b][i][:].bitcast(F32), 0.0).then_inc(made, 1)
                pool.memset(vz[b][:], 0.0).then_inc(made, 1)
            pool.memset(zero[:], 0.0).then_inc(made, 1)
            pool.memset(head_rows[:], 1.0).then_inc(made, 1)
            pool.wait_ge(made, 8)
            for b in (0, 1):
                pool.memset(vz[b][0:B, :, :, :, HD:V1], 1.0).then_inc(made, 1)
                pool.memset(vz[b][B:P, :, :, :, V1 + HD:2 * V1], 1.0).then_inc(made, 1)
            pool.wait_ge(made, 12)
            pool.affine_select(out=head_rows[:], in_=head_rows[:], compare_op=ALU.is_ge, fill=0.0, base=0,
                               pattern=[[-HD, NH]], channel_multiplier=1).then_inc(made, 1)
            pool.wait_ge(made, 13)
            pool.affine_select(out=head_rows[:], in_=head_rows[:], compare_op=ALU.is_ge, fill=0.0, base=HD - 1,
                               pattern=[[HD, NH]], channel_multiplier=-1).then_inc(made, 1)
            norm_factors(pool, s, factors)

            def q_parts(g, b):
                pool.wait_ge(q_out, g + 1)
                grouped = qf[:].rearrange("p (t a q) -> p t a q", a=2, q=B)
                for i in (0, 1):
                    for r in range(NH // 4):
                        rs = slice(r * ROWS, (r + 1) * ROWS)
                        hi, out = (qz[b][k][rs, r].rearrange("p t (a q) -> p t a q", a=3)[:, :, 0:3:2, :]
                                   for k in (0, i))
                        if i == 0:
                            none = zero[rs].rearrange("p (a b c) -> p a b c", a=1, b=1).broadcast_to([ROWS, TT, 2, B])
                            ins = pool.tensor_tensor(out, grouped[rs], none, ALU.add)
                        else:
                            ins = pool.tensor_tensor(out, grouped[rs], hi.bitcast(F32), ALU.subtract)
                    ins.then_inc(q_split if i else q_hi, 1)
                    if i == 0:
                        pool.wait_ge(q_hi, g + 1)
            pool.wait_ge(made, 14)
            q_parts(0, 0)

            def body(g, b):
                if exists(g + 1):
                    q_parts(g + 1, 1 - b)
            bodies(pool, body)

        @block.scalar
        def _(act):
            def c_round(g, b):
                act.wait_ge(c_in[b], (g - b) * 16 + 32)
                if not is0(g):
                    act.wait_ge(k_prod, g)
                act.activation(by_batch(cp[0]), cT[b][:, :, 0, :], ACT.Copy).then_inc(c_hi, 1)

            def q_evacuate(g):
                act.wait_ge(q_prod, g + 1)
                act.activation(qf[:], misc[:], ACT.Identity, bias=qbs[:, 0:1], scale=SCALE).then_inc(q_out, 1)

            def k_evacuate(g):
                act.wait_ge(k_prod, g + 1)
                act.activation(kf[:], misc[:], ACT.Identity, bias=kb[:, 0:1]).then_inc(k_out, 1)

            def mask_keys(g, b, i):
                act.wait_ge(k_split, g + 1)
                for j in range(4):
                    ins = act.activation(kz[b][i][:, j, :], kp[i][:], ACT.Copy, scale=mask[:, j:j + 1])
                ins.then_inc(k_masked, 1)

            def o_evacuate(g):
                act.wait_ge(o_turned, g + 1)
                act.activation(oT[:], misc[:], ACT.Copy).then_inc(o_out, 1)

            def eT_half(m):
                act.wait_ge(e_turned, 2 * m + 1)
                act.activation(eT[:, 0:HP // 2, :], turned_e[:, 0:HP // 2, :], ACT.Copy).then_inc(eT_act, 1)

            def exp(n, u):
                act.wait_ge(shifted, n + 1)
                act.activation(e[u][:], e[u][:], ACT.Exp).then_inc(exped, 1)

            c_round(0, 0)
            act.wait_ge(vec_in, 16 * 5)
            act.activation(qbs[:], qb[:], ACT.Copy, scale=SCALE).then_inc(w_split, 1)
            act.wait_ge(w_split, 3)
            q_evacuate(0)
            k_evacuate(0)
            act.wait_ge(mask_made, 1)
            mask_keys(0, 0, 0)
            mask_keys(0, 0, 1)

            def body(g, b):
                here, after = exists(g), exists(g + 1)
                for p in range(TT):
                    n = g * TT + p
                    if p == 0 and after:
                        c_round(g + 1, 1 - b)
                    if (not is0(g) or p >= 2) and (here or p < 2):
                        eT_half(n - 2)
                    if p == 1 and after:
                        q_evacuate(g + 1)
                        k_evacuate(g + 1)
                    if p == 2 and after:
                        mask_keys(g + 1, 1 - b, 0)
                    if p == 2 and not is0(g):
                        o_evacuate(g - 1)
                    if here:
                        exp(n, p % 2)
                    if p == 2 and after:
                        mask_keys(g + 1, 1 - b, 1)
            bodies(act, body)

        @block.vector
        def _(dve):
            dve.wait_ge(w_in, 32)
            split(dve, wq[0][:], wq[1][:], raw_q[:], w_hi, 1, w_split)
            split(dve, wk[0][:], wk[1][:], raw_kv[:, 0:D], w_hi, 2, w_split)
            dve.wait_ge(made, 14)
            dve.tensor_reduce(mask[:], head_rows[:].rearrange("p (q j) -> p j q", j=4), AX.X,
                              ALU.add).then_inc(mask_made, 1)

            def x_parts(g):
                dve.wait_ge(turned, g + 1)
                split(dve, xT[0][:], xT[1][:], misc[:], x_hi, g + 1, x_split)

            def c_low(g, b):
                dve.wait_ge(c_hi, g + 1)
                dve.tensor_tensor(by_batch(cp[1]), cT[b][:, :, 0, :], by_batch(cp[0]).bitcast(F32),
                                  ALU.subtract).then_inc(c_split, 1)

            def k_parts(g):
                dve.wait_ge(k_out, g + 1)
                if not is0(g):
                    dve.wait_ge(k_masked, 2 * g)
                dve.tensor_copy(kp[0][:].bitcast(F32R), kf[:]).then_inc(k_hi, 1)
                dve.wait_ge(k_hi, g + 1)
                dve.tensor_tensor(kp[1][:], kf[:], kp[0][:], ALU.subtract).then_inc(k_split, 1)

            def v_half(g, b, i):
                dve.wait_ge(v_prod, 2 * g + i + 1)
                ts = slice(i * TT // 2, (i + 1) * TT // 2)
                into = vz[b][:, ts].rearrange("p t h a c -> p t a h c")
                v = misc[:].rearrange("p (t a h o d) -> p t a h o d", t=TT // 2, a=2, o=2, d=HD)
                bias = vb[:].rearrange("p (a h o d) -> p a h o d", a=1, o=2, d=HD).broadcast_to([P, 2, HP, 2, HD])
                for odd in (0, 1):
                    rs = slice(odd * B, odd * B + B)
                    for t in range(TT // 2):
                        ins = dve.tensor_tensor(into[rs, t, :, :, odd * V1:odd * V1 + HD], v[rs, t, :, :, odd, :],
                                                bias[rs, :, :, odd, :], ALU.add)
                ins.then_inc(v_out, 1)

            def softmax(g, n, u):
                dve.wait_ge(scored, n + 1)
                dve.tensor_reduce(top[:, u], scores[u][:], AX.X, ALU.max).then_inc(top_done, 1)
                dve.wait_ge(top_done, n + 1)
                if not (isinstance(n, int) and n < 2):
                    dve.wait_ge(e_turned, 2 * n - 2)
                peak = top[:, u].rearrange("p (h a) -> p h a", a=1).broadcast_to([P, NH, B])
                dve.tensor_tensor(e[u][:], scores[u][:], peak, ALU.subtract).then_inc(shifted, 1)

            def eT_half(m):
                dve.wait_ge(e_turned, 2 * m + 2)
                dve.tensor_copy(eT[:, HP // 2:, :], turned_e[:, HP // 2:, :]).then_inc(eT_dve, 1)

            def o_normalise(m, t, g):
                dve.wait_ge(attended, m + 1)
                halves = [(slice(a * B, a * B + B), att[a * B:a * B + B, :, a]) for a in (0, 1)]
                for rs, got in halves:
                    ins = dve.reciprocal(inv[rs, t % 2], got[:, :, :, HD])
                ins.then_inc(inv_done, 1)
                dve.wait_ge(inv_done, m + 1)
                if t == 0 and not is0(g):
                    dve.wait_ge(o_turned, g)
                for rs, got in halves:
                    sums = inv[rs, t % 2].rearrange("p h (o a) -> p h o a", a=1).broadcast_to([B, HP, 2, HD])
                    ins = dve.tensor_tensor(o[rs, t, :].rearrange("p (h o d) -> p h o d", h=HP, o=2),
                                            got[:, :, :, 0:HD], sums, ALU.mult)
                ins.then_inc(normal, 1)

            def take_update(g):
                dve.wait_ge(proj_done, g + 1)
                bias = ob[:].rearrange("p (a d) -> p a d", a=1).broadcast_to([P, TT, D])
                update.take(dve, misc[:].rearrange("p (t d) -> p t d", d=D), bias, g + 1)

            def make_x(g):
                if not is0(g):
                    dve.wait_ge(turned, g)
                normalise(dve, s, xn, g * TT, TT, normed)

            c_low(0, 0)
            dve.wait_ge(factors, 4)
            make_x(0)
            x_parts(0)
            make_x(1)
            k_parts(0)
            dve.wait_ge(vec_in, 16 * 5)
            v_half(0, 0, 0)
            v_half(0, 0, 1)

            def body(g, b):
                here, after = exists(g), exists(g + 1)
                for p in range(TT):
                    n = g * TT + p
                    m = n - 2
                    behind = (not is0(g) or p >= 2) and (here or p < 2)
                    if p == 2 and after:
                        k_parts(g + 1)
                    if behind:
                        eT_half(m)
                    if p >= 2 and after:
                        v_half(g + 1, 1 - b, p - 2)
                    if here:
                        softmax(g, n, p % 2)
                    if p == 3 and exists(g + 2):
                        make_x(g + 2)
                    if p == 0 and after:
                        x_parts(g + 1)
                        c_low(g + 1, 1 - b)
                    if behind:
                        o_normalise(m, (p + 2) % TT, g)
                    if p == 2 and exists(g - 2):
                        update.finish(dve, (g - 2) * TT, g - 1)
                    if p == 3 and exists(g - 1):
                        take_update(g - 1)
            bodies(dve, body)
            update.finish(dve, (STEPS - 1) * TT, STEPS)
            dve.wait_ge(update.done, STEPS)

        @block.tensor
        def _(pe):
            def turn_x(g):
                pe.wait_ge(normed, (g + 1) * TT)
                for t in range(TT):
                    ins = pe.transpose(misc[:, t * P:(t + 1) * P], xn[:, t, :], s.ident[:])
                ins.then_inc(turned, 1)

            def make_q(g):
                pe.wait_ge(x_split, g + 1)
                for i, (a, c) in enumerate(PARTS):
                    ins = pe.matmul(misc[:], wq[a][:], xT[c][:], start=(i == 0), stop=(i == 2))
                ins.then_inc(q_prod, 1)

            def make_k(g):
                pe.wait_ge(c_split, g + 1)
                pe.wait_ge(q_out, g + 1)
                for i, (a, c) in enumerate(PARTS):
                    ins = pe.matmul(misc[:], wk[a][:], cp[c][:], start=(i == 0), stop=(i == 2))
                ins.then_inc(k_prod, 1)

            def make_v(g, b, i):
                if i == 0:
                    pe.wait_ge(k_out, g + 1)
                else:
                    pe.wait_ge(v_out, 2 * g + 1)
                for j in range(NB // 2):
                    twice = cT[b][:, i * NB // 2 + j].rearrange("c a k -> c (a k)")
                    ins = pe.matmul(misc[:, j * D:(j + 1) * D], twice, raw_kv[:, D:2 * D], start=True, stop=True)
                ins.then_inc(v_prod, 1)

            def score(g, b, p, n):
                if not (isinstance(n, int) and n < 2):
                    pe.wait_ge(shifted, n - 1)
                out = scores[p % 2][:].rearrange("q h k -> q (h k)")
                for r in range(NH // 4):
                    for half in (0, 1):
                        for i, (a, c) in enumerate(PARTS):
                            batch = 2 * p + half
                            ins = pe.matmul(out[:, r * 4 * B:(r + 1) * 4 * B],
                                            qz[b][c][:, r, p, half * B:half * B + P],
                                            kz[b][a][:, :, batch * B:(batch + 1) * B],
                                            start=(half == 0 and i == 0), stop=(half == 1 and i == 2))
                ins.then_inc(scored, 1)

            def turn_e(m, u):
                pe.wait_ge(exped, m + 1)
                for t in range(HP):
                    ins = pe.transpose(turned_e[:, t, :], e[u][:, 2 * t:2 * t + 2, :].rearrange("q h k -> q (h k)"),
                                       s.ident[:])
                    if t % (HP // 2) == HP // 2 - 1:
                        ins.then_inc(e_turned, 1)

            def attend(m, b, p):
                pe.wait_ge(eT_act, m + 1)
                if not (isinstance(m, int) and m == 0):
                    pe.wait_ge(normal, m)
                for t in range(HP):
                    if t == HP // 2:
                        pe.wait_ge(eT_dve, m + 1)
                    ins = pe.matmul(att[:, t].rearrange("q a h d -> q (a h d)"), eT[:, t, :],
                                    vz[b][:, p, t].rearrange("k a c -> k (a c)"), start=True, stop=True)
                ins.then_inc(attended, 1)

            def turn_o(g):
                pe.wait_ge(normal, (g + 1) * TT)
                for t in range(TT):
                    ins = pe.transpose(misc[:, t * P:(t + 1) * P], o[:, t, :], s.ident[:])
                ins.then_inc(o_turned, 1)

            def project(g):
                pe.wait_ge(o_out, g + 1)
                for t in range(TT):
                    ins = pe.matmul(misc[:, t * D:(t + 1) * D], oT[:, t * P:(t + 1) * P], wo[:], start=True,
                                    stop=True)
                ins.then_inc(proj_done, 1)

            turn_x(0)
            pe.wait_ge(w_split, 3)
            make_q(0)
            make_k(0)
            pe.wait_ge(vec_in, 16 * 5)
            pe.wait_ge(made, 14)
            make_v(0, 0, 0)
            make_v(0, 0, 1)

            def body(g, b):
                here, after = exists(g), exists(g + 1)
                for p in range(TT):
                    n = g * TT + p
                    behind = (not is0(g) or p >= 2) and (here or p < 2)
                    mb = b if p >= 2 else 1 - b
                    if behind:
                        turn_e(n - 2, p % 2)
                    if p == 2 and after:
                        make_v(g + 1, 1 - b, 0)
                    if p == 3 and after:
                        if not is0(g):
                            pe.wait_ge(o_out, g)
                        make_v(g + 1, 1 - b, 1)
                    if here:
                        if p == 0:
                            pe.wait_ge(q_split, g + 1)
                            pe.wait_ge(k_masked, 2 * (g + 1))
                        score(g, b, p, n)
                    if p == 0 and after:
                        if is0(g):
                            pe.wait_ge(v_out, 2)
                        else:
                            pe.wait_ge(eT_dve, n - 1)
                        turn_x(g + 1)
                    if p == 1 and after:
                        make_q(g + 1)
                    if p == 2 and not is0(g):
                        if after:
                            pe.wait_ge(v_out, 2 * g + 3)
                        turn_o(g - 1)
                    if behind:
                        attend(n - 2, mb, (p + 2) % TT)
                    if p == 1 and after:
                        make_k(g + 1)
                    if p == 3 and not is0(g) :
                        if after:
                            pe.wait_ge(v_out, 2 * (g + 2))
                        project(g - 1)
            bodies(pe, body)


def ffn_gated(nc, s, w):
    H = w["w1"].shape[1]
    HC = H // P
    RING = 4
    WIDE = 4 * HC
    STEPS = s.tiles // TT
    with ExitStack() as ctx:
        def sb(n, shape, dt=F32):
            return ctx.enter_context(nc.sbuf_tensor("b_" + n, shape, dt))

        def ps(n, shape):
            return ctx.enter_context(nc.psum_tensor("b_" + n, shape, F32))

        def sem(n):
            return s.sem("b_" + n)

        raw12, raw_h1, raw_h2 = sb("raw12", [P, 2, H]), sb("raw_h1", [P, HC, H]), sb("raw_h2", [P, HC, H])
        w1, w2 = ([sb(f"{n}_{i}", [P, H], F32R) for i in "01"] for n in ("w1", "w2"))
        h1, h2 = ([sb(f"{n}_{i}", [P, HC, H], F32R) for i in "01"] for n in ("h1", "h2"))
        w3, s3 = sb("w3", [P, HC, D]), sb("s3", [P, D])
        s1, s2, sh1, sh2 = (sb(n, [P, HC]) for n in ("s1", "s2", "sh1", "sh2"))
        xn = sb("xn", [P, TT, D])
        xT = [sb(f"xT_{i}", [P, TOK], F32R) for i in "01"]
        full = sb("full", [P, 2, TOK])
        a1, a2 = ([sb(f"{n}_{i}", [P, HC, TOK], F32R) for i in "01"] for n in ("a1", "a2"))
        a3 = sb("a3", [P, HC, TOK])
        update = Update(s, sb, "b_", TT)
        wide, turned, out = ps("wide", [P, RING, TOK]), ps("turned", [P, TOK]), ps("out", [P, TT, D])

        w_in = [sem(f"weights_in{i}") for i in range(3)]
        vec_in = sem("vectors_in")
        split = sem("weights_split")
        factors, normed = sem("norm_factors"), sem("normed")
        turned_done = sem("turned_done")
        xT_done = sem("xT_done")
        prod = sem("products")
        act_out = sem("act_out")
        gated = sem("gated")
        parts = sem("parts_done")
        out_done = sem("out_done")
        chain = sem("dve_chain")
        block = ctx.enter_context(nc.Block())

        def whole(eng, step):
            step(0, True, False)
            with eng.Fori(1, STEPS - 1) as g:
                step(g, False, False)
            step(STEPS - 1, False, True)

        @block.sync
        def _(sp):
            sp.dma_start(raw12[:, 0, :], w["w1"]).then_inc(w_in[0], 16)
            sp.dma_start(raw12[:, 1, :], w["w2"]).then_inc(w_in[0], 16)
            for v, n in ((s1, "w1s"), (s2, "w2s"), (sh1, "h1s"), (sh2, "h2s")):
                sp.dma_start(v[:], w[n]).then_inc(vec_in, 16)
            sp.dma_start(s3[:], rows(w["w3s"], D)).then_inc(vec_in, 16)
            sp.dma_start(w3[:], w["w3"].rearrange("(k p) o -> p k o", p=P)).then_inc(vec_in, 16)
            sp.dma_start(raw_h1[:], w["h1"].rearrange("(k p) o -> p k o", p=P)).then_inc(w_in[1], 16)
            sp.dma_start(raw_h2[:], w["h2"].rearrange("(k p) o -> p k o", p=P)).then_inc(w_in[2], 16)

        @block.gpsimd
        def _(pool):
            norm_factors(pool, s, factors)

        @block.scalar
        def _(act):
            act.wait_ge(vec_in, 16 * 6)

            def step(g, first, last):
                for f in range(2 * HC):
                    c = f % HC
                    n = 2 * c if f < HC else HC + f
                    act.wait_ge(prod, g * WIDE + n + 1)
                    if not (first and f < 2):
                        act.wait_ge(parts, g * 2 * HC + f - 1)
                    act.activation(full[:, f % 2, :], wide[:, n % RING, :], ACT.Silu if f < HC else ACT.Gelu,
                                   scale=(s1 if f < HC else sh1)[:, c:c + 1]).then_inc(act_out, 1)
                for c in range(HC):
                    act.wait_ge(prod, g * WIDE + 3 * HC + c + 1)
                    act.activation(a3[:, c, :], wide[:, (3 * HC + c) % RING, :], ACT.Gelu,
                                   scale=sh2[:, c:c + 1]).then_inc(act_out, 1)
            whole(act, step)

        @block.vector
        def _(dve):
            link = Chain(dve, chain)
            dve.wait_ge(w_in[0], 32)
            link.then(dve.tensor_copy(w1[0][:], raw12[:, 0, :]))
            dve.tensor_tensor(w1[1][:], raw12[:, 0, :], w1[0][:].bitcast(F32), ALU.subtract).then_inc(split, 1)
            link.then(dve.tensor_copy(w2[0][:], raw12[:, 1, :]))
            dve.tensor_tensor(w2[1][:], raw12[:, 1, :], w2[0][:].bitcast(F32), ALU.subtract).then_inc(split, 1)

            def make_x(g):
                normalise(dve, s, xn, g * TT, TT, normed)

            def split_x(g):
                dve.wait_ge(turned_done, g + 1)
                link.then(dve.tensor_copy(xT[0][:], turned[:]))
                dve.tensor_tensor(xT[1][:], turned[:], xT[0][:].bitcast(F32), ALU.subtract).then_inc(xT_done, 1)
            dve.wait_ge(factors, 4)
            make_x(0)
            split_x(0)
            for raw, h, i in ((raw_h1, h1, 1), (raw_h2, h2, 2)):
                dve.wait_ge(w_in[i], 16)
                link.then(dve.tensor_copy(h[0][:], raw[:]))
                dve.tensor_tensor(h[1][:], raw[:], h[0][:].bitcast(F32), ALU.subtract).then_inc(split, 1)
            dve.wait_ge(vec_in, 16 * 6)
            for k in range(HC):
                ins = dve.tensor_tensor(w3[:, k, :], w3[:, k, :], s3[:], ALU.mult)
            ins.then_inc(split, 1)
            before = link.base

            def update_x(g):
                dve.wait_ge(out_done, g + 1)
                update.run(dve, out[:], None, g * TT, g + 1)

            LINKS = 2 * HC + 1

            def step(g, first, last):
                link.start(before + g * LINKS)
                if not last:
                    dve.wait_ge(turned_done, g + 1)
                    make_x(g + 1)
                for f in range(2 * HC):
                    c, a = f % HC, (a1 if f < HC else a2)
                    dve.wait_ge(act_out, g * 3 * HC + f + 1)
                    if f < HC:
                        dve.wait_ge(prod, g * WIDE + 2 * c + 2)
                        dve.scalar_tensor_tensor(out=full[:, f % 2, :], in0=wide[:, (2 * c + 1) % RING, :],
                                                 scalar=s2[:, c:c + 1], in1=full[:, f % 2, :], op0=ALU.mult,
                                                 op1=ALU.mult).then_inc(gated, 1)
                        dve.wait_ge(gated, g * HC + c + 1)
                    link.then(dve.tensor_copy(a[0][:, c, :], full[:, f % 2, :]))
                    dve.tensor_tensor(a[1][:, c, :], full[:, f % 2, :], a[0][:, c, :].bitcast(F32),
                                      ALU.subtract).then_inc(parts, 1)
                if not last:
                    split_x(g + 1)
                if not first:
                    update_x(g - 1)
            whole(dve, step)
            update_x(STEPS - 1)
            dve.wait_ge(update.done, STEPS)

        @block.tensor
        def _(pe):
            def turn(g):
                pe.wait_ge(normed, (g + 1) * TT)
                for t in range(TT):
                    ins = pe.transpose(turned[:, t * P:(t + 1) * P], xn[:, t, :], s.ident[:])
                ins.then_inc(turned_done, 1)

            def product(g, n, first, weights, acts, ready):
                if n >= RING or not first:
                    m = n - RING
                    if 0 <= m < 2 * HC and m % 2:
                        pe.wait_ge(gated, g * HC + m // 2 + 1)
                    elif 0 <= m < 2 * HC:
                        pe.wait_ge(act_out, g * 3 * HC + m // 2 + 1)
                    else:
                        pe.wait_ge(act_out, g * 3 * HC + m - HC + 1)
                K = len(acts)
                for k in range(K):
                    ready(k)
                    for i, (a, b) in enumerate(PARTS):
                        ins = pe.matmul(wide[:, n % RING, :], weights[k][a], acts[k][b],
                                        start=(k == 0 and i == 0), stop=(k == K - 1 and i == 2))
                ins.then_inc(prod, 1)

            turn(0)

            def step(g, first, last):
                pe.wait_ge(xT_done, g + 1)
                if first:
                    pe.wait_ge(split, 2)
                for n in range(2 * HC):
                    c, v = n // 2, (w1 if n % 2 == 0 else w2)
                    product(g, n, first, [[v[i][:, c * P:(c + 1) * P] for i in (0, 1)]],
                            [[xT[i][:] for i in (0, 1)]], lambda k: None)
                for layer, h, a in ((0, h1, a1), (1, h2, a2)):
                    if first:
                        pe.wait_ge(split, 3 + layer)
                    for c in range(HC):
                        def ready(k, c=c, layer=layer):
                            if c == 0:
                                pe.wait_ge(parts, g * 2 * HC + layer * HC + k + 1)
                        product(g, (2 + layer) * HC + c, first,
                                [[h[i][:, k, c * P:(c + 1) * P] for i in (0, 1)] for k in range(HC)],
                                [[a[i][:, k, :] for i in (0, 1)] for k in range(HC)], ready)
                    if layer == 0 and not last:
                        turn(g + 1)
                if first:
                    pe.wait_ge(split, 5)
                else:
                    pe.wait_ge(update.read, g)
                pe.wait_ge(act_out, (g + 1) * 3 * HC)
                for t in range(TT):
                    for k in range(HC):
                        ins = pe.matmul(out[:, t, :], a3[:, k, t * P:(t + 1) * P], w3[:, k, :],
                                        start=(k == 0), stop=(k == HC - 1))
                ins.then_inc(out_done, 1)
            whole(pe, step)


def xattn_large(nc, s, cT_dram, w):
    NH, B = 16, 64
    HD = w["q"].shape[1] // NH
    HP = NH // 2
    CD = cT_dram.shape[0]
    SCALE = float(HD) ** -0.5
    TS = 2
    WIDE = TS * P
    NB = WIDE // B
    UH, UP = NH // 2, HP // 2
    STEPS = s.tiles // TS
    with ExitStack() as ctx:
        def sb(n, shape, dt=F32):
            return ctx.enter_context(nc.sbuf_tensor("c_" + n, shape, dt))

        def ps(n, shape):
            return ctx.enter_context(nc.psum_tensor("c_" + n, shape, F32))

        def sem(n):
            return s.sem("c_" + n)

        raw = {n: sb("raw_" + n, [r, HP, P]) for n, r in (("q", D), ("k", CD), ("v", CD))}
        parts = {n: [sb(f"w{n}_{i}", [r, HP, P], F32R) for i in "01"] for n, r in (("q", D), ("k", CD), ("v", CD))}
        wo, ob = sb("wo", [P, HP, D]), sb("ob", [P, D])
        xn = sb("xn", [P, TS, D])
        xT = [sb(f"xT_{i}", [P, WIDE], F32R) for i in "01"]
        cT = [sb(f"cT{b}", [CD, TS, 3 * B]) for b in "01"]
        cp = [sb(f"c_{i}", [CD, TS, 3 * B], F32R) for i in "01"]
        q = [sb(f"q{b}", [P, HP, WIDE]) for b in "01"]
        kz = [sb(f"kz{b}", [P, HP, NB, 2 * B]) for b in "01"]
        vz = [[sb(f"vz{b}_{t}", [P, 2, HP, 2 * HD]) for t in "01"] for b in "01"]
        top, total, inv = (sb(n, [P, 2, UH]) for n in ("top", "total", "inv"))
        e = [sb(f"e{u}", [P, UH, B]) for u in "01"]
        eT = sb("eT", [P, UP, P])
        oT = [sb(f"oT{t}", [P, HP, P]) for t in "01"]
        update = Update(s, sb, "c_", 1)
        scores = [ps(f"scores{u}", [P, UH, B]) for u in "01"]
        turned_e, att = ps("turned_e", [P, UP, P]), ps("att", [P, UP, P])
        misc = ps("misc", [P, 4, TOK])
        PROJ0, XT, Q0, K0, PROJ1, K1, V0 = 0, 1, 2, 6, 7, 8, 11

        def bank(job):
            return misc[:, job % 4, :]

        def k_bank(i):
            return bank(K0 if i == 0 else K1 + i - 1)

        w_in, vec_in = sem("weights_in"), sem("vectors_in")
        c_in = [sem("ctx_in0"), sem("ctx_in1")]
        w_hi, w_split, made = sem("weights_hi"), sem("weights_split"), sem("zeros_made")
        factors, normed = sem("norm_factors"), sem("normed")
        turned, x_hi, x_split = sem("xn_turned"), sem("x_hi"), sem("x_split")
        c_hi, c_split = sem("c_hi"), sem("c_split")
        q_prod, q_out = sem("q_product"), sem("q_out")
        k_prod, k_act, k_dve = sem("k_product"), sem("k_out_act"), sem("k_out_dve")
        v_prod, v_act, v_dve = sem("v_product"), sem("v_out_act"), sem("v_out_dve")
        proj_done = sem("projected")
        scored, top_done, shifted, exped, summed, inv_done, softmaxed = (sem(n) for n in (
            "scored", "top_done", "shifted", "exped", "summed", "inv_done", "softmaxed"))
        e_turned, eT_out, attended, oT_out = (sem(n) for n in ("e_turned", "eT_out", "attended", "oT_out"))
        block = ctx.enter_context(nc.Block())

        def bodies(eng, body):
            body(0, 0, True, True)
            with eng.Fori(0, STEPS // 2 - 1) as i:
                body(2 * i + 1, 1, True, True)
                body(2 * i + 2, 0, True, True)
            body(STEPS - 1, 1, True, False)
            body(STEPS, 0, False, False)

        def is0(g):
            return isinstance(g, int) and g == 0

        @block.sync
        def _(sp):
            def fetch(g, b):
                src = cT_dram[:, at(g * WIDE, WIDE)].rearrange("c (t k) -> c t k", k=P)
                sp.dma_start(cT[b][:, :, 0:P], src).then_inc(c_in[b], 16)
                sp.dma_start(cT[b][:, :, P:P + B], src[:, :, 0:B]).then_inc(c_in[b], 16)
            for n in ("q", "k", "v"):
                sp.dma_start(raw[n][:], w[n].rearrange("c (t d) -> c t d", d=P)).then_inc(w_in, 16)
            fetch(0, 0)
            sp.dma_start(wo[:], w["o"].rearrange("(k p) o -> p k o", p=P)).then_inc(vec_in, 16)
            sp.dma_start(ob[:], rows(w["ob"], D)).then_inc(vec_in, 16)

            def body(g, b, here, after):
                if after:
                    if not is0(g):
                        sp.wait_ge(c_split, g)
                    fetch(g + 1, 1 - b)
            bodies(sp, body)

        @block.gpsimd
        def _(pool):
            norm_factors(pool, s, factors)
            for b in (0, 1):
                pool.memset(kz[b][:], 0.0).then_inc(made, 1)
                for t in (0, 1):
                    pool.memset(vz[b][t][:], 0.0).then_inc(made, 1)

            def softmax_scale(n, u):
                pool.wait_ge(inv_done, n + 1)
                by = inv[:, u].rearrange("p (h a) -> p h a", a=1).broadcast_to([P, UH, B])
                pool.tensor_tensor(e[u][:], e[u][:], by, ALU.mult).then_inc(softmaxed, 1)

            def body(g, b, here, after):
                for p in range(4):
                    if (here or p == 0) and not (is0(g) and p == 0):
                        softmax_scale(4 * g + p - 1, (p + 1) % 2)
            bodies(pool, body)

        @block.scalar
        def _(act):
            def c_round(g, b):
                act.wait_ge(c_in[b], (g - b) * 16 + 32)
                if not is0(g):
                    act.wait_ge(v_prod, 4 * g)
                act.activation(cp[0][:], cT[b][:], ACT.Copy).then_inc(c_hi, 1)

            def q_evacuate(g, b, i):
                act.wait_ge(q_prod, 4 * g + i + 1)
                act.activation(q[b][:, 2 * i:2 * i + 2, :], bank(Q0 + i).rearrange("p (t k) -> p t k", t=2),
                               ACT.Copy, scale=SCALE).then_inc(q_out, 1)

            def k_evacuate(g, b, i):
                act.wait_ge(k_prod, 4 * g + i + 1)
                src = k_bank(i).rearrange("p (t b o k) -> p t b o k", t=2, o=2, k=B)
                for o in (0, 1):
                    dst = kz[b][0:HD, 2 * i:2 * i + 2, o::2, o * B:(o + 1) * B]
                    ins = act.activation(dst, src[0:HD, :, :, o, :], ACT.Copy)
                ins.then_inc(k_act, 1)

            def v_evacuate(g, b, i):
                act.wait_ge(v_prod, 4 * g + i + 1)
                odd = i % 2
                act.activation(vz[b][i // 2][0:B, odd, :, odd * HD:(odd + 1) * HD],
                               bank(V0 + i)[0:B, :].rearrange("p (t d) -> p t d", d=HD), ACT.Copy).then_inc(v_act, 1)

            def eT_evacuate(m):
                act.wait_ge(e_turned, m + 1)
                act.activation(eT[:], turned_e[:], ACT.Copy).then_inc(eT_out, 1)

            def oT_evacuate(m, u):
                act.wait_ge(attended, m + 1)
                half = u % 2
                act.activation(oT[u // 2][:, half * UP:(half + 1) * UP, :], att[:], ACT.Copy).then_inc(oT_out, 1)

            def exp(n, u):
                act.wait_ge(shifted, n + 1)
                act.activation(e[u][:], e[u][:], ACT.Exp).then_inc(exped, 1)

            c_round(0, 0)
            act.wait_ge(made, 6)
            for i in range(4):
                q_evacuate(0, 0, i)
            for i in range(4):
                k_evacuate(0, 0, i)
            for i in range(4):
                v_evacuate(0, 0, i)

            def body(g, b, here, after):
                for p in range(4):
                    n = 4 * g + p
                    behind = (not is0(g) or p >= 2) and (here or p < 2)
                    if p == 0 and after:
                        c_round(g + 1, 1 - b)
                    if behind:
                        eT_evacuate(n - 2)
                    if after:
                        for kind, i in SLOTS[p]["a"] + SLOTS[p]["b"]:
                            {"q": q_evacuate, "k": k_evacuate, "v": v_evacuate}.get(kind, lambda *_: None)(
                                g + 1, 1 - b, i)
                    if here:
                        exp(n, p % 2)
                    if behind:
                        oT_evacuate(n - 2, (p + 2) % 4)
                    if after:
                        for kind, i in SLOTS[p]["c"]:
                            {"q": q_evacuate, "k": k_evacuate, "v": v_evacuate}[kind](g + 1, 1 - b, i)
            bodies(act, body)

        @block.vector
        def _(dve):
            dve.wait_ge(w_in, 48)
            for n, name in enumerate(("q", "k", "v")):
                split(dve, parts[name][0][:], parts[name][1][:], raw[name][:], w_hi, n + 1, w_split)

            def x_parts(g, b, i):
                dve.wait_ge(turned, g + 1)
                split(dve, xT[0][:], xT[1][:], bank(XT)[:, 0:WIDE], x_hi, g + 1, x_split)

            def c_low(g, b):
                dve.wait_ge(c_hi, g + 1)
                dve.tensor_tensor(cp[1][:], cT[b][:], cp[0][:].bitcast(F32), ALU.subtract).then_inc(c_split, 1)

            def k_evacuate(g, b, i):
                dve.wait_ge(k_prod, 4 * g + i + 1)
                src = k_bank(i).rearrange("p (t b o k) -> p t b o k", t=2, o=2, k=B)
                for o in (0, 1):
                    dst = kz[b][HD:P, 2 * i:2 * i + 2, o::2, (1 - o) * B:(2 - o) * B]
                    ins = dve.tensor_copy(dst, src[HD:P, :, :, o, :])
                ins.then_inc(k_dve, 1)

            def v_evacuate(g, b, i):
                dve.wait_ge(v_prod, 4 * g + i + 1)
                odd = i % 2
                dve.tensor_copy(vz[b][i // 2][B:P, 1 - odd, :, odd * HD:(odd + 1) * HD],
                                bank(V0 + i)[B:P, :].rearrange("p (t d) -> p t d", d=HD)).then_inc(v_dve, 1)

            def softmax_shift(n, u):
                dve.wait_ge(scored, n + 1)
                dve.tensor_reduce(top[:, u], scores[u][:], AX.X, ALU.max).then_inc(top_done, 1)
                dve.wait_ge(top_done, n + 1)
                if not (isinstance(n, int) and n < 2):
                    dve.wait_ge(e_turned, n - 1)
                peak = top[:, u].rearrange("p (h a) -> p h a", a=1).broadcast_to([P, UH, B])
                dve.tensor_tensor(e[u][:], scores[u][:], peak, ALU.subtract).then_inc(shifted, 1)

            def softmax_sum(n, u):
                dve.wait_ge(exped, n + 1)
                dve.tensor_reduce(total[:, u], e[u][:], AX.X, ALU.add).then_inc(summed, 1)
                dve.wait_ge(summed, n + 1)
                dve.reciprocal(inv[:, u], total[:, u]).then_inc(inv_done, 1)

            def x_update(g, t):
                n = 2 * g + t + 1
                dve.wait_ge(proj_done, n)
                got = bank(PROJ1 if t else PROJ0)[:, 0:D].rearrange("p (a d) -> p a d", a=1)
                update.run(dve, got, ob[:].rearrange("p (a d) -> p a d", a=1), g * TS + t, n)

            c_low(0, 0)
            dve.wait_ge(factors, 4)
            normalise(dve, s, xn, 0, TS, normed)
            x_parts(0, 0, 0)
            dve.wait_ge(made, 6)
            for i in range(4):
                k_evacuate(0, 0, i)
            for i in range(4):
                v_evacuate(0, 0, i)
            dve.wait_ge(vec_in, 32)

            def jobs(g, b, slot, after):
                for kind, i in slot:
                    if kind == "proj":
                        if not is0(g):
                            x_update(g - 1, i)
                    elif after and kind in "kvx":
                        {"k": k_evacuate, "v": v_evacuate, "x": x_parts}[kind](g + 1, 1 - b, i)

            def body(g, b, here, after):
                for p in range(4):
                    n = 4 * g + p
                    if p == 0 and after:
                        dve.wait_ge(turned, g + 1)
                        normalise(dve, s, xn, (g + 1) * TS, TS, normed)
                    if (here or p == 0) and not (is0(g) and p == 0):
                        softmax_sum(n - 1, (p + 1) % 2)
                    jobs(g, b, SLOTS[p]["a"], after)
                    if here:
                        softmax_shift(n, p % 2)
                    if p == 1 and after:
                        c_low(g + 1, 1 - b)
                    jobs(g, b, SLOTS[p]["b"] + SLOTS[p]["c"], after)
            bodies(dve, body)
            dve.wait_ge(update.done, 2 * STEPS)

        @block.tensor
        def _(pe):
            def both(act_sem, dve_sem, count):
                pe.wait_ge(act_sem, count)
                pe.wait_ge(dve_sem, count)

            def turn_x(g, b, i, start=False):
                if not start:
                    both(v_act, v_dve, 4 * g - 1)
                pe.wait_ge(normed, (g + 1) * TS)
                for t in range(TS):
                    ins = pe.transpose(bank(XT)[:, t * P:(t + 1) * P], xn[:, t, :], s.ident[:])
                ins.then_inc(turned, 1)

            def make_q(g, b, i, start=False):
                if i == 3:
                    pe.wait_ge(x_split, g + 1)
                elif not start and i < 2:
                    both(v_act, v_dve, 4 * g)
                elif not start and is1(g):
                    both(v_act, v_dve, 4 * g)
                elif not start:
                    pe.wait_ge(update.read, 2 * g - 3)
                pe.wait_ge(x_split, g + 1)
                for j in range(2):
                    for k, (a, c) in enumerate(PARTS):
                        ins = pe.matmul(bank(Q0 + i)[:, j * WIDE:(j + 1) * WIDE], parts["q"][a][:, 2 * i + j, :],
                                        xT[c][:], start=(k == 0), stop=(k == 2))
                ins.then_inc(q_prod, 1)

            def make_k(g, b, i, start=False):
                if i < 3:
                    pe.wait_ge(q_out, 4 * g + (1, 3, 4)[i])
                else:
                    both(k_act, k_dve, 4 * g + 1)
                pe.wait_ge(c_split, g + 1)
                for j in range(2):
                    for k, (a, c) in enumerate(PARTS):
                        ins = pe.matmul(k_bank(i)[:, j * WIDE:(j + 1) * WIDE], parts["k"][a][:, 2 * i + j, :],
                                        cp[c][:, :, 0:P], start=(k == 0), stop=(k == 2))
                ins.then_inc(k_prod, 1)

            def make_v(g, b, i, start=False):
                if i > 0:
                    both(k_act, k_dve, 4 * g + i + 1)
                elif start or is1(g):
                    pe.wait_ge(q_out, 4 * g + 2)
                else:
                    pe.wait_ge(update.read, 2 * g - 2)
                t, odd = i // 2, i % 2
                for k, (a, c) in enumerate(PARTS):
                    ins = pe.matmul(bank(V0 + i), cp[c][:, t, odd * B:odd * B + P],
                                    parts["v"][a][:, :, odd * HD:(odd + 1) * HD], start=(k == 0), stop=(k == 2))
                ins.then_inc(v_prod, 1)

            def project(g, t):
                pe.wait_ge(oT_out, 4 * g + 2 * t + 2)
                for k in range(HP):
                    ins = pe.matmul(bank(PROJ1 if t else PROJ0)[:, 0:D], oT[t][:, k, :], wo[:, k, :],
                                    start=(k == 0), stop=(k == HP - 1))
                ins.then_inc(proj_done, 1)

            def is1(g):
                return isinstance(g, int) and g == 1

            def score(g, b, p, n):
                if not (isinstance(n, int) and n < 2):
                    pe.wait_ge(shifted, n - 1)
                t, hh = p // 2, p % 2
                for j in range(UP):
                    for half in (0, 1):
                        h = hh * UP + j
                        ins = pe.matmul(
                            scores[p % 2][half * B:(half + 1) * B, 2 * j:2 * j + 2, :].rearrange("q h k -> q (h k)"),
                            q[b][:, h, t * P + half * B:t * P + (half + 1) * B], kz[b][:, h, 2 * t + half, :],
                            start=True, stop=True)
                ins.then_inc(scored, 1)

            def turn_e(m, u):
                pe.wait_ge(softmaxed, m + 1)
                for j in range(UP):
                    ins = pe.transpose(turned_e[:, j, :], e[u][:, 2 * j:2 * j + 2, :].rearrange("q h k -> q (h k)"),
                                       s.ident[:])
                ins.then_inc(e_turned, 1)

            def attend(m, b, p):
                pe.wait_ge(eT_out, m + 1)
                if not (isinstance(m, int) and m == 0):
                    pe.wait_ge(oT_out, m)
                for j in range(UP):
                    for half in (0, 1):
                        ins = pe.matmul(att[:, j, half * B:(half + 1) * B],
                                        vz[b][p // 2][:, half, (p % 2) * UP + j, :],
                                        eT[:, j, half * B:(half + 1) * B], start=True, stop=True)
                ins.then_inc(attended, 1)

            make = {"x": turn_x, "q": make_q, "k": make_k, "v": make_v}
            turn_x(0, 0, 0, True)
            pe.wait_ge(w_split, 3)
            for kind in "qkv":
                for i in range(4):
                    make[kind](0, 0, i, True)
            pe.wait_ge(vec_in, 32)

            def jobs(g, b, slot, here, after):
                for kind, i in slot:
                    if kind == "proj":
                        if not is0(g):
                            if i == 0 and here:
                                both(v_act, v_dve, 4 * g + 2)
                            elif i == 1 and after:
                                pe.wait_ge(q_out, 4 * (g + 1) + 2)
                            project(g - 1, i)
                    elif after:
                        make[kind](g + 1, 1 - b, i)

            def body(g, b, here, after):
                for p in range(4):
                    n = 4 * g + p
                    behind = (not is0(g) or p >= 2) and (here or p < 2)
                    mb = b if p >= 2 else 1 - b
                    if behind:
                        turn_e(n - 2, p % 2)
                    jobs(g, b, SLOTS[p]["a"], here, after)
                    if here:
                        if p == 0:
                            pe.wait_ge(q_out, 4 * g + 4)
                            both(k_act, k_dve, 4 * g + 4)
                        score(g, b, p, n)
                    jobs(g, b, SLOTS[p]["b"], here, after)
                    if behind:
                        if p == 2 and here:
                            both(v_act, v_dve, 4 * g + 4)
                        attend(n - 2, mb, (p + 2) % 4)
                    jobs(g, b, SLOTS[p]["c"], here, after)
            bodies(pe, body)


SLOTS = (
    {"a": (), "b": (("x", 0), ("proj", 0)), "c": (("q", 0),)},
    {"a": (("q", 1),), "b": (("q", 2),), "c": (("q", 3),)},
    {"a": (("k", 0),), "b": (("proj", 1), ("k", 1)), "c": (("k", 2),)},
    {"a": (("k", 3),), "b": (("v", 0), ("v", 1)), "c": (("v", 2), ("v", 3))},
)


def ffn_expert(nc, s, w, y_dram):
    H = w["w1"].shape[1]
    HC = H // P
    STEPS = s.tiles // TT
    with ExitStack() as ctx:
        def sb(n, shape, dt=F32):
            return ctx.enter_context(nc.sbuf_tensor("d_" + n, shape, dt))

        def ps(n, shape):
            return ctx.enter_context(nc.psum_tensor("d_" + n, shape, F32))

        def sem(n):
            return s.sem("d_" + n)

        raw1 = sb("raw1", [P, H])
        w1 = [sb(f"w1_{i}", [P, H], F32R) for i in "01"]
        w2, b1 = sb("w2", [P, HC, D]), sb("b1", [P, HC])
        b2, gamma, beta = sb("b2", [P, D]), sb("gamma", [P, D]), sb("beta", [P, D])
        power, eps, zero = sb("power", [P, TT]), sb("eps", [P, TT]), sb("zero", [P, TT])
        xn = sb("xn", [P, 2, TT, D])
        xT = [sb(f"xT_{i}", [P, TOK], F32R) for i in "01"]
        a = sb("a", [P, HC, TOK])
        z = sb("z", [P, 2, TT, D])
        stats, moments = sb("stats", [P, TT, 6]), sb("step_moments", [P, 2, TT, 2])
        variance, product = sb("step_variance", [P, TT]), sb("step_product", [P, TT])
        rstd, shift = sb("step_rstd", [P, 2, TT]), sb("step_shift", [P, 2, TT])
        y = sb("y", [P, 2, TT, D])
        wide, turned, out = ps("wide", [P, HC, TOK]), ps("turned", [P, TOK]), ps("out", [P, 2, TT, D])
        yv = y_dram.rearrange("(t p) d -> p t d", p=P)

        w_in, vec_in, split = sem("weights_in"), sem("vectors_in"), sem("weights_split")
        factors, normed = sem("norm_factors"), sem("normed")
        turned_done, xT_done = sem("turned_done"), sem("xT_done")
        prod, act_out = sem("products"), sem("act_out")
        out_done = sem("out_done")
        z_done = sem("z_done")
        shift_done, made = sem("shift_done"), sem("constants_made")
        pool_chain, chain = sem("pool_chain"), sem("dve_chain")
        y_done = sem("y_done")
        stored = [sem("stored0"), sem("stored1")]
        block = ctx.enter_context(nc.Block())

        def pairs(eng, step):
            step(0, 0, True, False)
            step(1, 1, False, False)
            with eng.Fori(2, STEPS - 2, 2) as g:
                step(g, 0, False, False)
                step(g + 1, 1, False, False)
            step(STEPS - 2, 0, False, False)
            step(STEPS - 1, 1, False, True)

        @block.sync
        def _(sp):
            sp.dma_start(raw1[:], w["w1"]).then_inc(w_in, 16)
            sp.dma_start(w2[:], w["w2"].rearrange("(k p) o -> p k o", p=P)).then_inc(vec_in, 16)
            sp.dma_start(b1[:], w["b1"]).then_inc(vec_in, 16)
            for v, n in ((b2, "b2"), (gamma, "gamma"), (beta, "beta")):
                sp.dma_start(v[:], rows(w[n], D)).then_inc(vec_in, 16)

            def step(g, b, first, last):
                sp.wait_ge(y_done, g + 1)
                sp.dma_start(yv[:, at(g * TT, TT), :], y[:, b]).then_inc(stored[b], 16)
            pairs(sp, step)
            for b in (0, 1):
                sp.wait_ge(stored[b], 16 * (STEPS // 2))

        @block.gpsimd
        def _(pool):
            for tile, value in ((power, -0.5), (eps, EPS), (zero, 0.0)):
                pool.memset(tile[:], value).then_inc(made, 1)
            norm_factors(pool, s, factors)
            pool.wait_ge(made, 3)
            link = Chain(pool, pool_chain)

            def step(g, b, first, last):
                link.start(g * 3)
                pool.wait_ge(z_done, g + 1)
                if not (isinstance(g, int) and g < 2):
                    pool.wait_ge(y_done, g - 1)
                link.then(pool.tensor_tensor(variance[:], moments[:, b, :, 1], eps[:], ALU.add))
                link.then(pool.tensor_tensor(rstd[:, b], variance[:], power[:], ALU.pow))
                link.then(pool.tensor_tensor(product[:], moments[:, b, :, 0], rstd[:, b], ALU.mult))
                pool.tensor_tensor(shift[:, b], zero[:], product[:], ALU.subtract).then_inc(shift_done, 1)
                pool.wait_ge(shift_done, g + 1)
            pairs(pool, step)

        @block.scalar
        def _(act):
            act.wait_ge(vec_in, 16 * 5)

            def step(g, b, first, last):
                for c in range(HC):
                    act.wait_ge(prod, g * HC + c + 1)
                    if c == 0 and not first:
                        act.wait_ge(out_done, g)
                    act.activation(a[:, c, :], wide[:, c, :], ACT.Relu, bias=b1[:, c:c + 1]).then_inc(act_out, 1)
            pairs(act, step)

        @block.vector
        def _(dve):
            link = Chain(dve, chain)
            dve.wait_ge(w_in, 16)
            link.then(dve.tensor_copy(w1[0][:], raw1[:]))
            dve.tensor_tensor(w1[1][:], raw1[:], w1[0][:].bitcast(F32), ALU.subtract).then_inc(split, 1)

            def split_x(g):
                dve.wait_ge(turned_done, g + 1)
                link.then(dve.tensor_copy(xT[0][:], turned[:]))
                dve.tensor_tensor(xT[1][:], turned[:], xT[0][:].bitcast(F32), ALU.subtract).then_inc(xT_done, 1)
            dve.wait_ge(factors, 4)
            normalise(dve, s, xn[:, 0], 0, TT, normed)
            split_x(0)
            dve.wait_ge(vec_in, 16 * 5)
            before = link.base

            def bcast(v):
                return v[:].rearrange("p (a d) -> p a d", a=1).broadcast_to([P, TT, D])

            def make_z(g, b, after):
                dve.wait_ge(out_done, g + 1)
                link.then(dve.tensor_tensor(z[:, b], out[:, b], xn[:, b], ALU.add))
                link.then(dve.tensor_tensor(z[:, b], z[:, b], bcast(b2), ALU.add))
                for t in range(TT):
                    ins = dve.bn_stats(stats[:, t, :], z[:, b, t, :])
                link.then(ins)
                if after:
                    normalise(dve, s, xn[:, b], (g + 2) * TT, TT, normed)
                else:
                    dve.tensor_scalar(z[:, b], z[:, b], 1.0, None, ALU.mult)
                for t in range(TT):
                    ins = dve.bn_aggr(moments[:, b, t, :], stats[:, t, :])
                ins.then_inc(z_done, 1)

            def make_y(g, b):
                dve.wait_ge(shift_done, g + 1)
                if not (isinstance(g, int) and g < 2):
                    dve.wait_ge(stored[b], (g - b) * 8)
                for t in range(TT):
                    ins = dve.tensor_scalar(y[:, b, t, :], z[:, b, t, :], rstd[:, b, t:t + 1],
                                            shift[:, b, t:t + 1], ALU.mult, ALU.add)
                link.then(ins)
                link.then(dve.tensor_tensor(y[:, b], y[:, b], bcast(gamma), ALU.mult))
                link.then(dve.tensor_tensor(y[:, b], y[:, b], bcast(beta), ALU.add))
                dve.tensor_tensor(y[:, b], y[:, b], s.x[:, at(g * TT, TT), :], ALU.add).then_inc(y_done, 1)

            def step(g, b, first, last):
                if isinstance(g, int) and g < 2:
                    link.start(before + g)
                else:
                    link.start(before + 5 + (g - 2) * 7)
                if first:
                    normalise(dve, s, xn[:, 1], TT, TT, normed)
                else:
                    make_z(g - 1, 1 - b, not last)
                if not (isinstance(g, int) and g < 2):
                    make_y(g - 2, b)
                if not last:
                    split_x(g + 1)
            pairs(dve, step)
            make_y(STEPS - 2, 0)
            make_z(STEPS - 1, 1, False)
            make_y(STEPS - 1, 1)
            dve.wait_ge(y_done, STEPS)

        @block.tensor
        def _(pe):
            def turn(g, b):
                pe.wait_ge(normed, (g + 1) * TT)
                for t in range(TT):
                    ins = pe.transpose(turned[:, t * P:(t + 1) * P], xn[:, b, t, :], s.ident[:])
                ins.then_inc(turned_done, 1)
            turn(0, 0)
            pe.wait_ge(split, 1)

            def step(g, b, first, last):
                pe.wait_ge(xT_done, g + 1)
                for c in range(HC):
                    if not first:
                        pe.wait_ge(act_out, (g - 1) * HC + c + 1)
                    for i, (p, q) in enumerate(PARTS):
                        ins = pe.matmul(wide[:, c, :], w1[p][:, c * P:(c + 1) * P], xT[q][:],
                                        start=(i == 0), stop=(i == 2))
                    ins.then_inc(prod, 1)
                if not last:
                    turn(g + 1, 1 - b)
                if first:
                    pe.wait_ge(vec_in, 16 * 5)
                if not (isinstance(g, int) and g < 2):
                    pe.wait_ge(z_done, g - 1)
                pe.wait_ge(act_out, (g + 1) * HC)
                for t in range(TT):
                    for k in range(HC):
                        ins = pe.matmul(out[:, b, t, :], a[:, k, t * P:(t + 1) * P], w2[:, k, :],
                                        start=(k == 0), stop=(k == HC - 1))
                ins.then_inc(out_done, 1)
            pairs(pe, step)


def attention_stack(nc, a, y):
    with ExitStack() as ctx:
        s = Stream(nc, ctx, a["x"].shape[0])
        load_stream(nc, s, a["x"])
        xattn_small(nc, s, a["ctxT"], dict(q=a["q0_w"], qb=a["q0_b"], kv=a["kv0_w"], kb=a["k0_b"], vb=a["v0_b"],
                                           o=a["o0_w"], ob=a["o0_b"]))
        ffn_gated(nc, s, dict(w1=a["w1"], w2=a["w2"], h1=a["h1"], h2=a["h2"], w3=a["w3"], w1s=a["w1_s"],
                              w2s=a["w2_s"], h1s=a["h1_s"], h2s=a["h2_s"], w3s=a["w3_s"]))
        xattn_large(nc, s, a["ctxT"], dict(q=a["q1_w"], k=a["k1_w"], v=a["v1_w"], o=a["o1_w"], ob=a["o1_b"]))
        ffn_expert(nc, s, dict(w1=a["e_w1"], b1=a["e_b1"], w2=a["e_w2"], b2=a["e_b2"], gamma=a["gamma"],
                               beta=a["beta"]), y)


def kernel(x, ctx_768, L0_xattn_q_w, L0_xattn_q_b, L0_xattn_kv_w, L0_xattn_kv_b, L0_xattn_proj_w, L0_xattn_proj_b,
           L0_ffn_w1_w, L0_ffn_w1_s, L0_ffn_w2_w, L0_ffn_w2_s, L0_ffn_h1_w, L0_ffn_h1_s, L0_ffn_h2_w, L0_ffn_h2_s,
           L0_ffn_w3_w, L0_ffn_w3_s, L1_xattn_w_q, L1_xattn_w_k, L1_xattn_w_v, L1_xattn_w_out, L1_xattn_b_out,
           L1_ffn_router_w, L1_ffn_router_b, L1_ffn_w1, L1_ffn_b1, L1_ffn_w2, L1_ffn_b2, L1_ffn_gamma,
           L1_ffn_beta):
    import numpy as np
    import concourse.bacc as bacc
    from concourse.bass_utils import run_bass_kernel_spmd

    def by_chunk(v):
        return np.asarray(v).reshape(-1, P).T

    batches, length, width = x.shape
    tokens = batches * length
    operands = {
        "x": np.asarray(x).reshape(tokens, width),
        "ctxT": np.asarray(ctx_768).reshape(tokens, -1).T,
        "q0_w": L0_xattn_q_w, "q0_b": by_chunk(L0_xattn_q_b), "kv0_w": L0_xattn_kv_w,
        "k0_b": by_chunk(np.asarray(L0_xattn_kv_b)[:width]), "v0_b": np.asarray(L0_xattn_kv_b)[width:],
        "o0_w": L0_xattn_proj_w, "o0_b": L0_xattn_proj_b,
        "w1": np.asarray(L0_ffn_w1_w).T, "w1_s": by_chunk(L0_ffn_w1_s),
        "w2": np.asarray(L0_ffn_w2_w).T, "w2_s": by_chunk(L0_ffn_w2_s),
        "h1": np.asarray(L0_ffn_h1_w).T, "h1_s": by_chunk(L0_ffn_h1_s),
        "h2": np.asarray(L0_ffn_h2_w).T, "h2_s": by_chunk(L0_ffn_h2_s),
        "w3": np.asarray(L0_ffn_w3_w).T, "w3_s": L0_ffn_w3_s,
        "q1_w": L1_xattn_w_q, "k1_w": L1_xattn_w_k, "v1_w": L1_xattn_w_v, "o1_w": L1_xattn_w_out,
        "o1_b": L1_xattn_b_out,
        "e_w1": np.asarray(L1_ffn_w1)[0], "e_b1": by_chunk(np.asarray(L1_ffn_b1)[0]),
        "e_w2": np.asarray(L1_ffn_w2)[0], "e_b2": np.asarray(L1_ffn_b2)[0],
        "gamma": L1_ffn_gamma, "beta": L1_ffn_beta,
    }
    nc = bacc.Bacc("TRN2", target_bir_lowering=False, num_devices=1)
    arrays, aps = {}, {}
    for name, a in operands.items():
        arrays[f"in_{name}"] = np.ascontiguousarray(a)
        aps[name] = nc.dram_tensor(f"in_{name}", list(arrays[f"in_{name}"].shape), F32, kind="ExternalInput").ap()
    y = nc.dram_tensor("out_y", [tokens, width], F32, kind="ExternalOutput").ap()
    attention_stack(nc, aps, y)
    result = run_bass_kernel_spmd(nc, [arrays], core_ids=[0])
    return result.results[0]["out_y"].reshape(batches, length, width)
```

```python
from contextlib import ExitStack

import concourse.bass as bass
from concourse import mybir

ALU = mybir.AluOpType
ACT = mybir.ActivationFunctionType
AX = mybir.AxisListType
F32 = mybir.dt.float32
F32R = mybir.dt.float32r

P = 128
D = 128
TOK = 512
TT = TOK // P
EPS = 1e-5
PARTS = ((0, 0), (1, 0), (0, 1))


class Stream:

    def __init__(self, nc, ctx, tokens):
        def sb(name, shape):
            return ctx.enter_context(nc.sbuf_tensor(name, shape, F32))
        self.nc, self.ctx = nc, ctx
        self.tiles = tokens // P
        self.x = sb("x", [P, self.tiles, D])
        self.moments = sb("moments", [P, self.tiles, 2])
        self.rstd = sb("rstd", [P, self.tiles])
        self.shift = sb("shift", [P, self.tiles])
        self.ident = sb("ident", [P, P])
        self.power = sb("power", [P, self.tiles])
        self.stats = sb("load_stats", [P, self.tiles, 6])
        self.x_in = [self.sem(f"x_in{c}") for c in range(4)]
        self.stats_done, self.moments_done = self.sem("stats_done"), self.sem("moments_done")

    def sem(self, name):
        return self.ctx.enter_context(self.nc.semaphore(name))


def fetch_x(sp, s, x_dram, part):
    half = (EARLY if part < 2 else s.tiles - EARLY) // 2
    first = (0 if part < 2 else EARLY) + part % 2 * half
    sp.dma_start(s.x[:, first:first + half, :], x_dram.rearrange("(t p) d -> p t d", p=P)[
        :, first:first + half, :]).then_inc(s.x_in[part], 16)


def find_moments(dve, s, first, end):
    for t in range(first, end):
        dve.bn_stats(s.stats[:, t, :], s.x[:, t, :]).then_inc(s.stats_done, 1)
    for t in range(first, end):
        dve.wait_ge(s.stats_done, t + 1)
        dve.bn_aggr(s.moments[:, t, :], s.stats[:, t, :]).then_inc(s.moments_done, 1)


def rows(vec, n):
    return vec.rearrange("(a n) -> a n", a=1).broadcast_to([P, n])


def at(i, n=1):
    return slice(i, i + n) if isinstance(i, int) else bass.ds(i, n)


def norm_factors(pool, s, done, tiles, n):
    rstd, shift = s.rstd[:, tiles], s.shift[:, tiles]
    pool.tensor_scalar(rstd, s.moments[:, tiles, 1], EPS, 1.0, ALU.add, ALU.mult).then_inc(done, 1)
    pool.wait_ge(done, n + 1)
    pool.tensor_tensor(rstd, rstd, s.power[:, tiles], ALU.pow).then_inc(done, 1)
    pool.wait_ge(done, n + 2)
    pool.tensor_tensor(shift, s.moments[:, tiles, 0], rstd, ALU.mult).then_inc(done, 1)
    pool.wait_ge(done, n + 3)
    pool.tensor_scalar(shift, shift, -1.0, 0.0, ALU.mult, ALU.add).then_inc(done, 1)
    pool.wait_ge(done, n + 4)


EARLY = 16
FIRST, LATER = slice(0, 8), slice(8, None)


def normalise(dve, s, xn, first_tile, tiles, normed):
    for t in range(tiles):
        i = first_tile + t
        dve.tensor_scalar(xn[:, t, :], s.x[:, at(i), :], s.rstd[:, at(i)], s.shift[:, at(i)],
                           ALU.mult, ALU.add).then_inc(normed, 1)


class Update:

    def __init__(self, s, sb, prefix, tiles):
        self.s, self.tiles = s, tiles
        self.fresh, self.stats = sb("fresh", [P, tiles, D]), sb("stats", [P, tiles, 6])
        self.pair = sb("pair", [P, tiles, 2])
        self.read, self.added, self.measured, self.stored, self.gathered, self.done = (
            s.sem(prefix + n) for n in ("x_got_read", "x_added", "x_measured", "x_stored", "x_gathered", "x_done"))

    def take(self, dve, got, other, n):
        if not (isinstance(n, int) and n == 1):
            dve.wait_ge(self.stored, n - 1)
        dve.tensor_tensor(self.fresh[:], got, other, ALU.add).then_inc(self.read, 1)

    def finish(self, dve, first_tile, n, add_x=True):
        s, x = self.s, self.s.x[:, at(first_tile, self.tiles), :]
        dve.wait_ge(self.read, n)
        if add_x:
            dve.tensor_tensor(self.fresh[:], self.fresh[:], x, ALU.add).then_inc(self.added, 1)
            dve.wait_ge(self.added, n)
        for t in range(self.tiles):
            ins = dve.bn_stats(self.stats[:, t, :], self.fresh[:, t, :])
        ins.then_inc(self.measured, 1)
        dve.wait_ge(self.measured, n)
        dve.tensor_scalar(x, self.fresh[:], 1.0, None, ALU.mult).then_inc(self.stored, 1)
        for t in range(self.tiles):
            ins = dve.bn_aggr(self.pair[:, t, :], self.stats[:, t, :])
        ins.then_inc(self.gathered, 1)
        dve.wait_ge(self.gathered, n)
        dve.tensor_scalar(s.moments[:, at(first_tile, self.tiles), :], self.pair[:], 1.0, None,
                          ALU.mult).then_inc(self.done, 1)

    def run(self, dve, got, bias, first_tile, n):
        x = self.s.x[:, at(first_tile, self.tiles), :]
        self.take(dve, got, x if bias is None else bias, n)
        self.finish(dve, first_tile, n, bias is not None)


def load_stream(nc, s, x_dram):
    zeroed, made = s.sem("ident_zeroed"), s.sem("constants_made")
    with nc.Block() as block:
        @block.sync
        def _(sp):
            fetch_x(sp, s, x_dram, 0)
            fetch_x(sp, s, x_dram, 1)

        @block.gpsimd
        def _(pool):
            pool.memset(s.ident[:], 0.0).then_inc(zeroed, 1)
            pool.memset(s.power[:], -0.5).then_inc(made, 1)
            pool.wait_ge(zeroed, 1)
            pool.affine_select(out=s.ident[:], in_=s.ident[:], compare_op=ALU.not_equal, fill=1.0, base=0,
                               pattern=[[-1, P]], channel_multiplier=1).then_inc(made, 1)
            pool.wait_ge(made, 2)

        @block.vector
        def _(dve):
            for part in (0, 1):
                dve.wait_ge(s.x_in[part], 16)
                find_moments(dve, s, part * EARLY // 2, (part + 1) * EARLY // 2)
            dve.wait_ge(s.moments_done, EARLY)


class Chain:

    def __init__(self, eng, sem):
        self.eng, self.sem, self.base = eng, sem, 0

    def start(self, base):
        self.base = base

    def then(self, ins):
        ins.then_inc(self.sem, 1)
        self.base = self.base + 1
        self.eng.wait_ge(self.sem, self.base)


def split(dve, hi, lo, src, hi_sem, hi_count, lo_sem):
    dve.tensor_copy(hi, src).then_inc(hi_sem, 1)
    dve.wait_ge(hi_sem, hi_count)
    dve.tensor_tensor(lo, src, hi.bitcast(F32), ALU.subtract).then_inc(lo_sem, 1)


def xattn_small(nc, s, x_dram, cT_dram, w):
    NH, HD, B = 16, D // 16, 64
    HP = NH // 2
    CD = cT_dram.shape[0]
    SCALE = float(HD) ** -0.5
    ROWS = 4 * HD
    NB = TOK // B
    STEPS = s.tiles // TT
    V1 = HD + 1
    with ExitStack() as ctx:
        def sb(n, shape, dt=F32):
            return ctx.enter_context(nc.sbuf_tensor("a_" + n, shape, dt))

        def ps(n, shape):
            return ctx.enter_context(nc.psum_tensor("a_" + n, shape, F32))

        def sem(n):
            return s.sem("a_" + n)

        raw_q, raw_kv = sb("raw_q", [P, D]), sb("raw_kv", [CD, 2 * D])
        wq, wk = [sb(f"wq_{i}", [P, D], F32R) for i in "01"], [sb(f"wk_{i}", [CD, D], F32R) for i in "01"]
        wo, qb, kb = sb("wo", [P, D]), sb("qb", [P, 1]), sb("kb", [P, 1])
        qbs = sb("qb_scaled", [P, 1])
        vb, ob = sb("vb", [P, D]), sb("ob", [P, D])
        xn = sb("xn", [P, TT, D])
        xT = [sb(f"xT_{i}", [P, TOK], F32R) for i in "01"]
        cT = [sb(f"cT{b}", [CD, NB, 2, B]) for b in "01"]
        cp = [sb(f"c_{i}", [CD, TOK], F32R) for i in "01"]
        qf, kf = sb("qf", [P, TOK]), sb("kf", [P, TOK])
        kp = [sb(f"k_{i}", [P, TOK]) for i in "01"]
        qz = [[sb(f"qz{b}_{i}", [P, NH // 4, TT, 3 * B], F32R) for i in "01"] for b in "01"]
        zero = sb("zero", [P, 1])
        kz = [[sb(f"kz{b}_{i}", [P, 4, TOK], F32R) for i in "01"] for b in "01"]
        vz = [sb(f"vz{b}", [P, TT, HP, 2, 2 * V1]) for b in "01"]
        head_rows, mask = sb("head_rows", [P, NH]), sb("mask", [P, 4])
        top = sb("top", [P, 2, NH])
        e = [sb(f"e{u}", [P, NH, B]) for u in "01"]
        eT = sb("eT", [P, HP, P])
        inv = sb("inv", [P, 2, HP, 2])
        o = sb("o", [P, TT, D])
        oT = sb("oT", [P, TOK])
        update = Update(s, sb, "a_", TT)
        scores = [ps(f"scores{u}", [P, NH, B]) for u in "01"]
        turned_e, att, misc = ps("turned_e", [P, HP, P]), ps("att", [P, HP, 2, 2, V1]), ps("misc", [P, TOK])

        w_in, vec_in = sem("weights_in"), sem("vectors_in")
        c_in = [sem("ctx_in0"), sem("ctx_in1")]
        w_hi, w_split = sem("weights_hi"), sem("weights_split")
        made, made_1, mask_made = sem("constants_made"), sem("parity_1_cleared"), sem("mask_made")
        factors, normed = sem("norm_factors"), sem("normed")
        turned, x_hi, x_split = sem("xn_turned"), sem("x_hi"), sem("x_split")
        c_hi, c_split = sem("c_hi"), sem("c_split")
        q_prod, q_out, q_hi, q_split = sem("q_product"), sem("q_out"), sem("q_hi"), sem("q_split")
        k_prod, k_out, k_hi, k_split, k_masked = (sem(n) for n in ("k_product", "k_out", "k_hi", "k_split",
                                                                  "k_masked"))
        v_prod, v_out = sem("v_product"), sem("v_out")
        o_turned, o_out, proj_done = sem("o_turned"), sem("o_out"), sem("projected")
        scored, top_done, shifted, exped = sem("scored"), sem("top_done"), sem("shifted"), sem("exped")
        e_turned = sem("e_turned")
        eT_act, eT_dve = sem("eT_by_act"), sem("eT_by_dve")
        attended, inv_done, normal = sem("attended"), sem("inv_done"), sem("o_normalised")
        block = ctx.enter_context(nc.Block())

        def exists(g):
            return not isinstance(g, int) or 0 <= g < STEPS

        def bodies(eng, body):
            body(0, 0)
            body(1, 1)
            with eng.Fori(1, STEPS // 2 - 1) as i:
                body(2 * i, 0)
                body(2 * i + 1, 1)
            body(STEPS - 2, 0)
            body(STEPS - 1, 1)
            body(STEPS, 0)

        def by_batch(t):
            return t[:].rearrange("c (b k) -> c b k", k=B)

        def is0(g):
            return isinstance(g, int) and g == 0

        def clear_queries(eng, b, i, done):
            eng.memset(qz[b][i][:].bitcast(F32), 0.0).then_inc(done, 1)

        def clear_values(eng, b, done, n):
            eng.memset(vz[b][:], 0.0).then_inc(done, 1)
            eng.wait_ge(done, n + 1)
            eng.memset(vz[b][0:B, :, :, :, HD:V1], 1.0).then_inc(done, 1)
            eng.memset(vz[b][B:P, :, :, :, V1 + HD:2 * V1], 1.0).then_inc(done, 1)
        CLEARED = 9

        @block.sync
        def _(sp):
            def fetch(sp, g, b):
                for copy in (0, 1):
                    sp.dma_start(cT[b][:, :, copy, :], cT_dram[:, at(g * TOK, TOK)].rearrange(
                        "c (b k) -> c b k", k=B)).then_inc(c_in[b], 16)

            sp.dma_start(raw_q[:], w["q"]).then_inc(w_in, 16)
            sp.dma_start(raw_kv[:], w["kv"]).then_inc(w_in, 16)
            fetch(sp, 0, 0)
            sp.dma_start(qb[:], w["qb"]).then_inc(vec_in, 16)
            sp.dma_start(kb[:], w["kb"]).then_inc(vec_in, 16)
            sp.dma_start(vb[:], rows(w["vb"], D)).then_inc(vec_in, 16)
            sp.dma_start(ob[:], rows(w["ob"], D)).then_inc(vec_in, 16)
            sp.dma_start(wo[:], w["o"]).then_inc(vec_in, 16)

            def body(g, b):
                after = exists(g + 1)
                if after:
                    if not is0(g):
                        sp.wait_ge(v_prod, 2 * g)
                    fetch(sp, g + 1, 1 - b)
                if is0(g):
                    fetch_x(sp, s, x_dram, 2)
                    fetch_x(sp, s, x_dram, 3)
            bodies(sp, body)

        @block.gpsimd
        def _(pool):
            norm_factors(pool, s, factors, slice(0, EARLY), 0)
            pool.memset(zero[:], 0.0).then_inc(made, 1)
            pool.memset(head_rows[:], 1.0).then_inc(made, 1)
            pool.wait_ge(made, 2)
            pool.affine_select(out=head_rows[:], in_=head_rows[:], compare_op=ALU.is_ge, fill=0.0, base=0,
                               pattern=[[-HD, NH]], channel_multiplier=1).then_inc(made, 1)
            pool.wait_ge(made, 3)
            pool.affine_select(out=head_rows[:], in_=head_rows[:], compare_op=ALU.is_ge, fill=0.0, base=HD - 1,
                               pattern=[[HD, NH]], channel_multiplier=-1).then_inc(made, 1)
            clear_queries(pool, 0, 0, made)
            clear_queries(pool, 0, 1, made)
            clear_values(pool, 0, made, 6)

            def q_parts(g, b):
                pool.wait_ge(q_out, g + 1)
                grouped = qf[:].rearrange("p (t a q) -> p t a q", a=2, q=B)
                for i in (0, 1):
                    for r in range(NH // 4):
                        rs = slice(r * ROWS, (r + 1) * ROWS)
                        hi, out = (qz[b][k][rs, r].rearrange("p t (a q) -> p t a q", a=3)[:, :, 0:3:2, :]
                                   for k in (0, i))
                        if i == 0:
                            none = zero[rs].rearrange("p (a b c) -> p a b c", a=1, b=1).broadcast_to([ROWS, TT, 2, B])
                            ins = pool.tensor_tensor(out, grouped[rs], none, ALU.add)
                        else:
                            ins = pool.tensor_tensor(out, grouped[rs], hi.bitcast(F32), ALU.subtract)
                    ins.then_inc(q_split if i else q_hi, 1)
                    if i == 0:
                        pool.wait_ge(q_hi, g + 1)
            pool.wait_ge(made, CLEARED)
            q_parts(0, 0)

            def body(g, b):
                if is0(g):
                    pool.wait_ge(made_1, 5)
                if exists(g + 1):
                    q_parts(g + 1, 1 - b)
                if isinstance(g, int) and g == 1:
                    pool.wait_ge(s.moments_done, s.tiles)
                    pool.wait_ge(q_split, g + 2)
                    norm_factors(pool, s, factors, slice(EARLY, None), 4)
            bodies(pool, body)

        @block.scalar
        def _(act):
            def c_round(g, b):
                act.wait_ge(c_in[b], (g - b) * 16 + 32)
                if not is0(g):
                    act.wait_ge(k_prod, g)
                act.activation(by_batch(cp[0]), cT[b][:, :, 0, :], ACT.Copy).then_inc(c_hi, 1)

            def q_evacuate(g):
                act.wait_ge(q_prod, g + 1)
                act.activation(qf[:], misc[:], ACT.Identity, bias=qbs[:, 0:1], scale=SCALE).then_inc(q_out, 1)

            def k_evacuate(g):
                act.wait_ge(k_prod, g + 1)
                act.activation(kf[:], misc[:], ACT.Identity, bias=kb[:, 0:1]).then_inc(k_out, 1)

            def mask_keys(g, b, i):
                act.wait_ge(k_split, g + 1)
                for j in range(4):
                    ins = act.activation(kz[b][i][:, j, :], kp[i][:], ACT.Copy, scale=mask[:, j:j + 1])
                ins.then_inc(k_masked, 1)

            def o_evacuate(g):
                act.wait_ge(o_turned, g + 1)
                act.activation(oT[:], misc[:], ACT.Copy).then_inc(o_out, 1)

            def eT_half(m):
                act.wait_ge(e_turned, 2 * m + 1)
                act.activation(eT[:, 0:HP // 2, :], turned_e[:, 0:HP // 2, :], ACT.Copy).then_inc(eT_act, 1)

            def exp(n, u):
                act.wait_ge(shifted, n + 1)
                act.activation(e[u][:], e[u][:], ACT.Exp).then_inc(exped, 1)

            c_round(0, 0)
            act.wait_ge(vec_in, 16 * 5)
            act.activation(qbs[:], qb[:], ACT.Copy, scale=SCALE).then_inc(w_split, 1)
            act.wait_ge(w_split, 3)
            q_evacuate(0)
            k_evacuate(0)
            act.wait_ge(mask_made, 1)
            mask_keys(0, 0, 0)
            mask_keys(0, 0, 1)

            def body(g, b):
                here, after = exists(g), exists(g + 1)
                for p in range(TT):
                    n = g * TT + p
                    if p == 0 and after:
                        c_round(g + 1, 1 - b)
                    if (not is0(g) or p >= 2) and (here or p < 2):
                        eT_half(n - 2)
                    if p == 1 and after:
                        q_evacuate(g + 1)
                        k_evacuate(g + 1)
                    if p == 2 and after:
                        mask_keys(g + 1, 1 - b, 0)
                    if p == 2 and not is0(g):
                        o_evacuate(g - 1)
                    if here:
                        exp(n, p % 2)
                    if p == 2 and after:
                        mask_keys(g + 1, 1 - b, 1)
            bodies(act, body)

        @block.vector
        def _(dve):
            clear_queries(dve, 1, 0, made_1)
            dve.wait_ge(w_in, 32)
            split(dve, wq[0][:], wq[1][:], raw_q[:], w_hi, 1, w_split)
            split(dve, wk[0][:], wk[1][:], raw_kv[:, 0:D], w_hi, 2, w_split)
            dve.wait_ge(made, 4)
            dve.tensor_reduce(mask[:], head_rows[:].rearrange("p (q j) -> p j q", j=4), AX.X,
                              ALU.add).then_inc(mask_made, 1)

            def x_parts(g):
                dve.wait_ge(turned, g + 1)
                split(dve, xT[0][:], xT[1][:], misc[:], x_hi, g + 1, x_split)

            def c_low(g, b):
                dve.wait_ge(c_hi, g + 1)
                dve.tensor_tensor(by_batch(cp[1]), cT[b][:, :, 0, :], by_batch(cp[0]).bitcast(F32),
                                  ALU.subtract).then_inc(c_split, 1)

            def k_parts(g):
                dve.wait_ge(k_out, g + 1)
                if not is0(g):
                    dve.wait_ge(k_masked, 2 * g)
                dve.tensor_copy(kp[0][:].bitcast(F32R), kf[:]).then_inc(k_hi, 1)
                dve.wait_ge(k_hi, g + 1)
                dve.tensor_tensor(kp[1][:], kf[:], kp[0][:], ALU.subtract).then_inc(k_split, 1)

            def v_half(g, b, i):
                dve.wait_ge(v_prod, 2 * g + i + 1)
                ts = slice(i * TT // 2, (i + 1) * TT // 2)
                into = vz[b][:, ts].rearrange("p t h a c -> p t a h c")
                v = misc[:].rearrange("p (t a h o d) -> p t a h o d", t=TT // 2, a=2, o=2, d=HD)
                bias = vb[:].rearrange("p (a h o d) -> p a h o d", a=1, o=2, d=HD).broadcast_to([P, 2, HP, 2, HD])
                for odd in (0, 1):
                    rs = slice(odd * B, odd * B + B)
                    for t in range(TT // 2):
                        ins = dve.tensor_tensor(into[rs, t, :, :, odd * V1:odd * V1 + HD], v[rs, t, :, :, odd, :],
                                                bias[rs, :, :, odd, :], ALU.add)
                ins.then_inc(v_out, 1)

            def softmax(g, n, u):
                dve.wait_ge(scored, n + 1)
                dve.tensor_reduce(top[:, u], scores[u][:], AX.X, ALU.max).then_inc(top_done, 1)
                dve.wait_ge(top_done, n + 1)
                if not (isinstance(n, int) and n < 2):
                    dve.wait_ge(e_turned, 2 * n - 2)
                peak = top[:, u].rearrange("p (h a) -> p h a", a=1).broadcast_to([P, NH, B])
                dve.tensor_tensor(e[u][:], scores[u][:], peak, ALU.subtract).then_inc(shifted, 1)

            def eT_half(m):
                dve.wait_ge(e_turned, 2 * m + 2)
                dve.tensor_copy(eT[:, HP // 2:, :], turned_e[:, HP // 2:, :]).then_inc(eT_dve, 1)

            def o_normalise(m, t, g):
                dve.wait_ge(attended, m + 1)
                halves = [(slice(a * B, a * B + B), att[a * B:a * B + B, :, a]) for a in (0, 1)]
                for rs, got in halves:
                    ins = dve.reciprocal(inv[rs, t % 2], got[:, :, :, HD])
                ins.then_inc(inv_done, 1)
                dve.wait_ge(inv_done, m + 1)
                if t == 0 and not is0(g):
                    dve.wait_ge(o_turned, g)
                for rs, got in halves:
                    sums = inv[rs, t % 2].rearrange("p h (o a) -> p h o a", a=1).broadcast_to([B, HP, 2, HD])
                    ins = dve.tensor_tensor(o[rs, t, :].rearrange("p (h o d) -> p h o d", h=HP, o=2),
                                            got[:, :, :, 0:HD], sums, ALU.mult)
                ins.then_inc(normal, 1)

            def take_update(g):
                dve.wait_ge(proj_done, g + 1)
                bias = ob[:].rearrange("p (a d) -> p a d", a=1).broadcast_to([P, TT, D])
                update.take(dve, misc[:].rearrange("p (t d) -> p t d", d=D), bias, g + 1)

            def make_x(g):
                if not is0(g):
                    dve.wait_ge(turned, g)
                normalise(dve, s, xn, g * TT, TT, normed)

            c_low(0, 0)
            dve.wait_ge(factors, 4)
            make_x(0)
            x_parts(0)
            make_x(1)
            k_parts(0)
            dve.wait_ge(vec_in, 16 * 5)
            dve.wait_ge(made, CLEARED)
            v_half(0, 0, 0)
            v_half(0, 0, 1)
            clear_queries(dve, 1, 1, made_1)
            clear_values(dve, 1, made_1, 2)
            dve.wait_ge(made_1, 5)

            def body(g, b):
                here, after = exists(g), exists(g + 1)
                for p in range(TT):
                    n = g * TT + p
                    m = n - 2
                    behind = (not is0(g) or p >= 2) and (here or p < 2)
                    if p == 2 and after:
                        k_parts(g + 1)
                    if behind:
                        eT_half(m)
                    if p >= 2 and after:
                        v_half(g + 1, 1 - b, p - 2)
                    if here:
                        softmax(g, n, p % 2)
                    if p == 3 and exists(g + 2):
                        if not (isinstance(g, int) and g < 2):
                            dve.wait_ge(factors, 8)
                        make_x(g + 2)
                    if isinstance(g, int) and g < 2:
                        if p == 0:
                            dve.wait_ge(s.x_in[2 + g], 16)
                        share = (s.tiles - EARLY) // (2 * TT)
                        first = EARLY + n * share
                        find_moments(dve, s, first, first + share)
                    if p == 0 and after:
                        x_parts(g + 1)
                        c_low(g + 1, 1 - b)
                    if behind:
                        o_normalise(m, (p + 2) % TT, g)
                    if p == 2 and exists(g - 2):
                        update.finish(dve, (g - 2) * TT, g - 1)
                    if p == 3 and exists(g - 1):
                        take_update(g - 1)
            bodies(dve, body)
            update.finish(dve, (STEPS - 1) * TT, STEPS)
            dve.wait_ge(update.done, STEPS)

        @block.tensor
        def _(pe):
            def turn_x(g):
                pe.wait_ge(normed, (g + 1) * TT)
                for t in range(TT):
                    ins = pe.transpose(misc[:, t * P:(t + 1) * P], xn[:, t, :], s.ident[:])
                ins.then_inc(turned, 1)

            def make_q(g):
                pe.wait_ge(x_split, g + 1)
                for i, (a, c) in enumerate(PARTS):
                    ins = pe.matmul(misc[:], wq[a][:], xT[c][:], start=(i == 0), stop=(i == 2))
                ins.then_inc(q_prod, 1)

            def make_k(g):
                pe.wait_ge(c_split, g + 1)
                pe.wait_ge(q_out, g + 1)
                for i, (a, c) in enumerate(PARTS):
                    ins = pe.matmul(misc[:], wk[a][:], cp[c][:], start=(i == 0), stop=(i == 2))
                ins.then_inc(k_prod, 1)

            def make_v(g, b, i):
                if i == 0:
                    pe.wait_ge(k_out, g + 1)
                else:
                    pe.wait_ge(v_out, 2 * g + 1)
                for j in range(NB // 2):
                    twice = cT[b][:, i * NB // 2 + j].rearrange("c a k -> c (a k)")
                    ins = pe.matmul(misc[:, j * D:(j + 1) * D], twice, raw_kv[:, D:2 * D], start=True, stop=True)
                ins.then_inc(v_prod, 1)

            def score(g, b, p, n):
                if not (isinstance(n, int) and n < 2):
                    pe.wait_ge(shifted, n - 1)
                out = scores[p % 2][:].rearrange("q h k -> q (h k)")
                for r in range(NH // 4):
                    for half in (0, 1):
                        for i, (a, c) in enumerate(PARTS):
                            batch = 2 * p + half
                            ins = pe.matmul(out[:, r * 4 * B:(r + 1) * 4 * B],
                                            qz[b][c][:, r, p, half * B:half * B + P],
                                            kz[b][a][:, :, batch * B:(batch + 1) * B],
                                            start=(half == 0 and i == 0), stop=(half == 1 and i == 2))
                ins.then_inc(scored, 1)

            def turn_e(m, u):
                pe.wait_ge(exped, m + 1)
                for t in range(HP):
                    ins = pe.transpose(turned_e[:, t, :], e[u][:, 2 * t:2 * t + 2, :].rearrange("q h k -> q (h k)"),
                                       s.ident[:])
                    if t % (HP // 2) == HP // 2 - 1:
                        ins.then_inc(e_turned, 1)

            def attend(m, b, p):
                pe.wait_ge(eT_act, m + 1)
                if not (isinstance(m, int) and m == 0):
                    pe.wait_ge(normal, m)
                for t in range(HP):
                    if t == HP // 2:
                        pe.wait_ge(eT_dve, m + 1)
                    ins = pe.matmul(att[:, t].rearrange("q a h d -> q (a h d)"), eT[:, t, :],
                                    vz[b][:, p, t].rearrange("k a c -> k (a c)"), start=True, stop=True)
                ins.then_inc(attended, 1)

            def turn_o(g):
                pe.wait_ge(normal, (g + 1) * TT)
                for t in range(TT):
                    ins = pe.transpose(misc[:, t * P:(t + 1) * P], o[:, t, :], s.ident[:])
                ins.then_inc(o_turned, 1)

            def project(g):
                pe.wait_ge(o_out, g + 1)
                for t in range(TT):
                    ins = pe.matmul(misc[:, t * D:(t + 1) * D], oT[:, t * P:(t + 1) * P], wo[:], start=True,
                                    stop=True)
                ins.then_inc(proj_done, 1)

            turn_x(0)
            pe.wait_ge(w_split, 3)
            make_q(0)
            make_k(0)
            pe.wait_ge(vec_in, 16 * 5)
            pe.wait_ge(made, CLEARED)
            make_v(0, 0, 0)
            make_v(0, 0, 1)

            def body(g, b):
                here, after = exists(g), exists(g + 1)
                for p in range(TT):
                    n = g * TT + p
                    behind = (not is0(g) or p >= 2) and (here or p < 2)
                    mb = b if p >= 2 else 1 - b
                    if behind:
                        turn_e(n - 2, p % 2)
                    if p == 2 and after:
                        make_v(g + 1, 1 - b, 0)
                    if p == 3 and after:
                        if not is0(g):
                            pe.wait_ge(o_out, g)
                        make_v(g + 1, 1 - b, 1)
                    if here:
                        if p == 0:
                            pe.wait_ge(q_split, g + 1)
                            pe.wait_ge(k_masked, 2 * (g + 1))
                        score(g, b, p, n)
                    if p == 0 and after:
                        if is0(g):
                            pe.wait_ge(v_out, 2)
                        else:
                            pe.wait_ge(eT_dve, n - 1)
                        turn_x(g + 1)
                    if p == 1 and after:
                        make_q(g + 1)
                    if p == 2 and not is0(g):
                        if after:
                            pe.wait_ge(v_out, 2 * g + 3)
                        turn_o(g - 1)
                    if behind:
                        attend(n - 2, mb, (p + 2) % TT)
                    if p == 1 and after:
                        make_k(g + 1)
                    if p == 3 and not is0(g) :
                        if after:
                            pe.wait_ge(v_out, 2 * (g + 2))
                        project(g - 1)
            bodies(pe, body)


def ffn_gated(nc, s, w):
    H = w["w1"].shape[1]
    HC = H // P
    RING = 4
    WIDE = 4 * HC
    STEPS = s.tiles // TT
    with ExitStack() as ctx:
        def sb(n, shape, dt=F32):
            return ctx.enter_context(nc.sbuf_tensor("b_" + n, shape, dt))

        def ps(n, shape):
            return ctx.enter_context(nc.psum_tensor("b_" + n, shape, F32))

        def sem(n):
            return s.sem("b_" + n)

        raw12, raw_h1, raw_h2 = sb("raw12", [P, 2, H]), sb("raw_h1", [P, HC, H]), sb("raw_h2", [P, HC, H])
        w1, w2 = ([sb(f"{n}_{i}", [P, H], F32R) for i in "01"] for n in ("w1", "w2"))
        h1, h2 = ([sb(f"{n}_{i}", [P, HC, H], F32R) for i in "01"] for n in ("h1", "h2"))
        w3, s3 = sb("w3", [P, HC, D]), sb("s3", [P, D])
        s1, s2, sh1, sh2 = (sb(n, [P, HC]) for n in ("s1", "s2", "sh1", "sh2"))
        xn = sb("xn", [P, TT, D])
        xT = [sb(f"xT_{i}", [P, TOK], F32R) for i in "01"]
        full = sb("full", [P, 2, TOK])
        a1, a2 = ([sb(f"{n}_{i}", [P, HC, TOK], F32R) for i in "01"] for n in ("a1", "a2"))
        a3 = sb("a3", [P, HC, TOK])
        BF16 = mybir.dt.bfloat16
        flags, ones = sb("flags", [P, 2 + 2 * HC, H], BF16), sb("ones", [P, P], BF16)
        verdict = sb("verdict", [P, 1])
        update = Update(s, sb, "b_", TT)
        wide, turned, out = ps("wide", [P, RING, TOK]), ps("turned", [P, TOK]), ps("out", [P, TT, D])

        w_in = [sem(f"weights_in{i}") for i in range(3)]
        vec_in = sem("vectors_in")
        h_hi = sem("h_first_parts")
        split = sem("weights_split")
        factors, normed = sem("norm_factors"), sem("normed")
        turned_done = sem("turned_done")
        xT_done = sem("xT_done")
        prod = sem("products")
        act_out = sem("act_out")
        gated = sem("gated")
        even_hi = sem("even_chunks_hi")
        parts = [sem("even_parts"), sem("odd_parts")]
        out_done = sem("out_done")
        ones_made, flagged = sem("ones_made"), sem("weights_flagged")
        counted, judged = sem("flags_counted"), sem("judged")
        chain = sem("dve_chain")
        block = ctx.enter_context(nc.Block())

        def whole(eng, period):
            period(0, True, False)
            with eng.Fori(1, STEPS - 1) as g:
                period(g, False, False)
            period(STEPS - 1, False, True)

        def prod_h(g, layer, c):
            return 2 * HC + g * WIDE + layer * HC + c + 1

        def prod_w(g, i, c):
            return g * WIDE + 2 * c + i + 1

        def act_h(g, layer, c):
            return HC + 3 * HC * g + layer * HC + c + 1

        def act_w(g, c):
            return 3 * HC * g + c + 1

        def gates(g, c):
            return HC * g + c + 1

        def parts_a1(g, c):
            return HC * g + c // 2 + 1

        def parts_a2(g, c):
            return HC * g + HC // 2 + c // 2 + 1

        @block.sync
        def _(sp):
            sp.dma_start(raw12[:, 0, :], w["w1"]).then_inc(w_in[0], 16)
            sp.dma_start(raw12[:, 1, :], w["w2"]).then_inc(w_in[0], 16)
            for v, n in ((s1, "w1s"), (s2, "w2s"), (sh1, "h1s"), (sh2, "h2s")):
                sp.dma_start(v[:], w[n]).then_inc(vec_in, 16)
            sp.dma_start(s3[:], rows(w["w3s"], D)).then_inc(vec_in, 16)
            sp.dma_start(w3[:], w["w3"].rearrange("(k p) o -> p k o", p=P)).then_inc(vec_in, 16)
            sp.dma_start(raw_h1[:], w["h1"].rearrange("(k p) o -> p k o", p=P)).then_inc(w_in[1], 16)
            sp.dma_start(raw_h2[:], w["h2"].rearrange("(k p) o -> p k o", p=P)).then_inc(w_in[2], 16)

        @block.gpsimd
        def _(pool):
            norm_factors(pool, s, factors, FIRST, 0)
            norm_factors(pool, s, factors, LATER, 4)
            def second_parts(g, number, a):
                for c in range(0, HC, 2):
                    pool.wait_ge(even_hi, number(g, c))
                    pool.tensor_tensor(a[1][:, c, :], full[:, 0, :], a[0][:, c, :].bitcast(F32),
                                       ALU.subtract).then_inc(parts[0], 1)

            def flag(n, lo, out):
                pool.wait_ge(split, n)
                pool.tensor_scalar(out, lo.bitcast(F32), 0.0, 0.5, ALU.is_equal, ALU.is_lt).then_inc(flagged, 1)

            pool.memset(ones[:], 1.0).then_inc(ones_made, 1)
            flag(1, w1[1][:], flags[:, 0, :])
            flag(2, w2[1][:], flags[:, 1, :])
            second_parts(0, parts_a1, a1)
            flag(3, h1[1][:], flags[:, 2:2 + HC, :])

            def period(g, first, last):
                second_parts(g, parts_a2, a2)
                if first:
                    flag(4, h2[1][:], flags[:, 2 + HC:, :])
                if not last:
                    second_parts(g + 1, parts_a1, a1)
            whole(pool, period)

        @block.scalar
        def _(act):
            def first_part(i, raw, h):
                act.wait_ge(w_in[1 + i], 16)
                act.activation(h[0][:], raw[:], ACT.Copy).then_inc(h_hi, 1)
            first_part(0, raw_h1, h1)
            act.wait_ge(vec_in, 16 * 6)

            def gate(g):
                for c in range(HC):
                    act.wait_ge(prod, prod_w(g, 0, c))
                    if c >= 2 or not (isinstance(g, int) and g == 0):
                        act.wait_ge(parts[c % 2], parts_a1(g, c) - 1)
                    act.activation(full[:, c % 2, :], wide[:, 2 * c % RING, :], ACT.Silu,
                                   scale=s1[:, c:c + 1]).then_inc(act_out, 1)

            gate(0)
            first_part(1, raw_h2, h2)

            def period(g, first, last):
                for c in range(HC):
                    act.wait_ge(prod, prod_h(g, 0, c))
                    act.wait_ge(parts[c % 2], parts_a2(g, c) - 1)
                    act.activation(full[:, c % 2, :], wide[:, c % RING, :], ACT.Gelu,
                                   scale=sh1[:, c:c + 1]).then_inc(act_out, 1)
                for c in range(HC):
                    act.wait_ge(prod, prod_h(g, 1, c))
                    act.activation(a3[:, c, :], wide[:, (HC + c) % RING, :], ACT.Gelu,
                                   scale=sh2[:, c:c + 1]).then_inc(act_out, 1)
                if not last:
                    gate(g + 1)
            whole(act, period)

        @block.vector
        def _(dve):
            link = Chain(dve, chain)

            def make_x(g):
                normalise(dve, s, xn, g * TT, TT, normed)

            def split_x(g):
                dve.wait_ge(turned_done, g + 1)
                link.then(dve.tensor_copy(xT[0][:], turned[:]))
                dve.tensor_tensor(xT[1][:], turned[:], xT[0][:].bitcast(F32), ALU.subtract).then_inc(xT_done, 1)
            dve.wait_ge(factors, 4)
            make_x(0)
            dve.wait_ge(w_in[0], 32)
            link.then(dve.tensor_copy(w1[0][:], raw12[:, 0, :]))
            dve.tensor_tensor(w1[1][:], raw12[:, 0, :], w1[0][:].bitcast(F32), ALU.subtract).then_inc(split, 1)
            link.then(dve.tensor_copy(w2[0][:], raw12[:, 1, :]))
            dve.tensor_tensor(w2[1][:], raw12[:, 1, :], w2[0][:].bitcast(F32), ALU.subtract).then_inc(split, 1)
            split_x(0)

            def second_parts(i, raw, h):
                dve.wait_ge(h_hi, i + 1)
                dve.tensor_tensor(h[1][:], raw[:], h[0][:].bitcast(F32), ALU.subtract).then_inc(split, 1)
            second_parts(0, raw_h1, h1)
            def halve(a, c):
                hi = dve.tensor_copy(a[0][:, c, :], full[:, c % 2, :])
                if c % 2 == 0:
                    hi.then_inc(even_hi, 1)
                else:
                    link.then(hi)
                    dve.tensor_tensor(a[1][:, c, :], full[:, c % 2, :], a[0][:, c, :].bitcast(F32),
                                      ALU.subtract).then_inc(parts[1], 1)

            def gate(g):
                for c in range(HC):
                    dve.wait_ge(act_out, act_w(g, c))
                    dve.wait_ge(prod, prod_w(g, 1, c))
                    dve.scalar_tensor_tensor(out=full[:, c % 2, :], in0=wide[:, (2 * c + 1) % RING, :],
                                             scalar=s2[:, c:c + 1], in1=full[:, c % 2, :], op0=ALU.mult,
                                             op1=ALU.mult).then_inc(gated, 1)
                    dve.wait_ge(gated, gates(g, c))
                    halve(a1, c)
            gate(0)
            before = link.base
            LINKS = HC + 1

            def take_update(g):
                dve.wait_ge(out_done, g + 1)
                update.take(dve, out[:], s.x[:, at(g * TT, TT), :], g + 1)

            def period(g, first, last):
                link.start(before + g * LINKS)
                if not first:
                    take_update(g - 1)
                if not last:
                    dve.wait_ge(turned_done, g + 1)
                    dve.wait_ge(factors, 8)
                    make_x(g + 1)
                if first:
                    second_parts(1, raw_h2, h2)
                    dve.wait_ge(vec_in, 16 * 6)
                    for k in range(HC):
                        ins = dve.tensor_tensor(w3[:, k, :], w3[:, k, :], s3[:], ALU.mult)
                    ins.then_inc(split, 1)
                for c in range(HC):
                    dve.wait_ge(act_out, act_h(g, 0, c))
                    halve(a2, c)
                if not last:
                    split_x(g + 1)
                if first:
                    dve.wait_ge(counted, 1)
                    dve.tensor_reduce(verdict[:], out[:].rearrange("p t d -> p (t d)"), AX.X,
                                      ALU.add).then_inc(judged, 1)
                if not first:
                    update.finish(dve, (g - 1) * TT, g, False)
                if not last:
                    gate(g + 1)
            whole(dve, period)
            take_update(STEPS - 1)
            update.finish(dve, (STEPS - 1) * TT, STEPS, False)
            dve.wait_ge(update.done, STEPS)

        @block.tensor
        def _(pe):
            def turn(g):
                pe.wait_ge(normed, (g + 1) * TT)
                for t in range(TT):
                    ins = pe.transpose(turned[:, t * P:(t + 1) * P], xn[:, t, :], s.ident[:])
                ins.then_inc(turned_done, 1)

            def product(n, weights, acts, passes, ready=None):
                K = len(acts)
                for k in range(K):
                    if ready:
                        pe.wait_ge(parts[k % 2], ready(k))
                    for i, (a, b) in enumerate(passes):
                        ins = pe.matmul(wide[:, n % RING, :], weights[k][a], acts[k][b],
                                        start=(k == 0 and i == 0), stop=(k == K - 1 and i == len(passes) - 1))
                ins.then_inc(prod, 1)

            def gates_of(g, c, passes):
                if c == 0:
                    pe.wait_ge(xT_done, g + 1)
                for i, v in enumerate((w1, w2)):
                    if c >= 2 and i == 0:
                        pe.wait_ge(act_out, act_w(g, c - 2))
                    elif c >= 2:
                        pe.wait_ge(gated, gates(g, c - 2))
                    elif not (isinstance(g, int) and g == 0):
                        pe.wait_ge(act_out, act_h(g - 1, 1, 2 * c + i))
                    product(2 * HC + 2 * c + i, [[v[j][:, c * P:(c + 1) * P] for j in (0, 1)]],
                            [[xT[j][:] for j in (0, 1)]], passes)

            def hidden(g, layer, h, a, passes):
                for c in range(HC):
                    if layer:
                        pe.wait_ge(act_out, act_h(g, 0, c))
                    elif c % 2:
                        pe.wait_ge(gated, gates(g, 2 + c // 2))
                    else:
                        pe.wait_ge(act_out, act_w(g, 2 + c // 2))
                    product(layer * HC + c, [[h[j][:, k, c * P:(c + 1) * P] for j in (0, 1)] for k in range(HC)],
                            [[a[j][:, k, :] for j in (0, 1)] for k in range(HC)], passes,
                            None if c else lambda k: (parts_a2 if layer else parts_a1)(g, k))

            def outward(g, t):
                if t == 0:
                    pe.wait_ge(act_out, act_h(g, 1, HC - 1))
                for k in range(HC):
                    ins = pe.matmul(out[:, t, :], a3[:, k, t * P:(t + 1) * P], w3[:, k, :],
                                    start=(k == 0), stop=(k == HC - 1))
                if t == TT - 1:
                    ins.then_inc(out_done, 1)

            def period(g, first, last, passes):
                if first:
                    pe.wait_ge(split, 3)
                hidden(g, 0, h1, a1, passes)
                if not last:
                    turn(g + 1)
                if first:
                    pe.wait_ge(split, 4)
                hidden(g, 1, h2, a2, passes)
                if first:
                    pe.wait_ge(ones_made, 1)
                    pe.wait_ge(flagged, 4)
                    for k in range(2 + 2 * HC):
                        ins = pe.matmul(out[:].rearrange("p t d -> p (t d)"), ones[:], flags[:, k, :],
                                        start=(k == 0), stop=(k == 1 + 2 * HC))
                    ins.then_inc(counted, 1)
                if not last:
                    gates_of(g + 1, 0, passes)
                    gates_of(g + 1, 1, passes)
                if first:
                    pe.wait_ge(split, 5)
                    pe.wait_ge(judged, 1)
                else:
                    pe.wait_ge(update.read, g)
                for t in range(TT):
                    outward(g, t)
                    if t < 2 and not last:
                        gates_of(g + 1, 2 + t, passes)

            def rest(passes):
                with pe.Fori(1, STEPS - 1) as g:
                    period(g, False, False, passes)
                period(STEPS - 1, False, True, passes)

            turn(0)
            pe.wait_ge(split, 2)
            for c in range(HC):
                gates_of(0, c, PARTS)
            period(0, True, False, PARTS)
            pe.wait_ge(judged, 1)
            second_parts = pe.value_load(verdict[0:1, :].bitcast(mybir.dt.int32))
            with pe.If(second_parts == 0):
                rest(tuple(p for p in PARTS if p[0] == 0))
            with pe.Else():
                rest(PARTS)


def xattn_large(nc, s, cT_dram, w):
    NH, B = 16, 64
    HD = w["q"].shape[1] // NH
    HP = NH // 2
    CD = cT_dram.shape[0]
    SCALE = float(HD) ** -0.5
    TS = 2
    WIDE = TS * P
    NB = WIDE // B
    UH, UP = NH // 2, HP // 2
    STEPS = s.tiles // TS
    with ExitStack() as ctx:
        def sb(n, shape, dt=F32):
            return ctx.enter_context(nc.sbuf_tensor("c_" + n, shape, dt))

        def ps(n, shape):
            return ctx.enter_context(nc.psum_tensor("c_" + n, shape, F32))

        def sem(n):
            return s.sem("c_" + n)

        raw = {n: sb("raw_" + n, [r, HP, P]) for n, r in (("q", D), ("k", CD), ("v", CD))}
        parts = {n: [sb(f"w{n}_{i}", [r, HP, P], F32R) for i in "01"] for n, r in (("q", D), ("k", CD), ("v", CD))}
        wo, ob = sb("wo", [P, HP, D]), sb("ob", [P, D])
        xn = sb("xn", [P, TS, D])
        xT = [sb(f"xT_{i}", [P, WIDE], F32R) for i in "01"]
        cT = [sb(f"cT{b}", [CD, TS, 3 * B]) for b in "01"]
        cp = [sb(f"c_{i}", [CD, TS, 3 * B], F32R) for i in "01"]
        q = [sb(f"q{b}", [P, HP, WIDE]) for b in "01"]
        kz = [sb(f"kz{b}", [P, HP, NB, 2 * B]) for b in "01"]
        vz = [[sb(f"vz{b}_{t}", [P, 2, HP, 2 * HD]) for t in "01"] for b in "01"]
        top, total, inv = (sb(n, [P, 2, UH]) for n in ("top", "total", "inv"))
        e = [sb(f"e{u}", [P, UH, B]) for u in "01"]
        eT = sb("eT", [P, UP, P])
        oT = [sb(f"oT{t}", [P, HP, P]) for t in "01"]
        update = Update(s, sb, "c_", 1)
        scores = [ps(f"scores{u}", [P, UH, B]) for u in "01"]
        turned_e, att = ps("turned_e", [P, UP, P]), ps("att", [P, UP, P])
        misc = ps("misc", [P, 4, TOK])
        PROJ0, XT, Q0, K0, PROJ1, K1, V0 = 0, 1, 2, 6, 7, 8, 11

        def bank(job):
            return misc[:, job % 4, :]

        def k_bank(i):
            return bank(K0 if i == 0 else K1 + i - 1)

        w_in, vec_in = [sem(f"weights_in{i}") for i in range(3)], sem("vectors_in")
        c_in = [sem("ctx_in0"), sem("ctx_in1")]
        w_hi, w_split, made = sem("weights_hi"), sem("weights_split"), sem("zeros_made")
        factors, normed = sem("norm_factors"), sem("normed")
        turned, x_hi, x_split = sem("xn_turned"), sem("x_hi"), sem("x_split")
        c_hi, c_split = sem("c_hi"), sem("c_split")
        q_prod, q_out = sem("q_product"), sem("q_out")
        k_prod, k_act, k_dve = sem("k_product"), sem("k_out_act"), sem("k_out_dve")
        v_prod, v_act, v_dve = sem("v_product"), sem("v_out_act"), sem("v_out_dve")
        proj_done = sem("projected")
        scored, top_done, shifted, exped, summed, inv_done, softmaxed = (sem(n) for n in (
            "scored", "top_done", "shifted", "exped", "summed", "inv_done", "softmaxed"))
        e_turned, eT_out, attended, oT_out = (sem(n) for n in ("e_turned", "eT_out", "attended", "oT_out"))
        block = ctx.enter_context(nc.Block())

        def bodies(eng, body):
            body(0, 0, True, True)
            with eng.Fori(0, STEPS // 2 - 1) as i:
                body(2 * i + 1, 1, True, True)
                body(2 * i + 2, 0, True, True)
            body(STEPS - 1, 1, True, False)
            body(STEPS, 0, False, False)

        def is0(g):
            return isinstance(g, int) and g == 0

        @block.sync
        def _(sp):
            def fetch(g, b):
                src = cT_dram[:, at(g * WIDE, WIDE)].rearrange("c (t k) -> c t k", k=P)
                sp.dma_start(cT[b][:, :, 0:P], src).then_inc(c_in[b], 16)
                sp.dma_start(cT[b][:, :, P:P + B], src[:, :, 0:B]).then_inc(c_in[b], 16)
            for i, n in enumerate(("q", "k", "v")):
                sp.dma_start(raw[n][:], w[n].rearrange("c (t d) -> c t d", d=P)).then_inc(w_in[i], 16)
                if i == 0:
                    fetch(0, 0)
            sp.dma_start(wo[:], w["o"].rearrange("(k p) o -> p k o", p=P)).then_inc(vec_in, 16)
            sp.dma_start(ob[:], rows(w["ob"], D)).then_inc(vec_in, 16)

            def body(g, b, here, after):
                if after:
                    if not is0(g):
                        sp.wait_ge(c_split, g)
                    fetch(g + 1, 1 - b)
            bodies(sp, body)

        @block.gpsimd
        def _(pool):
            norm_factors(pool, s, factors, FIRST, 0)
            for b in (0, 1):
                pool.memset(kz[b][:], 0.0).then_inc(made, 1)
                for t in (0, 1):
                    pool.memset(vz[b][t][:], 0.0).then_inc(made, 1)
                if b == 0:
                    norm_factors(pool, s, factors, LATER, 4)

            def softmax_scale(n, u):
                pool.wait_ge(inv_done, n + 1)
                by = inv[:, u].rearrange("p (h a) -> p h a", a=1).broadcast_to([P, UH, B])
                pool.tensor_tensor(e[u][:], e[u][:], by, ALU.mult).then_inc(softmaxed, 1)

            def body(g, b, here, after):
                for p in range(4):
                    if (here or p == 0) and not (is0(g) and p == 0):
                        softmax_scale(4 * g + p - 1, (p + 1) % 2)
            bodies(pool, body)

        @block.scalar
        def _(act):
            def c_round(g, b):
                act.wait_ge(c_in[b], (g - b) * 16 + 32)
                if not is0(g):
                    act.wait_ge(v_prod, 4 * g)
                act.activation(cp[0][:], cT[b][:], ACT.Copy).then_inc(c_hi, 1)

            def q_evacuate(g, b, i):
                act.wait_ge(q_prod, 4 * g + i + 1)
                act.activation(q[b][:, 2 * i:2 * i + 2, :], bank(Q0 + i).rearrange("p (t k) -> p t k", t=2),
                               ACT.Copy, scale=SCALE).then_inc(q_out, 1)

            def k_evacuate(g, b, i):
                if isinstance(g, int) and g == 1 and i == 0:
                    act.wait_ge(made, 6)
                act.wait_ge(k_prod, 4 * g + i + 1)
                src = k_bank(i).rearrange("p (t b o k) -> p t b o k", t=2, o=2, k=B)
                for o in (0, 1):
                    dst = kz[b][0:HD, 2 * i:2 * i + 2, o::2, o * B:(o + 1) * B]
                    ins = act.activation(dst, src[0:HD, :, :, o, :], ACT.Copy)
                ins.then_inc(k_act, 1)

            def v_evacuate(g, b, i):
                act.wait_ge(v_prod, 4 * g + i + 1)
                odd = i % 2
                act.activation(vz[b][i // 2][0:B, odd, :, odd * HD:(odd + 1) * HD],
                               bank(V0 + i)[0:B, :].rearrange("p (t d) -> p t d", d=HD), ACT.Copy).then_inc(v_act, 1)

            def eT_evacuate(m):
                act.wait_ge(e_turned, m + 1)
                act.activation(eT[:], turned_e[:], ACT.Copy).then_inc(eT_out, 1)

            def oT_evacuate(m, u):
                act.wait_ge(attended, m + 1)
                half = u % 2
                act.activation(oT[u // 2][:, half * UP:(half + 1) * UP, :], att[:], ACT.Copy).then_inc(oT_out, 1)

            def exp(n, u):
                act.wait_ge(shifted, n + 1)
                act.activation(e[u][:], e[u][:], ACT.Exp).then_inc(exped, 1)

            c_round(0, 0)
            for i in range(4):
                q_evacuate(0, 0, i)
            act.wait_ge(made, 3)
            for i in range(4):
                k_evacuate(0, 0, i)
            for i in range(4):
                v_evacuate(0, 0, i)

            def body(g, b, here, after):
                for p in range(4):
                    n = 4 * g + p
                    behind = (not is0(g) or p >= 2) and (here or p < 2)
                    if p == 0 and after:
                        c_round(g + 1, 1 - b)
                    if behind:
                        eT_evacuate(n - 2)
                    if after:
                        for kind, i in SLOTS[p]["a"] + SLOTS[p]["b"]:
                            {"q": q_evacuate, "k": k_evacuate, "v": v_evacuate}.get(kind, lambda *_: None)(
                                g + 1, 1 - b, i)
                    if here:
                        exp(n, p % 2)
                    if behind:
                        oT_evacuate(n - 2, (p + 2) % 4)
                    if after:
                        for kind, i in SLOTS[p]["c"]:
                            {"q": q_evacuate, "k": k_evacuate, "v": v_evacuate}[kind](g + 1, 1 - b, i)
            bodies(act, body)

        @block.vector
        def _(dve):
            def split_weights(n, name):
                dve.wait_ge(w_in[n], 16)
                split(dve, parts[name][0][:], parts[name][1][:], raw[name][:], w_hi, n + 1, w_split)

            def x_parts(g, b, i):
                dve.wait_ge(turned, g + 1)
                split(dve, xT[0][:], xT[1][:], bank(XT)[:, 0:WIDE], x_hi, g + 1, x_split)

            def c_low(g, b):
                dve.wait_ge(c_hi, g + 1)
                dve.tensor_tensor(cp[1][:], cT[b][:], cp[0][:].bitcast(F32), ALU.subtract).then_inc(c_split, 1)

            def k_evacuate(g, b, i):
                if isinstance(g, int) and g == 1 and i == 0:
                    dve.wait_ge(made, 6)
                dve.wait_ge(k_prod, 4 * g + i + 1)
                src = k_bank(i).rearrange("p (t b o k) -> p t b o k", t=2, o=2, k=B)
                for o in (0, 1):
                    dst = kz[b][HD:P, 2 * i:2 * i + 2, o::2, (1 - o) * B:(2 - o) * B]
                    ins = dve.tensor_copy(dst, src[HD:P, :, :, o, :])
                ins.then_inc(k_dve, 1)

            def v_evacuate(g, b, i):
                dve.wait_ge(v_prod, 4 * g + i + 1)
                odd = i % 2
                dve.tensor_copy(vz[b][i // 2][B:P, 1 - odd, :, odd * HD:(odd + 1) * HD],
                                bank(V0 + i)[B:P, :].rearrange("p (t d) -> p t d", d=HD)).then_inc(v_dve, 1)

            def softmax_shift(n, u):
                dve.wait_ge(scored, n + 1)
                dve.tensor_reduce(top[:, u], scores[u][:], AX.X, ALU.max).then_inc(top_done, 1)
                dve.wait_ge(top_done, n + 1)
                if not (isinstance(n, int) and n < 2):
                    dve.wait_ge(e_turned, n - 1)
                peak = top[:, u].rearrange("p (h a) -> p h a", a=1).broadcast_to([P, UH, B])
                dve.tensor_tensor(e[u][:], scores[u][:], peak, ALU.subtract).then_inc(shifted, 1)

            def softmax_sum(n, u):
                dve.wait_ge(exped, n + 1)
                dve.tensor_reduce(total[:, u], e[u][:], AX.X, ALU.add).then_inc(summed, 1)
                dve.wait_ge(summed, n + 1)
                dve.reciprocal(inv[:, u], total[:, u]).then_inc(inv_done, 1)

            def x_update(g, t):
                n = 2 * g + t + 1
                dve.wait_ge(proj_done, n)
                got = bank(PROJ1 if t else PROJ0)[:, 0:D].rearrange("p (a d) -> p a d", a=1)
                update.run(dve, got, ob[:].rearrange("p (a d) -> p a d", a=1), g * TS + t, n)

            dve.wait_ge(factors, 4)
            normalise(dve, s, xn, 0, TS, normed)
            split_weights(0, "q")
            x_parts(0, 0, 0)
            c_low(0, 0)
            split_weights(1, "k")
            split_weights(2, "v")
            dve.wait_ge(made, 3)
            for i in range(4):
                k_evacuate(0, 0, i)
            for i in range(4):
                v_evacuate(0, 0, i)
            dve.wait_ge(vec_in, 32)

            def jobs(g, b, slot, after):
                for kind, i in slot:
                    if kind == "proj":
                        if not is0(g):
                            x_update(g - 1, i)
                    elif after and kind in "kvx":
                        {"k": k_evacuate, "v": v_evacuate, "x": x_parts}[kind](g + 1, 1 - b, i)

            def body(g, b, here, after):
                for p in range(4):
                    n = 4 * g + p
                    if p == 0 and after:
                        if not is0(g):
                            dve.wait_ge(factors, 8)
                        dve.wait_ge(turned, g + 1)
                        normalise(dve, s, xn, (g + 1) * TS, TS, normed)
                    if (here or p == 0) and not (is0(g) and p == 0):
                        softmax_sum(n - 1, (p + 1) % 2)
                    jobs(g, b, SLOTS[p]["a"], after)
                    if here:
                        softmax_shift(n, p % 2)
                    if p == 1 and after:
                        c_low(g + 1, 1 - b)
                    jobs(g, b, SLOTS[p]["b"] + SLOTS[p]["c"], after)
            bodies(dve, body)
            dve.wait_ge(update.done, 2 * STEPS)

        @block.tensor
        def _(pe):
            def both(act_sem, dve_sem, count):
                pe.wait_ge(act_sem, count)
                pe.wait_ge(dve_sem, count)

            def turn_x(g, b, i, start=False):
                if not start:
                    both(v_act, v_dve, 4 * g - 1)
                pe.wait_ge(normed, (g + 1) * TS)
                for t in range(TS):
                    ins = pe.transpose(bank(XT)[:, t * P:(t + 1) * P], xn[:, t, :], s.ident[:])
                ins.then_inc(turned, 1)

            def make_q(g, b, i, start=False):
                if i == 3:
                    pe.wait_ge(x_split, g + 1)
                elif not start and i < 2:
                    both(v_act, v_dve, 4 * g)
                elif not start and is1(g):
                    both(v_act, v_dve, 4 * g)
                elif not start:
                    pe.wait_ge(update.read, 2 * g - 3)
                pe.wait_ge(x_split, g + 1)
                for j in range(2):
                    for k, (a, c) in enumerate(PARTS):
                        ins = pe.matmul(bank(Q0 + i)[:, j * WIDE:(j + 1) * WIDE], parts["q"][a][:, 2 * i + j, :],
                                        xT[c][:], start=(k == 0), stop=(k == 2))
                ins.then_inc(q_prod, 1)

            def make_k(g, b, i, start=False):
                if i < 3:
                    pe.wait_ge(q_out, 4 * g + (1, 3, 4)[i])
                else:
                    both(k_act, k_dve, 4 * g + 1)
                pe.wait_ge(c_split, g + 1)
                for j in range(2):
                    for k, (a, c) in enumerate(PARTS):
                        ins = pe.matmul(k_bank(i)[:, j * WIDE:(j + 1) * WIDE], parts["k"][a][:, 2 * i + j, :],
                                        cp[c][:, :, 0:P], start=(k == 0), stop=(k == 2))
                ins.then_inc(k_prod, 1)

            def make_v(g, b, i, start=False):
                if i > 0:
                    both(k_act, k_dve, 4 * g + i + 1)
                elif start or is1(g):
                    pe.wait_ge(q_out, 4 * g + 2)
                else:
                    pe.wait_ge(update.read, 2 * g - 2)
                t, odd = i // 2, i % 2
                for k, (a, c) in enumerate(PARTS):
                    ins = pe.matmul(bank(V0 + i), cp[c][:, t, odd * B:odd * B + P],
                                    parts["v"][a][:, :, odd * HD:(odd + 1) * HD], start=(k == 0), stop=(k == 2))
                ins.then_inc(v_prod, 1)

            def project(g, t):
                pe.wait_ge(oT_out, 4 * g + 2 * t + 2)
                for k in range(HP):
                    ins = pe.matmul(bank(PROJ1 if t else PROJ0)[:, 0:D], oT[t][:, k, :], wo[:, k, :],
                                    start=(k == 0), stop=(k == HP - 1))
                ins.then_inc(proj_done, 1)

            def is1(g):
                return isinstance(g, int) and g == 1

            def score(g, b, p, n):
                if not (isinstance(n, int) and n < 2):
                    pe.wait_ge(shifted, n - 1)
                t, hh = p // 2, p % 2
                for j in range(UP):
                    for half in (0, 1):
                        h = hh * UP + j
                        ins = pe.matmul(
                            scores[p % 2][half * B:(half + 1) * B, 2 * j:2 * j + 2, :].rearrange("q h k -> q (h k)"),
                            q[b][:, h, t * P + half * B:t * P + (half + 1) * B], kz[b][:, h, 2 * t + half, :],
                            start=True, stop=True)
                ins.then_inc(scored, 1)

            def turn_e(m, u):
                pe.wait_ge(softmaxed, m + 1)
                for j in range(UP):
                    ins = pe.transpose(turned_e[:, j, :], e[u][:, 2 * j:2 * j + 2, :].rearrange("q h k -> q (h k)"),
                                       s.ident[:])
                ins.then_inc(e_turned, 1)

            def attend(m, b, p):
                pe.wait_ge(eT_out, m + 1)
                if not (isinstance(m, int) and m == 0):
                    pe.wait_ge(oT_out, m)
                for j in range(UP):
                    for half in (0, 1):
                        ins = pe.matmul(att[:, j, half * B:(half + 1) * B],
                                        vz[b][p // 2][:, half, (p % 2) * UP + j, :],
                                        eT[:, j, half * B:(half + 1) * B], start=True, stop=True)
                ins.then_inc(attended, 1)

            make = {"x": turn_x, "q": make_q, "k": make_k, "v": make_v}
            turn_x(0, 0, 0, True)
            for n, kind in enumerate("qkv"):
                pe.wait_ge(w_split, n + 1)
                for i in range(4):
                    make[kind](0, 0, i, True)
            pe.wait_ge(vec_in, 32)

            def jobs(g, b, slot, here, after):
                for kind, i in slot:
                    if kind == "proj":
                        if not is0(g):
                            if i == 0 and here:
                                both(v_act, v_dve, 4 * g + 2)
                            elif i == 1 and after:
                                pe.wait_ge(q_out, 4 * (g + 1) + 2)
                            project(g - 1, i)
                    elif after:
                        make[kind](g + 1, 1 - b, i)

            def body(g, b, here, after):
                for p in range(4):
                    n = 4 * g + p
                    behind = (not is0(g) or p >= 2) and (here or p < 2)
                    mb = b if p >= 2 else 1 - b
                    if behind:
                        turn_e(n - 2, p % 2)
                    jobs(g, b, SLOTS[p]["a"], here, after)
                    if here:
                        if p == 0:
                            pe.wait_ge(q_out, 4 * g + 4)
                            both(k_act, k_dve, 4 * g + 4)
                        score(g, b, p, n)
                    jobs(g, b, SLOTS[p]["b"], here, after)
                    if behind:
                        if p == 2 and here:
                            both(v_act, v_dve, 4 * g + 4)
                        attend(n - 2, mb, (p + 2) % 4)
                    jobs(g, b, SLOTS[p]["c"], here, after)
            bodies(pe, body)


SLOTS = (
    {"a": (), "b": (("x", 0), ("proj", 0)), "c": (("q", 0),)},
    {"a": (("q", 1),), "b": (("q", 2),), "c": (("q", 3),)},
    {"a": (("k", 0),), "b": (("proj", 1), ("k", 1)), "c": (("k", 2),)},
    {"a": (("k", 3),), "b": (("v", 0), ("v", 1)), "c": (("v", 2), ("v", 3))},
)


def ffn_expert(nc, s, w, y_dram):
    H = w["w1"].shape[1]
    HC = H // P
    STEPS = s.tiles // TT
    with ExitStack() as ctx:
        def sb(n, shape, dt=F32):
            return ctx.enter_context(nc.sbuf_tensor("d_" + n, shape, dt))

        def ps(n, shape):
            return ctx.enter_context(nc.psum_tensor("d_" + n, shape, F32))

        def sem(n):
            return s.sem("d_" + n)

        raw1 = sb("raw1", [P, H])
        w1 = [sb(f"w1_{i}", [P, H], F32R) for i in "01"]
        w2, b1 = sb("w2", [P, HC, D]), sb("b1", [P, HC])
        b2, gamma, beta = sb("b2", [P, D]), sb("gamma", [P, D]), sb("beta", [P, D])
        power, eps, zero = sb("power", [P, TT]), sb("eps", [P, TT]), sb("zero", [P, TT])
        xn, xb = sb("xn", [P, 2, TT, D]), sb("xn_plus_b2", [P, 2, TT, D])
        xT = [sb(f"xT_{i}", [P, TOK], F32R) for i in "01"]
        a = sb("a", [P, HC, TOK])
        z = sb("z", [P, 2, TT, D])
        stats, moments = sb("stats", [P, TT, 6]), sb("step_moments", [P, 2, TT, 2])
        variance, product = sb("step_variance", [P, TT]), sb("step_product", [P, TT])
        rstd, shift = sb("step_rstd", [P, 2, TT]), sb("step_shift", [P, 2, TT])
        y = sb("y", [P, 2, TT, D])
        wide, turned, out = ps("wide", [P, HC, TOK]), ps("turned", [P, TOK]), ps("out", [P, 2, TT, D])
        yv = y_dram.rearrange("(t p) d -> p t d", p=P)

        w_in, vec_in, split = sem("weights_in"), sem("vectors_in"), sem("weights_split")
        factors, normed = sem("norm_factors"), sem("normed")
        turned_done, xT_hi, xT_done = sem("turned_done"), sem("xT_hi"), sem("xT_done")
        prod, act_out = sem("products"), sem("act_out")
        out_done = sem("out_done")
        xb_done = sem("xb_done")
        z_added, z_done = sem("z_added"), sem("z_done")
        shift_done, made = sem("shift_done"), sem("constants_made")
        pool_chain, chain = sem("pool_chain"), sem("dve_chain")
        scaled, times_gamma, plus_beta, y_done = (sem(n) for n in ("scaled", "times_gamma", "plus_beta", "y_done"))
        stored = [sem("stored0"), sem("stored1")]
        block = ctx.enter_context(nc.Block())

        def pairs(eng, step):
            for g in range(4):
                step(g, g % 2, g == 0, False)
            with eng.Fori(4, STEPS - 2, 2) as g:
                step(g, 0, False, False)
                step(g + 1, 1, False, False)
            step(STEPS - 2, 0, False, False)
            step(STEPS - 1, 1, False, True)

        @block.sync
        def _(sp):
            sp.dma_start(raw1[:], w["w1"]).then_inc(w_in, 16)
            sp.dma_start(w2[:], w["w2"].rearrange("(k p) o -> p k o", p=P)).then_inc(vec_in, 16)
            sp.dma_start(b1[:], w["b1"]).then_inc(vec_in, 16)
            for v, n in ((b2, "b2"), (gamma, "gamma"), (beta, "beta")):
                sp.dma_start(v[:], rows(w[n], D)).then_inc(vec_in, 16)

            def step(g, b, first, last):
                sp.wait_ge(y_done, g + 1)
                sp.dma_start(yv[:, at(g * TT, TT), :], y[:, b]).then_inc(stored[b], 16)
            pairs(sp, step)
            for b in (0, 1):
                sp.wait_ge(stored[b], 16 * (STEPS // 2))

        @block.gpsimd
        def _(pool):
            for tile, value in ((power, -0.5), (eps, EPS), (zero, 0.0)):
                pool.memset(tile[:], value).then_inc(made, 1)
            norm_factors(pool, s, factors, FIRST, 0)
            norm_factors(pool, s, factors, LATER, 4)
            pool.wait_ge(made, 3)
            link = Chain(pool, pool_chain)

            def bcast(v):
                return v[:].rearrange("p (a d) -> p a d", a=1).broadcast_to([P, TT, D])

            def add_b2(g, b):
                pool.wait_ge(normed, (g + 1) * TT)
                if not (isinstance(g, int) and g < 2):
                    pool.wait_ge(z_added, g - 1)
                pool.tensor_tensor(xb[:, b], xn[:, b], bcast(b2), ALU.add).then_inc(xb_done, 1)

            def affine(g, b):
                pool.wait_ge(scaled, g + 1)
                pool.tensor_tensor(y[:, b], y[:, b], bcast(gamma), ALU.mult).then_inc(times_gamma, 1)
                pool.wait_ge(times_gamma, g + 1)
                pool.tensor_tensor(y[:, b], y[:, b], bcast(beta), ALU.add).then_inc(plus_beta, 1)

            def step(g, b, first, last):
                if not last:
                    add_b2(g + 1, 1 - b)
                link.start(g * 3)
                pool.wait_ge(z_done, g + 1)
                if not (isinstance(g, int) and g < 2):
                    pool.wait_ge(scaled, g - 1)
                link.then(pool.tensor_tensor(variance[:], moments[:, b, :, 1], eps[:], ALU.add))
                link.then(pool.tensor_tensor(rstd[:, b], variance[:], power[:], ALU.pow))
                link.then(pool.tensor_tensor(product[:], moments[:, b, :, 0], rstd[:, b], ALU.mult))
                pool.tensor_tensor(shift[:, b], zero[:], product[:], ALU.subtract).then_inc(shift_done, 1)
                if not first:
                    affine(g - 1, 1 - b)
            pool.wait_ge(vec_in, 16 * 5)
            add_b2(0, 0)
            pairs(pool, step)
            affine(STEPS - 1, 1)

        @block.scalar
        def _(act):
            def first_part(g):
                act.wait_ge(turned_done, g + 1)
                act.activation(xT[0][:], turned[:], ACT.Copy).then_inc(xT_hi, 1)
            first_part(0)
            act.wait_ge(vec_in, 16 * 5)

            def step(g, b, first, last):
                for c in range(HC):
                    act.wait_ge(prod, g * HC + c + 1)
                    if c == 0 and not first:
                        act.wait_ge(out_done, g)
                    act.activation(a[:, c, :], wide[:, c, :], ACT.Relu, bias=b1[:, c:c + 1]).then_inc(act_out, 1)
                if not last:
                    first_part(g + 1)
            pairs(act, step)

        @block.vector
        def _(dve):
            link = Chain(dve, chain)

            def split_x(g):
                dve.wait_ge(xT_hi, g + 1)
                dve.tensor_tensor(xT[1][:], turned[:], xT[0][:].bitcast(F32), ALU.subtract).then_inc(xT_done, 1)
            dve.wait_ge(factors, 4)
            normalise(dve, s, xn[:, 0], 0, TT, normed)
            dve.wait_ge(w_in, 16)
            link.then(dve.tensor_copy(w1[0][:], raw1[:]))
            dve.tensor_tensor(w1[1][:], raw1[:], w1[0][:].bitcast(F32), ALU.subtract).then_inc(split, 1)
            split_x(0)
            dve.wait_ge(factors, 8)
            dve.wait_ge(vec_in, 16 * 5)
            before = link.base

            def make_x(g, b):
                if not (isinstance(g, int) and g < 2):
                    dve.wait_ge(turned_done, g - 1)
                    dve.wait_ge(xb_done, g - 1)
                normalise(dve, s, xn[:, b], g * TT, TT, normed)

            def make_z(g, b, meanwhile):
                dve.wait_ge(xb_done, g + 1)
                if not (isinstance(g, int) and g < 2):
                    dve.wait_ge(scaled, g - 1)
                dve.wait_ge(out_done, g + 1)
                dve.tensor_tensor(z[:, b], out[:, b], xb[:, b], ALU.add).then_inc(z_added, 1)
                dve.wait_ge(z_added, g + 1)
                for t in range(TT):
                    ins = dve.bn_stats(stats[:, t, :], z[:, b, t, :])
                link.then(ins)
                meanwhile()
                for t in range(TT):
                    ins = dve.bn_aggr(moments[:, b, t, :], stats[:, t, :])
                ins.then_inc(z_done, 1)

            def scale(g, b):
                dve.wait_ge(shift_done, g + 1)
                if not (isinstance(g, int) and g < 2):
                    dve.wait_ge(stored[b], (g - b) * 8)
                for t in range(TT):
                    ins = dve.tensor_scalar(y[:, b, t, :], z[:, b, t, :], rstd[:, b, t:t + 1],
                                            shift[:, b, t:t + 1], ALU.mult, ALU.add)
                ins.then_inc(scaled, 1)

            def add_x(g, b):
                dve.wait_ge(plus_beta, g + 1)
                dve.tensor_tensor(y[:, b], y[:, b], s.x[:, at(g * TT, TT), :], ALU.add).then_inc(y_done, 1)

            def step(g, b, first, last):
                if not last:
                    make_x(g + 1, 1 - b)
                link.start(before + (0 if first else g - 1))
                if not first:
                    make_z(g - 1, 1 - b, (lambda: None) if isinstance(g, int) and g == 1 else lambda: scale(g - 2, b))
                if not last:
                    split_x(g + 1)
                if not (isinstance(g, int) and g < 3):
                    add_x(g - 3, 1 - b)
            pairs(dve, step)
            add_x(STEPS - 3, 1)
            link.start(before + STEPS - 1)
            make_z(STEPS - 1, 1, lambda: scale(STEPS - 2, 0))
            add_x(STEPS - 2, 0)
            scale(STEPS - 1, 1)
            add_x(STEPS - 1, 1)
            dve.wait_ge(y_done, STEPS)

        @block.tensor
        def _(pe):
            def turn(g, b):
                pe.wait_ge(normed, (g + 1) * TT)
                for t in range(TT):
                    ins = pe.transpose(turned[:, t * P:(t + 1) * P], xn[:, b, t, :], s.ident[:])
                ins.then_inc(turned_done, 1)
            turn(0, 0)
            pe.wait_ge(split, 1)

            def step(g, b, first, last):
                pe.wait_ge(xT_done, g + 1)
                for c in range(HC):
                    if not first:
                        pe.wait_ge(act_out, (g - 1) * HC + c + 1)
                    for i, (p, q) in enumerate(PARTS):
                        ins = pe.matmul(wide[:, c, :], w1[p][:, c * P:(c + 1) * P], xT[q][:],
                                        start=(i == 0), stop=(i == 2))
                    ins.then_inc(prod, 1)
                if not last:
                    turn(g + 1, 1 - b)
                if first:
                    pe.wait_ge(vec_in, 16 * 5)
                if not (isinstance(g, int) and g < 2):
                    pe.wait_ge(z_done, g - 1)
                for t in range(TT):
                    for k in range(HC):
                        if t == 0:
                            pe.wait_ge(act_out, g * HC + k + 1)
                        ins = pe.matmul(out[:, b, t, :], a[:, k, t * P:(t + 1) * P], w2[:, k, :],
                                        start=(k == 0), stop=(k == HC - 1))
                ins.then_inc(out_done, 1)
            pairs(pe, step)


def attention_stack(nc, a, y):
    with ExitStack() as ctx:
        s = Stream(nc, ctx, a["x"].shape[0])
        load_stream(nc, s, a["x"])
        xattn_small(nc, s, a["x"], a["ctxT"], dict(q=a["q0_w"], qb=a["q0_b"], kv=a["kv0_w"], kb=a["k0_b"], vb=a["v0_b"],
                                                    o=a["o0_w"], ob=a["o0_b"]))
        ffn_gated(nc, s, dict(w1=a["w1"], w2=a["w2"], h1=a["h1"], h2=a["h2"], w3=a["w3"], w1s=a["w1_s"],
                              w2s=a["w2_s"], h1s=a["h1_s"], h2s=a["h2_s"], w3s=a["w3_s"]))
        xattn_large(nc, s, a["ctxT"], dict(q=a["q1_w"], k=a["k1_w"], v=a["v1_w"], o=a["o1_w"], ob=a["o1_b"]))
        ffn_expert(nc, s, dict(w1=a["e_w1"], b1=a["e_b1"], w2=a["e_w2"], b2=a["e_b2"], gamma=a["gamma"],
                               beta=a["beta"]), y)


def kernel(x, ctx_768, L0_xattn_q_w, L0_xattn_q_b, L0_xattn_kv_w, L0_xattn_kv_b, L0_xattn_proj_w, L0_xattn_proj_b,
           L0_ffn_w1_w, L0_ffn_w1_s, L0_ffn_w2_w, L0_ffn_w2_s, L0_ffn_h1_w, L0_ffn_h1_s, L0_ffn_h2_w, L0_ffn_h2_s,
           L0_ffn_w3_w, L0_ffn_w3_s, L1_xattn_w_q, L1_xattn_w_k, L1_xattn_w_v, L1_xattn_w_out, L1_xattn_b_out,
           L1_ffn_router_w, L1_ffn_router_b, L1_ffn_w1, L1_ffn_b1, L1_ffn_w2, L1_ffn_b2, L1_ffn_gamma,
           L1_ffn_beta):
    import numpy as np
    import concourse.bacc as bacc
    from concourse.bass_utils import run_bass_kernel_spmd

    def by_chunk(v):
        return np.asarray(v).reshape(-1, P).T

    batches, length, width = x.shape
    tokens = batches * length
    operands = {
        "x": np.asarray(x).reshape(tokens, width),
        "ctxT": np.asarray(ctx_768).reshape(tokens, -1).T,
        "q0_w": L0_xattn_q_w, "q0_b": by_chunk(L0_xattn_q_b), "kv0_w": L0_xattn_kv_w,
        "k0_b": by_chunk(np.asarray(L0_xattn_kv_b)[:width]), "v0_b": np.asarray(L0_xattn_kv_b)[width:],
        "o0_w": L0_xattn_proj_w, "o0_b": L0_xattn_proj_b,
        "w1": np.asarray(L0_ffn_w1_w).T, "w1_s": by_chunk(L0_ffn_w1_s),
        "w2": np.asarray(L0_ffn_w2_w).T, "w2_s": by_chunk(L0_ffn_w2_s),
        "h1": np.asarray(L0_ffn_h1_w).T, "h1_s": by_chunk(L0_ffn_h1_s),
        "h2": np.asarray(L0_ffn_h2_w).T, "h2_s": by_chunk(L0_ffn_h2_s),
        "w3": np.asarray(L0_ffn_w3_w).T, "w3_s": L0_ffn_w3_s,
        "q1_w": L1_xattn_w_q, "k1_w": L1_xattn_w_k, "v1_w": L1_xattn_w_v, "o1_w": L1_xattn_w_out,
        "o1_b": L1_xattn_b_out,
        "e_w1": np.asarray(L1_ffn_w1)[0], "e_b1": by_chunk(np.asarray(L1_ffn_b1)[0]),
        "e_w2": np.asarray(L1_ffn_w2)[0], "e_b2": np.asarray(L1_ffn_b2)[0],
        "gamma": L1_ffn_gamma, "beta": L1_ffn_beta,
    }
    nc = bacc.Bacc("TRN2", target_bir_lowering=False, num_devices=1)
    arrays, aps = {}, {}
    for name, a in operands.items():
        arrays[f"in_{name}"] = np.ascontiguousarray(a)
        aps[name] = nc.dram_tensor(f"in_{name}", list(arrays[f"in_{name}"].shape), F32, kind="ExternalInput").ap()
    y = nc.dram_tensor("out_y", [tokens, width], F32, kind="ExternalOutput").ap()
    attention_stack(nc, aps, y)
    result = run_bass_kernel_spmd(nc, [arrays], core_ids=[0])
    return result.results[0]["out_y"].reshape(batches, length, width)
```

```python
from contextlib import ExitStack

import concourse.bass as bass
from concourse import mybir

ALU = mybir.AluOpType
ACT = mybir.ActivationFunctionType
AX = mybir.AxisListType
F32 = mybir.dt.float32
F32R = mybir.dt.float32r

P = 128
D = 128
TOK = 512
TT = TOK // P
EPS = 1e-5
PARTS = ((0, 0), (1, 0), (0, 1))


class Stream:

    def __init__(self, nc, ctx, tokens):
        def sb(name, shape):
            return ctx.enter_context(nc.sbuf_tensor(name, shape, F32))
        self.nc, self.ctx = nc, ctx
        self.tiles = tokens // P
        self.x = sb("x", [P, self.tiles, D])
        self.moments = sb("moments", [P, self.tiles, 2])
        self.rstd = sb("rstd", [P, self.tiles])
        self.shift = sb("shift", [P, self.tiles])
        self.ident = sb("ident", [P, P])
        self.power = sb("power", [P, self.tiles])
        self.stats = sb("load_stats", [P, self.tiles, 6])
        self.x_in = [self.sem(f"x_in{c}") for c in range(4)]
        self.factors = {layer: self.sem(layer + "_norm_factors") for layer in "bcd"}
        self.stats_done, self.moments_done = self.sem("stats_done"), self.sem("moments_done")

    def sem(self, name):
        return self.ctx.enter_context(self.nc.semaphore(name))


def fetch_x(sp, s, x_dram, part):
    half = (EARLY if part < 2 else s.tiles - EARLY) // 2
    first = (0 if part < 2 else EARLY) + part % 2 * half
    sp.dma_start(s.x[:, first:first + half, :], x_dram.rearrange("(t p) d -> p t d", p=P)[
        :, first:first + half, :]).then_inc(s.x_in[part], 16)


def find_moments(dve, s, first, end):
    for t in range(first, end):
        dve.bn_stats(s.stats[:, t, :], s.x[:, t, :]).then_inc(s.stats_done, 1)
    for t in range(first, end):
        dve.wait_ge(s.stats_done, t + 1)
        dve.bn_aggr(s.moments[:, t, :], s.stats[:, t, :]).then_inc(s.moments_done, 1)


def rows(vec, n):
    return vec.rearrange("(a n) -> a n", a=1).broadcast_to([P, n])


def at(i, n=1):
    return slice(i, i + n) if isinstance(i, int) else bass.ds(i, n)


def norm_factors(pool, s, done, tiles, n):
    rstd, shift = s.rstd[:, tiles], s.shift[:, tiles]
    pool.tensor_scalar(rstd, s.moments[:, tiles, 1], EPS, 1.0, ALU.add, ALU.mult).then_inc(done, 1)
    pool.wait_ge(done, n + 1)
    pool.tensor_tensor(rstd, rstd, s.power[:, tiles], ALU.pow).then_inc(done, 1)
    pool.wait_ge(done, n + 2)
    pool.tensor_tensor(shift, s.moments[:, tiles, 0], rstd, ALU.mult).then_inc(done, 1)
    pool.wait_ge(done, n + 3)
    pool.tensor_scalar(shift, shift, -1.0, 0.0, ALU.mult, ALU.add).then_inc(done, 1)
    pool.wait_ge(done, n + 4)


def next_factors(pool, s, layer, update, tiles):
    pool.wait_ge(update.done, FIRST.stop // tiles)
    norm_factors(pool, s, s.factors[layer], FIRST, 0)
    pool.wait_ge(s.factors[layer], 4)


EARLY = 16
FIRST, LATER = slice(0, 8), slice(8, None)


def normalise(dve, s, xn, first_tile, tiles, normed):
    for t in range(tiles):
        i = first_tile + t
        dve.tensor_scalar(xn[:, t, :], s.x[:, at(i), :], s.rstd[:, at(i)], s.shift[:, at(i)],
                           ALU.mult, ALU.add).then_inc(normed, 1)


class Update:

    def __init__(self, s, sb, prefix, tiles):
        self.s, self.tiles = s, tiles
        self.fresh, self.stats = sb("fresh", [P, tiles, D]), sb("stats", [P, tiles, 6])
        self.pair = sb("pair", [P, tiles, 2])
        self.read, self.added, self.measured, self.stored, self.gathered, self.done = (
            s.sem(prefix + n) for n in ("x_got_read", "x_added", "x_measured", "x_stored", "x_gathered", "x_done"))

    def take(self, dve, got, other, n):
        if not (isinstance(n, int) and n == 1):
            dve.wait_ge(self.stored, n - 1)
        dve.tensor_tensor(self.fresh[:], got, other, ALU.add).then_inc(self.read, 1)

    def finish(self, dve, first_tile, n, add_x=True):
        s, x = self.s, self.s.x[:, at(first_tile, self.tiles), :]
        dve.wait_ge(self.read, n)
        if add_x:
            dve.tensor_tensor(self.fresh[:], self.fresh[:], x, ALU.add).then_inc(self.added, 1)
            dve.wait_ge(self.added, n)
        for t in range(self.tiles):
            ins = dve.bn_stats(self.stats[:, t, :], self.fresh[:, t, :])
        ins.then_inc(self.measured, 1)
        dve.wait_ge(self.measured, n)
        dve.tensor_scalar(x, self.fresh[:], 1.0, None, ALU.mult).then_inc(self.stored, 1)
        for t in range(self.tiles):
            ins = dve.bn_aggr(self.pair[:, t, :], self.stats[:, t, :])
        ins.then_inc(self.gathered, 1)
        dve.wait_ge(self.gathered, n)
        dve.tensor_scalar(s.moments[:, at(first_tile, self.tiles), :], self.pair[:], 1.0, None,
                          ALU.mult).then_inc(self.done, 1)

    def run(self, dve, got, bias, first_tile, n):
        x = self.s.x[:, at(first_tile, self.tiles), :]
        self.take(dve, got, x if bias is None else bias, n)
        self.finish(dve, first_tile, n, bias is not None)


def load_stream(nc, s, x_dram):
    zeroed, made = s.sem("ident_zeroed"), s.sem("constants_made")
    with nc.Block() as block:
        @block.sync
        def _(sp):
            fetch_x(sp, s, x_dram, 0)
            fetch_x(sp, s, x_dram, 1)

        @block.gpsimd
        def _(pool):
            pool.memset(s.ident[:], 0.0).then_inc(zeroed, 1)
            pool.memset(s.power[:], -0.5).then_inc(made, 1)
            pool.wait_ge(zeroed, 1)
            pool.affine_select(out=s.ident[:], in_=s.ident[:], compare_op=ALU.not_equal, fill=1.0, base=0,
                               pattern=[[-1, P]], channel_multiplier=1).then_inc(made, 1)
            pool.wait_ge(made, 2)

        @block.vector
        def _(dve):
            for part in (0, 1):
                dve.wait_ge(s.x_in[part], 16)
                find_moments(dve, s, part * EARLY // 2, (part + 1) * EARLY // 2)
            dve.wait_ge(s.moments_done, EARLY)


class Chain:

    def __init__(self, eng, sem):
        self.eng, self.sem, self.base = eng, sem, 0

    def start(self, base):
        self.base = base

    def then(self, ins):
        ins.then_inc(self.sem, 1)
        self.base = self.base + 1
        self.eng.wait_ge(self.sem, self.base)


def split(dve, hi, lo, src, hi_sem, hi_count, lo_sem):
    dve.tensor_copy(hi, src).then_inc(hi_sem, 1)
    dve.wait_ge(hi_sem, hi_count)
    dve.tensor_tensor(lo, src, hi.bitcast(F32), ALU.subtract).then_inc(lo_sem, 1)


def xattn_small(nc, s, x_dram, cT_dram, w):
    NH, HD, B = 16, D // 16, 64
    HP = NH // 2
    CD = cT_dram.shape[0]
    SCALE = float(HD) ** -0.5
    ROWS = 4 * HD
    NB = TOK // B
    STEPS = s.tiles // TT
    V1 = HD + 1
    with ExitStack() as ctx:
        def sb(n, shape, dt=F32):
            return ctx.enter_context(nc.sbuf_tensor("a_" + n, shape, dt))

        def ps(n, shape):
            return ctx.enter_context(nc.psum_tensor("a_" + n, shape, F32))

        def sem(n):
            return s.sem("a_" + n)

        raw_q, raw_kv = sb("raw_q", [P, D]), sb("raw_kv", [CD, 2 * D])
        wq, wk = [sb(f"wq_{i}", [P, D], F32R) for i in "01"], [sb(f"wk_{i}", [CD, D], F32R) for i in "01"]
        wo, qb, kb = sb("wo", [P, D]), sb("qb", [P, 1]), sb("kb", [P, 1])
        qbs = sb("qb_scaled", [P, 1])
        vb, ob = sb("vb", [P, D]), sb("ob", [P, D])
        xn = sb("xn", [P, TT, D])
        xT = [sb(f"xT_{i}", [P, TOK], F32R) for i in "01"]
        cT = [sb(f"cT{b}", [CD, NB, 2, B]) for b in "01"]
        cp = [sb(f"c_{i}", [CD, TOK], F32R) for i in "01"]
        qf, kf = sb("qf", [P, TOK]), sb("kf", [P, TOK])
        kp = [sb(f"k_{i}", [P, TOK]) for i in "01"]
        qz = [[sb(f"qz{b}_{i}", [P, NH // 4, TT, 3 * B], F32R) for i in "01"] for b in "01"]
        zero = sb("zero", [P, 1])
        kz = [[sb(f"kz{b}_{i}", [P, 4, TOK], F32R) for i in "01"] for b in "01"]
        vz = [sb(f"vz{b}", [P, TT, HP, 2, 2 * V1]) for b in "01"]
        head_rows, mask = sb("head_rows", [P, NH]), sb("mask", [P, 4])
        top = sb("top", [P, 2, NH])
        e = [sb(f"e{u}", [P, NH, B]) for u in "01"]
        eT = sb("eT", [P, HP, P])
        inv = sb("inv", [P, 2, HP, 2])
        o = sb("o", [P, TT, D])
        oT = sb("oT", [P, TOK])
        update = Update(s, sb, "a_", TT)
        scores = [ps(f"scores{u}", [P, NH, B]) for u in "01"]
        turned_e, att, misc = ps("turned_e", [P, HP, P]), ps("att", [P, HP, 2, 2, V1]), ps("misc", [P, TOK])

        w_in, vec_in = sem("weights_in"), sem("vectors_in")
        c_in = [sem("ctx_in0"), sem("ctx_in1")]
        w_hi, w_split = sem("weights_hi"), sem("weights_split")
        made, made_1, mask_made = sem("constants_made"), sem("parity_1_cleared"), sem("mask_made")
        factors, normed = sem("norm_factors"), sem("normed")
        turned, x_hi, x_split = sem("xn_turned"), sem("x_hi"), sem("x_split")
        c_hi, c_split = sem("c_hi"), sem("c_split")
        q_prod, q_out, q_hi, q_split = sem("q_product"), sem("q_out"), sem("q_hi"), sem("q_split")
        k_prod, k_out, k_hi, k_split, k_masked = (sem(n) for n in ("k_product", "k_out", "k_hi", "k_split",
                                                                  "k_masked"))
        v_prod, v_out = sem("v_product"), sem("v_out")
        o_turned, o_out, proj_done = sem("o_turned"), sem("o_out"), sem("projected")
        scored, top_done, shifted, exped = sem("scored"), sem("top_done"), sem("shifted"), sem("exped")
        e_turned = sem("e_turned")
        eT_act, eT_dve = sem("eT_by_act"), sem("eT_by_dve")
        attended, inv_done, normal = sem("attended"), sem("inv_done"), sem("o_normalised")
        block = ctx.enter_context(nc.Block())

        def exists(g):
            return not isinstance(g, int) or 0 <= g < STEPS

        def bodies(eng, body):
            body(0, 0)
            body(1, 1)
            with eng.Fori(1, STEPS // 2 - 1) as i:
                body(2 * i, 0)
                body(2 * i + 1, 1)
            body(STEPS - 2, 0)
            body(STEPS - 1, 1)
            body(STEPS, 0)

        def by_batch(t):
            return t[:].rearrange("c (b k) -> c b k", k=B)

        def is0(g):
            return isinstance(g, int) and g == 0

        def clear_queries(eng, b, i, done):
            eng.memset(qz[b][i][:].bitcast(F32), 0.0).then_inc(done, 1)

        def clear_values(eng, b, done, n):
            eng.memset(vz[b][:], 0.0).then_inc(done, 1)
            eng.wait_ge(done, n + 1)
            eng.memset(vz[b][0:B, :, :, :, HD:V1], 1.0).then_inc(done, 1)
            eng.memset(vz[b][B:P, :, :, :, V1 + HD:2 * V1], 1.0).then_inc(done, 1)
        CLEARED = 9

        @block.sync
        def _(sp):
            def fetch(sp, g, b):
                for copy in (0, 1):
                    sp.dma_start(cT[b][:, :, copy, :], cT_dram[:, at(g * TOK, TOK)].rearrange(
                        "c (b k) -> c b k", k=B)).then_inc(c_in[b], 16)

            sp.dma_start(raw_q[:], w["q"]).then_inc(w_in, 16)
            sp.dma_start(raw_kv[:], w["kv"]).then_inc(w_in, 16)
            fetch(sp, 0, 0)
            sp.dma_start(qb[:], w["qb"]).then_inc(vec_in, 16)
            sp.dma_start(kb[:], w["kb"]).then_inc(vec_in, 16)
            sp.dma_start(vb[:], rows(w["vb"], D)).then_inc(vec_in, 16)
            sp.dma_start(ob[:], rows(w["ob"], D)).then_inc(vec_in, 16)
            sp.dma_start(wo[:], w["o"]).then_inc(vec_in, 16)

            def body(g, b):
                after = exists(g + 1)
                if after:
                    if not is0(g):
                        sp.wait_ge(v_prod, 2 * g)
                    fetch(sp, g + 1, 1 - b)
                if is0(g):
                    fetch_x(sp, s, x_dram, 2)
                    fetch_x(sp, s, x_dram, 3)
            bodies(sp, body)

        @block.gpsimd
        def _(pool):
            norm_factors(pool, s, factors, slice(0, EARLY), 0)
            pool.memset(zero[:], 0.0).then_inc(made, 1)
            pool.memset(head_rows[:], 1.0).then_inc(made, 1)
            pool.wait_ge(made, 2)
            pool.affine_select(out=head_rows[:], in_=head_rows[:], compare_op=ALU.is_ge, fill=0.0, base=0,
                               pattern=[[-HD, NH]], channel_multiplier=1).then_inc(made, 1)
            pool.wait_ge(made, 3)
            pool.affine_select(out=head_rows[:], in_=head_rows[:], compare_op=ALU.is_ge, fill=0.0, base=HD - 1,
                               pattern=[[HD, NH]], channel_multiplier=-1).then_inc(made, 1)
            clear_queries(pool, 0, 0, made)
            clear_queries(pool, 0, 1, made)
            clear_values(pool, 0, made, 6)

            def q_parts(g, b):
                pool.wait_ge(q_out, g + 1)
                grouped = qf[:].rearrange("p (t a q) -> p t a q", a=2, q=B)
                for i in (0, 1):
                    for r in range(NH // 4):
                        rs = slice(r * ROWS, (r + 1) * ROWS)
                        hi, out = (qz[b][k][rs, r].rearrange("p t (a q) -> p t a q", a=3)[:, :, 0:3:2, :]
                                   for k in (0, i))
                        if i == 0:
                            none = zero[rs].rearrange("p (a b c) -> p a b c", a=1, b=1).broadcast_to([ROWS, TT, 2, B])
                            ins = pool.tensor_tensor(out, grouped[rs], none, ALU.add)
                        else:
                            ins = pool.tensor_tensor(out, grouped[rs], hi.bitcast(F32), ALU.subtract)
                    ins.then_inc(q_split if i else q_hi, 1)
                    if i == 0:
                        pool.wait_ge(q_hi, g + 1)
            pool.wait_ge(made, CLEARED)
            q_parts(0, 0)

            def body(g, b):
                if is0(g):
                    pool.wait_ge(made_1, 5)
                if exists(g + 1):
                    q_parts(g + 1, 1 - b)
                if isinstance(g, int) and g == 1:
                    pool.wait_ge(s.moments_done, s.tiles)
                    pool.wait_ge(q_split, g + 2)
                    norm_factors(pool, s, factors, slice(EARLY, None), 4)
            bodies(pool, body)
            pool.wait_ge(q_split, STEPS)
            next_factors(pool, s, "b", update, TT)

        @block.scalar
        def _(act):
            def c_round(g, b):
                act.wait_ge(c_in[b], (g - b) * 16 + 32)
                if not is0(g):
                    act.wait_ge(k_prod, g)
                act.activation(by_batch(cp[0]), cT[b][:, :, 0, :], ACT.Copy).then_inc(c_hi, 1)

            def q_evacuate(g):
                act.wait_ge(q_prod, g + 1)
                act.activation(qf[:], misc[:], ACT.Identity, bias=qbs[:, 0:1], scale=SCALE).then_inc(q_out, 1)

            def k_evacuate(g):
                act.wait_ge(k_prod, g + 1)
                act.activation(kf[:], misc[:], ACT.Identity, bias=kb[:, 0:1]).then_inc(k_out, 1)

            def mask_keys(g, b, i):
                act.wait_ge(k_split, g + 1)
                for j in range(4):
                    ins = act.activation(kz[b][i][:, j, :], kp[i][:], ACT.Copy, scale=mask[:, j:j + 1])
                ins.then_inc(k_masked, 1)

            def o_evacuate(g):
                act.wait_ge(o_turned, g + 1)
                act.activation(oT[:], misc[:], ACT.Copy).then_inc(o_out, 1)

            def eT_half(m):
                act.wait_ge(e_turned, 2 * m + 1)
                act.activation(eT[:, 0:HP // 2, :], turned_e[:, 0:HP // 2, :], ACT.Copy).then_inc(eT_act, 1)

            def exp(n, u):
                act.wait_ge(shifted, n + 1)
                act.activation(e[u][:], e[u][:], ACT.Exp).then_inc(exped, 1)

            c_round(0, 0)
            act.wait_ge(vec_in, 16 * 5)
            act.activation(qbs[:], qb[:], ACT.Copy, scale=SCALE).then_inc(w_split, 1)
            act.wait_ge(w_split, 3)
            q_evacuate(0)
            k_evacuate(0)
            act.wait_ge(mask_made, 1)
            mask_keys(0, 0, 0)
            mask_keys(0, 0, 1)

            def body(g, b):
                here, after = exists(g), exists(g + 1)
                for p in range(TT):
                    n = g * TT + p
                    if p == 0 and after:
                        c_round(g + 1, 1 - b)
                    if (not is0(g) or p >= 2) and (here or p < 2):
                        eT_half(n - 2)
                    if p == 1 and after:
                        q_evacuate(g + 1)
                        k_evacuate(g + 1)
                    if p == 2 and after:
                        mask_keys(g + 1, 1 - b, 0)
                    if p == 2 and not is0(g):
                        o_evacuate(g - 1)
                    if here:
                        exp(n, p % 2)
                    if p == 2 and after:
                        mask_keys(g + 1, 1 - b, 1)
            bodies(act, body)

        @block.vector
        def _(dve):
            clear_queries(dve, 1, 0, made_1)
            dve.wait_ge(w_in, 32)
            split(dve, wq[0][:], wq[1][:], raw_q[:], w_hi, 1, w_split)
            split(dve, wk[0][:], wk[1][:], raw_kv[:, 0:D], w_hi, 2, w_split)
            dve.wait_ge(made, 4)
            dve.tensor_reduce(mask[:], head_rows[:].rearrange("p (q j) -> p j q", j=4), AX.X,
                              ALU.add).then_inc(mask_made, 1)

            def x_parts(g):
                dve.wait_ge(turned, g + 1)
                split(dve, xT[0][:], xT[1][:], misc[:], x_hi, g + 1, x_split)

            def c_low(g, b):
                dve.wait_ge(c_hi, g + 1)
                dve.tensor_tensor(by_batch(cp[1]), cT[b][:, :, 0, :], by_batch(cp[0]).bitcast(F32),
                                  ALU.subtract).then_inc(c_split, 1)

            def k_parts(g):
                dve.wait_ge(k_out, g + 1)
                if not is0(g):
                    dve.wait_ge(k_masked, 2 * g)
                dve.tensor_copy(kp[0][:].bitcast(F32R), kf[:]).then_inc(k_hi, 1)
                dve.wait_ge(k_hi, g + 1)
                dve.tensor_tensor(kp[1][:], kf[:], kp[0][:], ALU.subtract).then_inc(k_split, 1)

            def v_half(g, b, i):
                dve.wait_ge(v_prod, 2 * g + i + 1)
                ts = slice(i * TT // 2, (i + 1) * TT // 2)
                into = vz[b][:, ts].rearrange("p t h a c -> p t a h c")
                v = misc[:].rearrange("p (t a h o d) -> p t a h o d", t=TT // 2, a=2, o=2, d=HD)
                bias = vb[:].rearrange("p (a h o d) -> p a h o d", a=1, o=2, d=HD).broadcast_to([P, 2, HP, 2, HD])
                for odd in (0, 1):
                    rs = slice(odd * B, odd * B + B)
                    for t in range(TT // 2):
                        ins = dve.tensor_tensor(into[rs, t, :, :, odd * V1:odd * V1 + HD], v[rs, t, :, :, odd, :],
                                                bias[rs, :, :, odd, :], ALU.add)
                ins.then_inc(v_out, 1)

            def softmax(g, n, u):
                dve.wait_ge(scored, n + 1)
                dve.tensor_reduce(top[:, u], scores[u][:], AX.X, ALU.max).then_inc(top_done, 1)
                dve.wait_ge(top_done, n + 1)
                if not (isinstance(n, int) and n < 2):
                    dve.wait_ge(e_turned, 2 * n - 2)
                peak = top[:, u].rearrange("p (h a) -> p h a", a=1).broadcast_to([P, NH, B])
                dve.tensor_tensor(e[u][:], scores[u][:], peak, ALU.subtract).then_inc(shifted, 1)

            def eT_half(m):
                dve.wait_ge(e_turned, 2 * m + 2)
                dve.tensor_copy(eT[:, HP // 2:, :], turned_e[:, HP // 2:, :]).then_inc(eT_dve, 1)

            def o_normalise(m, t, g):
                dve.wait_ge(attended, m + 1)
                halves = [(slice(a * B, a * B + B), att[a * B:a * B + B, :, a]) for a in (0, 1)]
                for rs, got in halves:
                    ins = dve.reciprocal(inv[rs, t % 2], got[:, :, :, HD])
                ins.then_inc(inv_done, 1)
                dve.wait_ge(inv_done, m + 1)
                if t == 0 and not is0(g):
                    dve.wait_ge(o_turned, g)
                for rs, got in halves:
                    sums = inv[rs, t % 2].rearrange("p h (o a) -> p h o a", a=1).broadcast_to([B, HP, 2, HD])
                    ins = dve.tensor_tensor(o[rs, t, :].rearrange("p (h o d) -> p h o d", h=HP, o=2),
                                            got[:, :, :, 0:HD], sums, ALU.mult)
                ins.then_inc(normal, 1)

            def take_update(g):
                dve.wait_ge(proj_done, g + 1)
                bias = ob[:].rearrange("p (a d) -> p a d", a=1).broadcast_to([P, TT, D])
                update.take(dve, misc[:].rearrange("p (t d) -> p t d", d=D), bias, g + 1)

            def make_x(g):
                if not is0(g):
                    dve.wait_ge(turned, g)
                normalise(dve, s, xn, g * TT, TT, normed)

            c_low(0, 0)
            dve.wait_ge(factors, 4)
            make_x(0)
            x_parts(0)
            make_x(1)
            k_parts(0)
            dve.wait_ge(vec_in, 16 * 5)
            dve.wait_ge(made, CLEARED)
            v_half(0, 0, 0)
            v_half(0, 0, 1)
            clear_queries(dve, 1, 1, made_1)
            clear_values(dve, 1, made_1, 2)
            dve.wait_ge(made_1, 5)

            def body(g, b):
                here, after = exists(g), exists(g + 1)
                for p in range(TT):
                    n = g * TT + p
                    m = n - 2
                    behind = (not is0(g) or p >= 2) and (here or p < 2)
                    if p == 2 and after:
                        k_parts(g + 1)
                    if behind:
                        eT_half(m)
                    if p >= 2 and after:
                        v_half(g + 1, 1 - b, p - 2)
                    if here:
                        softmax(g, n, p % 2)
                    if p == 3 and exists(g + 2):
                        if not (isinstance(g, int) and g < 2):
                            dve.wait_ge(factors, 8)
                        make_x(g + 2)
                    if isinstance(g, int) and g < 2:
                        if p == 0:
                            dve.wait_ge(s.x_in[2 + g], 16)
                        share = (s.tiles - EARLY) // (2 * TT)
                        first = EARLY + n * share
                        find_moments(dve, s, first, first + share)
                    if p == 0 and after:
                        x_parts(g + 1)
                        c_low(g + 1, 1 - b)
                    if behind:
                        o_normalise(m, (p + 2) % TT, g)
                    if p == 2 and exists(g - 2):
                        update.finish(dve, (g - 2) * TT, g - 1)
                    if p == 3 and exists(g - 1):
                        take_update(g - 1)
            bodies(dve, body)
            update.finish(dve, (STEPS - 1) * TT, STEPS)
            dve.wait_ge(update.done, STEPS)

        @block.tensor
        def _(pe):
            def turn_x(g):
                pe.wait_ge(normed, (g + 1) * TT)
                for t in range(TT):
                    ins = pe.transpose(misc[:, t * P:(t + 1) * P], xn[:, t, :], s.ident[:])
                ins.then_inc(turned, 1)

            def make_q(g):
                pe.wait_ge(x_split, g + 1)
                for i, (a, c) in enumerate(PARTS):
                    ins = pe.matmul(misc[:], wq[a][:], xT[c][:], start=(i == 0), stop=(i == 2))
                ins.then_inc(q_prod, 1)

            def make_k(g):
                pe.wait_ge(c_split, g + 1)
                pe.wait_ge(q_out, g + 1)
                for i, (a, c) in enumerate(PARTS):
                    ins = pe.matmul(misc[:], wk[a][:], cp[c][:], start=(i == 0), stop=(i == 2))
                ins.then_inc(k_prod, 1)

            def make_v(g, b, i):
                if i == 0:
                    pe.wait_ge(k_out, g + 1)
                else:
                    pe.wait_ge(v_out, 2 * g + 1)
                for j in range(NB // 2):
                    twice = cT[b][:, i * NB // 2 + j].rearrange("c a k -> c (a k)")
                    ins = pe.matmul(misc[:, j * D:(j + 1) * D], twice, raw_kv[:, D:2 * D], start=True, stop=True)
                ins.then_inc(v_prod, 1)

            def score(g, b, p, n):
                if not (isinstance(n, int) and n < 2):
                    pe.wait_ge(shifted, n - 1)
                out = scores[p % 2][:].rearrange("q h k -> q (h k)")
                for r in range(NH // 4):
                    for half in (0, 1):
                        for i, (a, c) in enumerate(PARTS):
                            batch = 2 * p + half
                            ins = pe.matmul(out[:, r * 4 * B:(r + 1) * 4 * B],
                                            qz[b][c][:, r, p, half * B:half * B + P],
                                            kz[b][a][:, :, batch * B:(batch + 1) * B],
                                            start=(half == 0 and i == 0), stop=(half == 1 and i == 2))
                ins.then_inc(scored, 1)

            def turn_e(m, u):
                pe.wait_ge(exped, m + 1)
                for t in range(HP):
                    ins = pe.transpose(turned_e[:, t, :], e[u][:, 2 * t:2 * t + 2, :].rearrange("q h k -> q (h k)"),
                                       s.ident[:])
                    if t % (HP // 2) == HP // 2 - 1:
                        ins.then_inc(e_turned, 1)

            def attend(m, b, p):
                pe.wait_ge(eT_act, m + 1)
                if not (isinstance(m, int) and m == 0):
                    pe.wait_ge(normal, m)
                for t in range(HP):
                    if t == HP // 2:
                        pe.wait_ge(eT_dve, m + 1)
                    ins = pe.matmul(att[:, t].rearrange("q a h d -> q (a h d)"), eT[:, t, :],
                                    vz[b][:, p, t].rearrange("k a c -> k (a c)"), start=True, stop=True)
                ins.then_inc(attended, 1)

            def turn_o(g):
                pe.wait_ge(normal, (g + 1) * TT)
                for t in range(TT):
                    ins = pe.transpose(misc[:, t * P:(t + 1) * P], o[:, t, :], s.ident[:])
                ins.then_inc(o_turned, 1)

            def project(g):
                pe.wait_ge(o_out, g + 1)
                for t in range(TT):
                    ins = pe.matmul(misc[:, t * D:(t + 1) * D], oT[:, t * P:(t + 1) * P], wo[:], start=True,
                                    stop=True)
                ins.then_inc(proj_done, 1)

            turn_x(0)
            pe.wait_ge(w_split, 3)
            make_q(0)
            make_k(0)
            pe.wait_ge(vec_in, 16 * 5)
            pe.wait_ge(made, CLEARED)
            make_v(0, 0, 0)
            make_v(0, 0, 1)

            def body(g, b):
                here, after = exists(g), exists(g + 1)
                for p in range(TT):
                    n = g * TT + p
                    behind = (not is0(g) or p >= 2) and (here or p < 2)
                    mb = b if p >= 2 else 1 - b
                    if behind:
                        turn_e(n - 2, p % 2)
                    if p == 2 and after:
                        make_v(g + 1, 1 - b, 0)
                    if p == 3 and after:
                        if not is0(g):
                            pe.wait_ge(o_out, g)
                        make_v(g + 1, 1 - b, 1)
                    if here:
                        if p == 0:
                            pe.wait_ge(q_split, g + 1)
                            pe.wait_ge(k_masked, 2 * (g + 1))
                        score(g, b, p, n)
                    if p == 0 and after:
                        if is0(g):
                            pe.wait_ge(v_out, 2)
                        else:
                            pe.wait_ge(eT_dve, n - 1)
                        turn_x(g + 1)
                    if p == 1 and after:
                        make_q(g + 1)
                    if p == 2 and not is0(g):
                        if after:
                            pe.wait_ge(v_out, 2 * g + 3)
                        turn_o(g - 1)
                    if behind:
                        attend(n - 2, mb, (p + 2) % TT)
                    if p == 1 and after:
                        make_k(g + 1)
                    if p == 3 and not is0(g) :
                        if after:
                            pe.wait_ge(v_out, 2 * (g + 2))
                        project(g - 1)
            bodies(pe, body)


def ffn_gated(nc, s, w):
    H = w["w1"].shape[1]
    HC = H // P
    RING = 4
    STEPS = s.tiles // TT
    with ExitStack() as ctx:
        def sb(n, shape, dt=F32):
            return ctx.enter_context(nc.sbuf_tensor("b_" + n, shape, dt))

        def ps(n, shape):
            return ctx.enter_context(nc.psum_tensor("b_" + n, shape, F32))

        def sem(n):
            return s.sem("b_" + n)

        raw12, raw_h1, raw_h2 = sb("raw12", [P, 2, H]), sb("raw_h1", [P, HC, H]), sb("raw_h2", [P, HC, H])
        w1, w2 = ([sb(f"{n}_{i}", [P, H], F32R) for i in "01"] for n in ("w1", "w2"))
        h1, h2 = ([sb(f"{n}_{i}", [P, HC, H], F32R) for i in "01"] for n in ("h1", "h2"))
        raw_w3, s3 = sb("raw_w3", [P, HC, D]), sb("s3", [P, 1])
        w3 = [sb(f"w3_{i}", [P, HC, D], F32R) for i in "01"]
        s1, s2, sh1, sh2 = (sb(n, [P, HC]) for n in ("s1", "s2", "sh1", "sh2"))
        xn = sb("xn", [P, TT, D])
        xT = [sb(f"xT_{i}", [P, TOK], F32R) for i in "01"]
        full = sb("full", [P, HC, TOK])
        a1, a2, a3 = ([sb(f"{n}_{i}", [P, HC, TOK], F32R) for i in "01"] for n in ("a1", "a2", "a3"))
        outT_sb = sb("outT_sb", [P, TOK])
        FLAGS = 3 + 2 * HC
        BF16 = mybir.dt.bfloat16
        flags, ones = sb("flags", [P, FLAGS, H], BF16), sb("ones", [P, P], BF16)
        verdict = sb("verdict", [P, 1])
        update = Update(s, sb, "b_", TT)
        wide, turned = ps("wide", [P, RING, TOK]), ps("turned", [P, TOK])
        outT, out = ps("outT", [P, TOK]), ps("out", [P, TT, D])

        w_in = [sem(f"weights_in{i}") for i in range(4)]
        vec_in = sem("vectors_in")
        hi_done = sem("first_parts")
        split = sem("weights_split")
        factors, normed = s.factors["b"], sem("normed")
        turned_done = sem("turned_done")
        xT_done = sem("xT_done")
        w_prod = sem("w_products")
        h_prod = sem("h_products")
        w_act = sem("w_gates")
        h_act = sem("h_gelu")
        gated = sem("gated")
        even_hi = sem("even_chunks_hi")
        parts = [sem("even_parts"), sem("odd_parts")]
        a3_parts = sem("a3_parts")
        outT_done = sem("outT_done")
        scaled = sem("outT_scaled")
        out_done = sem("out_done")
        ones_made, flagged = sem("ones_made"), sem("weights_flagged")
        counted, judged = sem("flags_counted"), sem("judged")
        chain = sem("dve_chain")
        block = ctx.enter_context(nc.Block())

        def whole(eng, period):
            period(0, True, False)
            with eng.Fori(1, STEPS - 1) as g:
                period(g, False, False)
            period(STEPS - 1, False, True)

        def nth_h(g, layer, c):
            return 2 * HC * g + layer * HC + c + 1

        def nth_w(g, i, c):
            return 2 * HC * g + 2 * c + i + 1

        def nth(g, c):
            return HC * g + c + 1

        def parts_a1(g, c):
            return HC * g + c // 2 + 1

        def parts_a2(g, c):
            return HC * g + HC // 2 + c // 2 + 1

        @block.sync
        def _(sp):
            sp.dma_start(raw12[:, 0, :], w["w1"]).then_inc(w_in[0], 16)
            sp.dma_start(raw12[:, 1, :], w["w2"]).then_inc(w_in[0], 16)
            for v, n in ((s1, "w1s"), (s2, "w2s"), (sh1, "h1s"), (sh2, "h2s")):
                sp.dma_start(v[:], w[n]).then_inc(vec_in, 16)
            sp.dma_start(s3[:], w["w3s"].rearrange("(p a) -> p a", a=1)).then_inc(vec_in, 16)
            sp.dma_start(raw_h1[:], w["h1"].rearrange("(k p) o -> p k o", p=P)).then_inc(w_in[1], 16)
            sp.dma_start(raw_h2[:], w["h2"].rearrange("(k p) o -> p k o", p=P)).then_inc(w_in[2], 16)
            sp.dma_start(raw_w3[:], w["w3"].rearrange("(k p) o -> p k o", p=P)).then_inc(w_in[3], 16)

        @block.gpsimd
        def _(pool):
            norm_factors(pool, s, factors, LATER, 4)
            def second_parts(g, number, a):
                for c in range(0, HC, 2):
                    pool.wait_ge(even_hi, number(g, c))
                    pool.tensor_tensor(a[1][:, c, :], full[:, c, :], a[0][:, c, :].bitcast(F32),
                                       ALU.subtract).then_inc(parts[0], 1)

            def flag(n, lo, out):
                pool.wait_ge(split, n)
                pool.tensor_scalar(out, lo.bitcast(F32), 0.0, 0.5, ALU.is_equal, ALU.is_lt).then_inc(flagged, 1)

            pool.memset(ones[:], 1.0).then_inc(ones_made, 1)
            flag(1, w1[1][:], flags[:, 0, :])
            flag(2, w2[1][:], flags[:, 1, :])
            second_parts(0, parts_a1, a1)
            flag(3, h1[1][:], flags[:, 2:2 + HC, :])

            def period(g, first, last):
                second_parts(g, parts_a2, a2)
                if first:
                    flag(4, h2[1][:], flags[:, 2 + HC:2 + 2 * HC, :])
                    flag(5, w3[1][:].rearrange("p k o -> p (k o)"), flags[:, 2 + 2 * HC, :])
                if not last:
                    second_parts(g + 1, parts_a1, a1)
            whole(pool, period)
            next_factors(pool, s, "c", update, TT)

        @block.scalar
        def _(act):
            def first_part(i, raw, h):
                act.wait_ge(w_in[1 + i], 16)
                act.activation(h[0][:], raw[:], ACT.Copy).then_inc(hi_done, 1)
            first_part(0, raw_h1, h1)
            act.wait_ge(vec_in, 16 * 5)

            def gate(g):
                for c in range(HC):
                    act.wait_ge(w_prod, nth_w(g, 0, c))
                    if not (isinstance(g, int) and g == 0):
                        act.wait_ge(parts[c % 2], parts_a2(g - 1, c))
                    act.activation(full[:, c, :], wide[:, 2 * c % RING, :], ACT.Silu,
                                   scale=s1[:, c:c + 1]).then_inc(w_act, 1)

            def scale_out(g):
                act.wait_ge(outT_done, g + 1)
                if not (isinstance(g, int) and g == 0):
                    act.wait_ge(out_done, g)
                act.activation(outT_sb[:], outT[:], ACT.Copy, scale=s3[:, 0:1]).then_inc(scaled, 1)

            gate(0)
            first_part(1, raw_h2, h2)
            first_part(2, raw_w3, w3)

            def period(g, first, last):
                for c in range(HC):
                    act.wait_ge(h_prod, nth_h(g, 0, c))
                    if first:
                        act.wait_ge(parts[c % 2], parts_a1(g, c))
                    else:
                        act.wait_ge(a3_parts, nth(g - 1, c))
                    act.activation(full[:, c, :], wide[:, c % RING, :], ACT.Gelu,
                                   scale=sh1[:, c:c + 1]).then_inc(h_act, 1)
                if not last:
                    gate(g + 1)
                if not first:
                    scale_out(g - 1)
                for c in range(HC):
                    act.wait_ge(h_prod, nth_h(g, 1, c))
                    act.wait_ge(parts[c % 2], parts_a2(g, c) if last else parts_a1(g + 1, c))
                    act.activation(full[:, c, :], wide[:, c % RING, :], ACT.Gelu,
                                   scale=sh2[:, c:c + 1]).then_inc(h_act, 1)
            whole(act, period)
            scale_out(STEPS - 1)

        @block.vector
        def _(dve):
            link = Chain(dve, chain)

            def make_x(g):
                normalise(dve, s, xn, g * TT, TT, normed)

            def split_x(g):
                dve.wait_ge(turned_done, g + 1)
                link.then(dve.tensor_copy(xT[0][:], turned[:]))
                dve.tensor_tensor(xT[1][:], turned[:], xT[0][:].bitcast(F32), ALU.subtract).then_inc(xT_done, 1)
            dve.wait_ge(factors, 4)
            make_x(0)
            dve.wait_ge(w_in[0], 32)
            link.then(dve.tensor_copy(w1[0][:], raw12[:, 0, :]))
            dve.tensor_tensor(w1[1][:], raw12[:, 0, :], w1[0][:].bitcast(F32), ALU.subtract).then_inc(split, 1)
            link.then(dve.tensor_copy(w2[0][:], raw12[:, 1, :]))
            dve.tensor_tensor(w2[1][:], raw12[:, 1, :], w2[0][:].bitcast(F32), ALU.subtract).then_inc(split, 1)
            split_x(0)

            def second_parts(i, raw, h):
                dve.wait_ge(hi_done, i + 1)
                dve.tensor_tensor(h[1][:], raw[:], h[0][:].bitcast(F32), ALU.subtract).then_inc(split, 1)
            second_parts(0, raw_h1, h1)
            dve.wait_ge(turned_done, 1)
            make_x(1)

            def halve(a, c, both=False):
                hi = dve.tensor_copy(a[0][:, c, :], full[:, c, :])
                if c % 2 == 0 and not both:
                    hi.then_inc(even_hi, 1)
                else:
                    link.then(hi)
                    dve.tensor_tensor(a[1][:, c, :], full[:, c, :], a[0][:, c, :].bitcast(F32),
                                      ALU.subtract).then_inc(a3_parts if both else parts[1], 1)

            def gate(g):
                for c in range(HC):
                    dve.wait_ge(w_act, nth(g, c))
                    dve.wait_ge(w_prod, nth_w(g, 1, c))
                    dve.scalar_tensor_tensor(out=full[:, c, :], in0=wide[:, (2 * c + 1) % RING, :],
                                             scalar=s2[:, c:c + 1], in1=full[:, c, :], op0=ALU.mult,
                                             op1=ALU.mult).then_inc(gated, 1)
                    dve.wait_ge(gated, nth(g, c))
                    halve(a1, c)
            gate(0)
            before = link.base
            LINKS = 2 * HC + 1

            def take_update(g):
                dve.wait_ge(out_done, g + 1)
                update.take(dve, out[:], s.x[:, at(g * TT, TT), :], g + 1)

            def period(g, first, last, make=True):
                link.start(before + g * LINKS)
                if first:
                    second_parts(1, raw_h2, h2)
                    second_parts(2, raw_w3, w3)
                for c in range(HC):
                    dve.wait_ge(h_act, nth_h(g, 0, c))
                    halve(a2, c)
                    if c == 0 and not last:
                        split_x(g + 1)
                if not last:
                    gate(g + 1)
                if first:
                    dve.wait_ge(counted, 1)
                    dve.tensor_reduce(verdict[:], out[:].rearrange("p t d -> p (t d)"), AX.X,
                                      ALU.add).then_inc(judged, 1)
                else:
                    take_update(g - 1)
                for c in range(HC):
                    dve.wait_ge(h_act, nth_h(g, 1, c))
                    halve(a3, c, True)
                    if c == 2 and not first:
                        update.finish(dve, (g - 1) * TT, g, False)
                    if c == 1 and make:
                        dve.wait_ge(factors, 8)
                        dve.wait_ge(turned_done, g + 2)
                        make_x(g + 2)
            period(0, True, False)
            with dve.Fori(1, STEPS - 2) as g:
                period(g, False, False)
            period(STEPS - 2, False, False, False)
            period(STEPS - 1, False, True, False)
            take_update(STEPS - 1)
            update.finish(dve, (STEPS - 1) * TT, STEPS, False)
            dve.wait_ge(update.done, STEPS)

        @block.tensor
        def _(pe):
            def turn(g):
                pe.wait_ge(normed, (g + 1) * TT)
                for t in range(TT):
                    ins = pe.transpose(turned[:, t * P:(t + 1) * P], xn[:, t, :], s.ident[:])
                ins.then_inc(turned_done, 1)

            def product(bank, weights, acts, passes, ready=None):
                K = len(acts)
                for k in range(K):
                    if ready:
                        pe.wait_ge(parts[k % 2], ready(k))
                    for i, (a, b) in enumerate(passes):
                        ins = pe.matmul(wide[:, bank % RING, :], weights[k][a], acts[k][b],
                                        start=(k == 0 and i == 0), stop=(k == K - 1 and i == len(passes) - 1))
                return ins

            def gates_of(g, c, passes):
                if c == 0:
                    pe.wait_ge(xT_done, g + 1)
                for i, v in enumerate((w1, w2)):
                    if c >= 2 and i == 0:
                        pe.wait_ge(w_act, nth(g, c - 2))
                    elif c >= 2:
                        pe.wait_ge(gated, nth(g, c - 2))
                    elif not (isinstance(g, int) and g == 0):
                        pe.wait_ge(h_act, nth_h(g - 1, 0, 2 * c + i))
                    product(2 * c + i, [[v[j][:, c * P:(c + 1) * P] for j in (0, 1)]],
                            [[xT[j][:] for j in (0, 1)]], passes).then_inc(w_prod, 1)

            def hidden(g, c, layer, passes, after_gates):
                h, a = (h2, a2) if layer else (h1, a1)
                if after_gates is None:
                    pe.wait_ge(h_act, nth_h(g, 0, c) if layer else nth_h(g - 1, 1, c))
                elif c % 2:
                    pe.wait_ge(gated, nth(after_gates, 2 + c // 2))
                else:
                    pe.wait_ge(w_act, nth(after_gates, 2 + c // 2))
                product(c, [[h[j][:, k, c * P:(c + 1) * P] for j in (0, 1)] for k in range(HC)],
                        [[a[j][:, k, :] for j in (0, 1)] for k in range(HC)], passes,
                        None if c else lambda k: (parts_a2 if layer else parts_a1)(g, k)).then_inc(h_prod, 1)

            def outward(g, passes):
                if not (isinstance(g, int) and g == 0):
                    pe.wait_ge(scaled, g)
                for k in range(HC):
                    pe.wait_ge(a3_parts, nth(g, k))
                    for i, (a, b) in enumerate(passes):
                        ins = pe.matmul(outT[:], w3[a][:, k, :], a3[b][:, k, :], start=(k == 0 and i == 0),
                                        stop=(k == HC - 1 and i == len(passes) - 1))
                ins.then_inc(outT_done, 1)

            def turn_back(g):
                pe.wait_ge(scaled, g + 1)
                if isinstance(g, int) and g == 0:
                    pe.wait_ge(judged, 1)
                else:
                    pe.wait_ge(update.read, g)
                for t in range(TT):
                    ins = pe.transpose(out[:, t, :], outT_sb[:, t * P:(t + 1) * P], s.ident[:])
                ins.then_inc(out_done, 1)

            def period(g, first, last, passes):
                if first:
                    pe.wait_ge(split, 3)
                for c in range(HC):
                    hidden(g, c, 0, passes, g if first else None)
                    if c == 0 and not last:
                        turn(g + 1)
                if not last:
                    gates_of(g + 1, 0, passes)
                    gates_of(g + 1, 1, passes)
                if first:
                    pe.wait_ge(split, 5)
                else:
                    outward(g - 1, passes)
                if not last:
                    gates_of(g + 1, 2, passes)
                    gates_of(g + 1, 3, passes)
                if first:
                    pe.wait_ge(ones_made, 1)
                    pe.wait_ge(flagged, 5)
                    for k in range(FLAGS):
                        ins = pe.matmul(out[:].rearrange("p t d -> p (t d)"), ones[:], flags[:, k, :],
                                        start=(k == 0), stop=(k == FLAGS - 1))
                    ins.then_inc(counted, 1)
                for c in range(HC):
                    hidden(g, c, 1, passes, None if last else g + 1)
                    if c == 1 and not first:
                        turn_back(g - 1)

            def rest(passes):
                with pe.Fori(1, STEPS - 1) as g:
                    period(g, False, False, passes)
                period(STEPS - 1, False, True, passes)
                outward(STEPS - 1, passes)
                turn_back(STEPS - 1)

            turn(0)
            pe.wait_ge(split, 2)
            for c in range(HC):
                gates_of(0, c, PARTS)
            period(0, True, False, PARTS)
            pe.wait_ge(judged, 1)
            second_parts = pe.value_load(verdict[0:1, :].bitcast(mybir.dt.int32))
            with pe.If(second_parts == 0):
                rest(tuple(p for p in PARTS if p[0] == 0))
            with pe.Else():
                rest(PARTS)


def xattn_large(nc, s, cT_dram, w):
    NH, B = 16, 64
    HD = w["q"].shape[1] // NH
    HP = NH // 2
    CD = cT_dram.shape[0]
    SCALE = float(HD) ** -0.5
    TS = 2
    WIDE = TS * P
    NB = WIDE // B
    UH, UP = NH // 2, HP // 2
    STEPS = s.tiles // TS
    with ExitStack() as ctx:
        def sb(n, shape, dt=F32):
            return ctx.enter_context(nc.sbuf_tensor("c_" + n, shape, dt))

        def ps(n, shape):
            return ctx.enter_context(nc.psum_tensor("c_" + n, shape, F32))

        def sem(n):
            return s.sem("c_" + n)

        raw = {n: sb("raw_" + n, [r, HP, P]) for n, r in (("q", D), ("k", CD), ("v", CD))}
        parts = {n: [sb(f"w{n}_{i}", [r, HP, P], F32R) for i in "01"] for n, r in (("q", D), ("k", CD), ("v", CD))}
        ob = sb("ob", [P, D])
        raw["o"], parts["o"] = sb("raw_o", [P, HP, D]), [sb(f"wo_{i}", [P, HP, D], F32R) for i in "01"]
        xn = sb("xn", [P, TS, D])
        xT = [sb(f"xT_{i}", [P, WIDE], F32R) for i in "01"]
        cT = [sb(f"cT{b}", [CD, TS, 3 * B]) for b in "01"]
        cp = [sb(f"c_{i}", [CD, TS, 3 * B], F32R) for i in "01"]
        q = [sb(f"q{b}", [P, HP, WIDE]) for b in "01"]
        kz = [sb(f"kz{b}", [P, HP, NB, 2 * B]) for b in "01"]
        vz = [[sb(f"vz{b}_{t}", [P, 2, HP, 2 * HD]) for t in "01"] for b in "01"]
        top, total, inv = (sb(n, [P, 2, UH]) for n in ("top", "total", "inv"))
        e = [sb(f"e{u}", [P, UH, B]) for u in "01"]
        eT = sb("eT", [P, UP, P])
        oT = [sb(f"oT_{i}", [P, HP, WIDE], F32R) for i in "01"]
        proj = sb("proj", [P, WIDE])
        update = Update(s, sb, "c_", TS)
        scores = [ps(f"scores{u}", [P, UH, B]) for u in "01"]
        turned_e, att = ps("turned_e", [P, UP, P]), ps("att", [P, UP, P])
        misc = ps("misc", [P, 4, TOK])
        XT, Q0, K0, PROJ, K1, BACK, V0 = 1, 2, 6, 7, 8, 11, 12

        def bank(job):
            return misc[:, job % 4, :]

        def k_bank(i):
            return bank(K0 if i == 0 else K1 + i - 1)

        w_in, vec_in = [sem(f"weights_in{i}") for i in range(3)], sem("vectors_in")
        c_in = [sem("ctx_in0"), sem("ctx_in1")]
        w_hi, w_split, made = sem("weights_hi"), sem("weights_split"), sem("zeros_made")
        factors, normed = s.factors["c"], sem("normed")
        turned, x_hi, x_split = sem("xn_turned"), sem("x_hi"), sem("x_split")
        c_hi, c_split = sem("c_hi"), sem("c_split")
        q_prod, q_out = sem("q_product"), sem("q_out")
        k_prod, k_act, k_dve = sem("k_product"), sem("k_out_act"), sem("k_out_dve")
        v_prod, v_act, v_dve = sem("v_product"), sem("v_out_act"), sem("v_out_dve")
        proj_done, proj_out, back_done = sem("projected"), sem("proj_out"), sem("proj_turned_back")
        scored, top_done, shifted, exped, summed, inv_done, softmaxed = (sem(n) for n in (
            "scored", "top_done", "shifted", "exped", "summed", "inv_done", "softmaxed"))
        e_turned, eT_out, attended, oT_hi, oT_split = (sem(n) for n in (
            "e_turned", "eT_out", "attended", "oT_hi", "oT_split"))
        block = ctx.enter_context(nc.Block())

        def bodies(eng, body, peeled=1, end=2):
            for g in range(peeled):
                body(g, g % 2, True, True)
            with eng.Fori(peeled // 2, (STEPS - end) // 2) as i:
                body(2 * i + 1, 1, True, True)
                body(2 * i + 2, 0, True, True)
            for g in range(STEPS + 1 - end, STEPS - 1):
                body(g, g % 2, True, True)
            body(STEPS - 1, 1, True, False)
            body(STEPS, 0, False, False)

        def unit_of(o, u):
            return o[:, u % 2 * UP:(u % 2 + 1) * UP, u // 2 * P:(u // 2 + 1) * P]

        def is0(g):
            return isinstance(g, int) and g == 0

        @block.sync
        def _(sp):
            def fetch(g, b):
                src = cT_dram[:, at(g * WIDE, WIDE)].rearrange("c (t k) -> c t k", k=P)
                sp.dma_start(cT[b][:, :, 0:P], src).then_inc(c_in[b], 16)
                sp.dma_start(cT[b][:, :, P:P + B], src[:, :, 0:B]).then_inc(c_in[b], 16)
            for i, n in enumerate(("q", "k", "v")):
                sp.dma_start(raw[n][:], w[n].rearrange("c (t d) -> c t d", d=P)).then_inc(w_in[i], 16)
                if i == 0:
                    fetch(0, 0)
            sp.dma_start(raw["o"][:], w["o"].rearrange("(k p) o -> p k o", p=P)).then_inc(vec_in, 16)
            sp.dma_start(ob[:], rows(w["ob"], D)).then_inc(vec_in, 16)

            def body(g, b, here, after):
                if after:
                    if not is0(g):
                        sp.wait_ge(c_split, g)
                    fetch(g + 1, 1 - b)
            bodies(sp, body)

        @block.gpsimd
        def _(pool):
            for b in (0, 1):
                pool.memset(kz[b][:], 0.0).then_inc(made, 1)
                for t in (0, 1):
                    pool.memset(vz[b][t][:], 0.0).then_inc(made, 1)
                if b == 0:
                    norm_factors(pool, s, factors, LATER, 4)

            def softmax_scale(n, u):
                pool.wait_ge(inv_done, n + 1)
                by = inv[:, u].rearrange("p (h a) -> p h a", a=1).broadcast_to([P, UH, B])
                pool.tensor_tensor(e[u][:], e[u][:], by, ALU.mult).then_inc(softmaxed, 1)

            def body(g, b, here, after):
                for p in range(4):
                    if (here or p == 0) and not (is0(g) and p == 0):
                        softmax_scale(4 * g + p - 1, (p + 1) % 2)
            bodies(pool, body)
            next_factors(pool, s, "d", update, TS)

        @block.scalar
        def _(act):
            def c_round(g, b):
                act.wait_ge(c_in[b], (g - b) * 16 + 32)
                if not is0(g):
                    act.wait_ge(v_prod, 4 * g)
                act.activation(cp[0][:], cT[b][:], ACT.Copy).then_inc(c_hi, 1)

            def q_evacuate(g, b, i):
                act.wait_ge(q_prod, 4 * g + i + 1)
                act.activation(q[b][:, 2 * i:2 * i + 2, :], bank(Q0 + i).rearrange("p (t k) -> p t k", t=2),
                               ACT.Copy, scale=SCALE).then_inc(q_out, 1)

            def k_evacuate(g, b, i):
                if isinstance(g, int) and g == 1 and i == 0:
                    act.wait_ge(made, 6)
                act.wait_ge(k_prod, 4 * g + i + 1)
                src = k_bank(i).rearrange("p (t b o k) -> p t b o k", t=2, o=2, k=B)
                for o in (0, 1):
                    dst = kz[b][0:HD, 2 * i:2 * i + 2, o::2, o * B:(o + 1) * B]
                    ins = act.activation(dst, src[0:HD, :, :, o, :], ACT.Copy)
                ins.then_inc(k_act, 1)

            def v_evacuate(g, b, i):
                act.wait_ge(v_prod, 4 * g + i + 1)
                odd = i % 2
                act.activation(vz[b][i // 2][0:B, odd, :, odd * HD:(odd + 1) * HD],
                               bank(V0 + i)[0:B, :].rearrange("p (t d) -> p t d", d=HD), ACT.Copy).then_inc(v_act, 1)

            def eT_evacuate(m):
                act.wait_ge(e_turned, m + 1)
                act.activation(eT[:], turned_e[:], ACT.Copy).then_inc(eT_out, 1)

            def oT_round(m, u):
                act.wait_ge(attended, m + 1)
                act.activation(unit_of(oT[0], u), att[:], ACT.Copy).then_inc(oT_hi, 1)

            def proj_evacuate(g):
                act.wait_ge(proj_done, g + 1)
                act.activation(proj[:], bank(PROJ)[:, 0:WIDE], ACT.Copy).then_inc(proj_out, 1)

            def exp(n, u):
                act.wait_ge(shifted, n + 1)
                act.activation(e[u][:], e[u][:], ACT.Exp).then_inc(exped, 1)

            c_round(0, 0)
            for i in range(4):
                q_evacuate(0, 0, i)
            act.wait_ge(made, 3)
            for i in range(4):
                k_evacuate(0, 0, i)
            for i in range(4):
                v_evacuate(0, 0, i)

            def body(g, b, here, after):
                for p in range(4):
                    n = 4 * g + p
                    behind = (not is0(g) or p >= 2) and (here or p < 2)
                    if p == 0 and after:
                        c_round(g + 1, 1 - b)
                    if behind:
                        eT_evacuate(n - 2)
                    if after:
                        for kind, i in SLOTS[p]["a"] + SLOTS[p]["b"]:
                            {"q": q_evacuate, "k": k_evacuate, "v": v_evacuate}.get(kind, lambda *_: None)(
                                g + 1, 1 - b, i)
                    if here:
                        exp(n, p % 2)
                    if behind:
                        oT_round(n - 2, (p + 2) % 4)
                    if p == 2 and not is0(g):
                        proj_evacuate(g - 1)
                    if after:
                        for kind, i in SLOTS[p]["c"]:
                            {"q": q_evacuate, "k": k_evacuate, "v": v_evacuate}[kind](g + 1, 1 - b, i)
            bodies(act, body)

        @block.vector
        def _(dve):
            def split_weights(n, name):
                dve.wait_ge(w_in[n], 16)
                split(dve, parts[name][0][:], parts[name][1][:], raw[name][:], w_hi, n + 1, w_split)

            def x_parts(g, b, i):
                dve.wait_ge(turned, g + 1)
                split(dve, xT[0][:], xT[1][:], bank(XT)[:, 0:WIDE], x_hi, g + 1, x_split)

            def c_low(g, b):
                dve.wait_ge(c_hi, g + 1)
                dve.tensor_tensor(cp[1][:], cT[b][:], cp[0][:].bitcast(F32), ALU.subtract).then_inc(c_split, 1)

            def k_evacuate(g, b, i):
                if isinstance(g, int) and g == 1 and i == 0:
                    dve.wait_ge(made, 6)
                dve.wait_ge(k_prod, 4 * g + i + 1)
                src = k_bank(i).rearrange("p (t b o k) -> p t b o k", t=2, o=2, k=B)
                for o in (0, 1):
                    dst = kz[b][HD:P, 2 * i:2 * i + 2, o::2, (1 - o) * B:(2 - o) * B]
                    ins = dve.tensor_copy(dst, src[HD:P, :, :, o, :])
                ins.then_inc(k_dve, 1)

            def v_evacuate(g, b, i):
                dve.wait_ge(v_prod, 4 * g + i + 1)
                odd = i % 2
                dve.tensor_copy(vz[b][i // 2][B:P, 1 - odd, :, odd * HD:(odd + 1) * HD],
                                bank(V0 + i)[B:P, :].rearrange("p (t d) -> p t d", d=HD)).then_inc(v_dve, 1)

            def softmax_shift(n, u):
                dve.wait_ge(scored, n + 1)
                dve.tensor_reduce(top[:, u], scores[u][:], AX.X, ALU.max).then_inc(top_done, 1)
                dve.wait_ge(top_done, n + 1)
                if not (isinstance(n, int) and n < 2):
                    dve.wait_ge(e_turned, n - 1)
                peak = top[:, u].rearrange("p (h a) -> p h a", a=1).broadcast_to([P, UH, B])
                dve.tensor_tensor(e[u][:], scores[u][:], peak, ALU.subtract).then_inc(shifted, 1)

            def softmax_sum(n, u):
                dve.wait_ge(exped, n + 1)
                dve.tensor_reduce(total[:, u], e[u][:], AX.X, ALU.add).then_inc(summed, 1)
                dve.wait_ge(summed, n + 1)
                dve.reciprocal(inv[:, u], total[:, u]).then_inc(inv_done, 1)

            def oT_low(m, u):
                dve.wait_ge(oT_hi, m + 1)
                dve.tensor_tensor(unit_of(oT[1], u), att[:], unit_of(oT[0], u).bitcast(F32),
                                  ALU.subtract).then_inc(oT_split, 1)

            def x_take(g):
                dve.wait_ge(back_done, g + 1)
                update.take(dve, bank(BACK)[:, 0:WIDE].rearrange("p (t d) -> p t d", t=TS),
                            ob[:].rearrange("p (a d) -> p a d", a=1).broadcast_to([P, TS, D]), g + 1)

            dve.wait_ge(factors, 4)
            normalise(dve, s, xn, 0, TS, normed)
            split_weights(0, "q")
            x_parts(0, 0, 0)
            c_low(0, 0)
            split_weights(1, "k")
            split_weights(2, "v")
            dve.wait_ge(made, 3)
            for i in range(4):
                k_evacuate(0, 0, i)
            for i in range(4):
                v_evacuate(0, 0, i)
            dve.wait_ge(turned, 1)
            normalise(dve, s, xn, TS, TS, normed)
            dve.wait_ge(vec_in, 32)
            split(dve, parts["o"][0][:], parts["o"][1][:], raw["o"][:], w_hi, 4, w_split)

            def jobs(g, b, slot, after):
                for kind, i in slot:
                    if kind == "back":
                        if not is0(g):
                            x_take(g - 1)
                    elif after and kind in "kvx":
                        {"k": k_evacuate, "v": v_evacuate, "x": x_parts}[kind](g + 1, 1 - b, i)

            def body(g, b, here, after):
                for p in range(4):
                    n = 4 * g + p
                    if (here or p == 0) and not (is0(g) and p == 0):
                        softmax_sum(n - 1, (p + 1) % 2)
                    jobs(g, b, SLOTS[p]["a"], after)
                    if here:
                        softmax_shift(n, p % 2)
                    if p == 1 and after:
                        c_low(g + 1, 1 - b)
                    jobs(g, b, SLOTS[p]["b"], after)
                    if p == 2 and after and not (isinstance(g, int) and g == STEPS - 2):
                        if not is0(g):
                            dve.wait_ge(factors, 8)
                        dve.wait_ge(turned, g + 2)
                        normalise(dve, s, xn, (g + 2) * TS, TS, normed)
                    if p == 1 and not (isinstance(g, int) and g < 2):
                        update.finish(dve, (g - 2) * TS, g - 1)
                    if (not is0(g) or p >= 2) and (here or p < 2):
                        oT_low(n - 2, (p + 2) % 4)
                    jobs(g, b, SLOTS[p]["c"], after)
            bodies(dve, body, 3, 4)
            update.finish(dve, (STEPS - 1) * TS, STEPS)
            dve.wait_ge(update.done, STEPS)

        @block.tensor
        def _(pe):
            def both(act_sem, dve_sem, count):
                pe.wait_ge(act_sem, count)
                pe.wait_ge(dve_sem, count)

            def turn_x(g, b, i, start=False):
                if not start:
                    both(v_act, v_dve, 4 * g - 2)
                pe.wait_ge(normed, (g + 1) * TS)
                for t in range(TS):
                    ins = pe.transpose(bank(XT)[:, t * P:(t + 1) * P], xn[:, t, :], s.ident[:])
                ins.then_inc(turned, 1)

            def make_q(g, b, i, start=False):
                if i == 3:
                    pe.wait_ge(x_split, g + 1)
                elif not start:
                    both(v_act, v_dve, 4 * g)
                pe.wait_ge(x_split, g + 1)
                for j in range(2):
                    for k, (a, c) in enumerate(PARTS):
                        ins = pe.matmul(bank(Q0 + i)[:, j * WIDE:(j + 1) * WIDE], parts["q"][a][:, 2 * i + j, :],
                                        xT[c][:], start=(k == 0), stop=(k == 2))
                ins.then_inc(q_prod, 1)

            def make_k(g, b, i, start=False):
                if i < 3:
                    pe.wait_ge(q_out, 4 * g + (1, 3, 4)[i])
                else:
                    both(k_act, k_dve, 4 * g + 1)
                pe.wait_ge(c_split, g + 1)
                for j in range(2):
                    for k, (a, c) in enumerate(PARTS):
                        ins = pe.matmul(k_bank(i)[:, j * WIDE:(j + 1) * WIDE], parts["k"][a][:, 2 * i + j, :],
                                        cp[c][:, :, 0:P], start=(k == 0), stop=(k == 2))
                ins.then_inc(k_prod, 1)

            def make_v(g, b, i, start=False):
                if i < 3:
                    both(k_act, k_dve, 4 * g + i + 2)
                elif start or is1(g):
                    pe.wait_ge(q_out, 4 * g + 2)
                else:
                    pe.wait_ge(update.read, g - 1)
                t, odd = i // 2, i % 2
                for k, (a, c) in enumerate(PARTS):
                    ins = pe.matmul(bank(V0 + i), cp[c][:, t, odd * B:odd * B + P],
                                    parts["v"][a][:, :, odd * HD:(odd + 1) * HD], start=(k == 0), stop=(k == 2))
                ins.then_inc(v_prod, 1)

            def project(g):
                pe.wait_ge(oT_split, 4 * g + 4)
                for k in range(HP):
                    for n, (a, c) in enumerate(PARTS):
                        ins = pe.matmul(bank(PROJ)[:, 0:WIDE], parts["o"][a][:, k, :], oT[c][:, k, :],
                                        start=(k == 0 and n == 0), stop=(k == HP - 1 and n == 2))
                ins.then_inc(proj_done, 1)

            def turn_back(g):
                pe.wait_ge(proj_out, g + 1)
                for t in range(TS):
                    ins = pe.transpose(bank(BACK)[:, t * P:(t + 1) * P], proj[:, t * P:(t + 1) * P], s.ident[:])
                ins.then_inc(back_done, 1)

            def is1(g):
                return isinstance(g, int) and g == 1

            def score(g, b, p, n):
                if not (isinstance(n, int) and n < 2):
                    pe.wait_ge(shifted, n - 1)
                t, hh = p // 2, p % 2
                for j in range(UP):
                    for half in (0, 1):
                        h = hh * UP + j
                        ins = pe.matmul(
                            scores[p % 2][half * B:(half + 1) * B, 2 * j:2 * j + 2, :].rearrange("q h k -> q (h k)"),
                            q[b][:, h, t * P + half * B:t * P + (half + 1) * B], kz[b][:, h, 2 * t + half, :],
                            start=True, stop=True)
                ins.then_inc(scored, 1)

            def turn_e(m, u):
                pe.wait_ge(softmaxed, m + 1)
                for j in range(UP):
                    ins = pe.transpose(turned_e[:, j, :], e[u][:, 2 * j:2 * j + 2, :].rearrange("q h k -> q (h k)"),
                                       s.ident[:])
                ins.then_inc(e_turned, 1)

            def attend(m, b, p):
                pe.wait_ge(eT_out, m + 1)
                if not (isinstance(m, int) and m == 0):
                    pe.wait_ge(oT_split, m)
                for j in range(UP):
                    for half in (0, 1):
                        ins = pe.matmul(att[:, j, half * B:(half + 1) * B],
                                        vz[b][p // 2][:, half, (p % 2) * UP + j, :],
                                        eT[:, j, half * B:(half + 1) * B], start=True, stop=True)
                ins.then_inc(attended, 1)

            make = {"x": turn_x, "q": make_q, "k": make_k, "v": make_v}
            turn_x(0, 0, 0, True)
            for n, kind in enumerate("qkv"):
                pe.wait_ge(w_split, n + 1)
                for i in range(4):
                    make[kind](0, 0, i, True)
            pe.wait_ge(w_split, 4)

            def jobs(g, b, slot, here, after):
                for kind, i in slot:
                    if kind == "proj":
                        if not is0(g):
                            if after:
                                pe.wait_ge(q_out, 4 * (g + 1) + 2)
                            elif here:
                                both(v_act, v_dve, 4 * g + 4)
                            else:
                                pe.wait_ge(update.read, g - 1)
                            project(g - 1)
                    elif kind == "back":
                        if not is0(g):
                            turn_back(g - 1)
                    elif after:
                        make[kind](g + 1, 1 - b, i)

            def body(g, b, here, after):
                for p in range(4):
                    n = 4 * g + p
                    behind = (not is0(g) or p >= 2) and (here or p < 2)
                    mb = b if p >= 2 else 1 - b
                    if behind:
                        turn_e(n - 2, p % 2)
                    jobs(g, b, SLOTS[p]["a"], here, after)
                    if here:
                        if p == 0:
                            pe.wait_ge(q_out, 4 * g + 4)
                            both(k_act, k_dve, 4 * g + 4)
                        score(g, b, p, n)
                    jobs(g, b, SLOTS[p]["b"], here, after)
                    if behind:
                        if p == 2 and here:
                            both(v_act, v_dve, 4 * g + 4)
                        attend(n - 2, mb, (p + 2) % 4)
                    jobs(g, b, SLOTS[p]["c"], here, after)
            bodies(pe, body)


SLOTS = (
    {"a": (("x", 0),), "b": (), "c": (("q", 0),)},
    {"a": (("q", 1),), "b": (("q", 2),), "c": (("q", 3),)},
    {"a": (("k", 0),), "b": (("proj", 0), ("k", 1)), "c": (("k", 2),)},
    {"a": (("k", 3),), "b": (("back", 0), ("v", 0), ("v", 1)), "c": (("v", 2), ("v", 3))},
)


def ffn_expert(nc, s, w, y_dram):
    H = w["w1"].shape[1]
    HC = H // P
    STEPS = s.tiles // TT
    with ExitStack() as ctx:
        def sb(n, shape, dt=F32):
            return ctx.enter_context(nc.sbuf_tensor("d_" + n, shape, dt))

        def ps(n, shape):
            return ctx.enter_context(nc.psum_tensor("d_" + n, shape, F32))

        def sem(n):
            return s.sem("d_" + n)

        raw1 = sb("raw1", [P, H])
        w1 = [sb(f"w1_{i}", [P, H], F32R) for i in "01"]
        w2, b1 = sb("w2", [P, HC, D]), sb("b1", [P, HC])
        b2, gamma, beta = sb("b2", [P, D]), sb("gamma", [P, D]), sb("beta", [P, D])
        power, eps, zero = sb("power", [P, TT]), sb("eps", [P, TT]), sb("zero", [P, TT])
        xn, xb = sb("xn", [P, 2, TT, D]), sb("xn_plus_b2", [P, 2, TT, D])
        xT = [sb(f"xT_{i}", [P, TOK], F32R) for i in "01"]
        a = sb("a", [P, HC, TOK])
        z = sb("z", [P, 2, TT, D])
        stats, moments = sb("stats", [P, TT, 6]), sb("step_moments", [P, 2, TT, 2])
        variance, product = sb("step_variance", [P, TT]), sb("step_product", [P, TT])
        rstd, shift = sb("step_rstd", [P, 2, TT]), sb("step_shift", [P, 2, TT])
        y = sb("y", [P, 2, TT, D])
        wide, turned, out = ps("wide", [P, HC, TOK]), ps("turned", [P, TOK]), ps("out", [P, 2, TT, D])
        yv = y_dram.rearrange("(t p) d -> p t d", p=P)

        w_in, vec_in, split = sem("weights_in"), sem("vectors_in"), sem("weights_split")
        factors, normed = s.factors["d"], sem("normed")
        turned_done, xT_hi, xT_done = sem("turned_done"), sem("xT_hi"), sem("xT_done")
        prod, act_out = sem("products"), sem("act_out")
        out_done = sem("out_done")
        xb_done = sem("xb_done")
        z_added, z_done = sem("z_added"), sem("z_done")
        shift_done, made = sem("shift_done"), sem("constants_made")
        pool_chain, chain = sem("pool_chain"), sem("dve_chain")
        scaled, times_gamma, plus_beta, y_done = (sem(n) for n in ("scaled", "times_gamma", "plus_beta", "y_done"))
        stored = [sem("stored0"), sem("stored1")]
        block = ctx.enter_context(nc.Block())

        def pairs(eng, step):
            for g in range(4):
                step(g, g % 2, g == 0, False)
            with eng.Fori(4, STEPS - 2, 2) as g:
                step(g, 0, False, False)
                step(g + 1, 1, False, False)
            step(STEPS - 2, 0, False, False)
            step(STEPS - 1, 1, False, True)

        @block.sync
        def _(sp):
            sp.dma_start(raw1[:], w["w1"]).then_inc(w_in, 16)
            sp.dma_start(w2[:], w["w2"].rearrange("(k p) o -> p k o", p=P)).then_inc(vec_in, 16)
            sp.dma_start(b1[:], w["b1"]).then_inc(vec_in, 16)
            for v, n in ((b2, "b2"), (gamma, "gamma"), (beta, "beta")):
                sp.dma_start(v[:], rows(w[n], D)).then_inc(vec_in, 16)

            def step(g, b, first, last):
                sp.wait_ge(y_done, g + 1)
                sp.dma_start(yv[:, at(g * TT, TT), :], y[:, b]).then_inc(stored[b], 16)
            pairs(sp, step)
            for b in (0, 1):
                sp.wait_ge(stored[b], 16 * (STEPS // 2))

        @block.gpsimd
        def _(pool):
            for tile, value in ((power, -0.5), (eps, EPS), (zero, 0.0)):
                pool.memset(tile[:], value).then_inc(made, 1)
            norm_factors(pool, s, factors, LATER, 4)
            pool.wait_ge(made, 3)
            link = Chain(pool, pool_chain)

            def bcast(v):
                return v[:].rearrange("p (a d) -> p a d", a=1).broadcast_to([P, TT, D])

            def add_b2(g, b):
                pool.wait_ge(normed, (g + 1) * TT)
                if not (isinstance(g, int) and g < 2):
                    pool.wait_ge(z_added, g - 1)
                pool.tensor_tensor(xb[:, b], xn[:, b], bcast(b2), ALU.add).then_inc(xb_done, 1)

            def affine(g, b):
                pool.wait_ge(scaled, g + 1)
                pool.tensor_tensor(y[:, b], y[:, b], bcast(gamma), ALU.mult).then_inc(times_gamma, 1)
                pool.wait_ge(times_gamma, g + 1)
                pool.tensor_tensor(y[:, b], y[:, b], bcast(beta), ALU.add).then_inc(plus_beta, 1)

            def step(g, b, first, last):
                if not last:
                    add_b2(g + 1, 1 - b)
                link.start(g * 3)
                pool.wait_ge(z_done, g + 1)
                if not (isinstance(g, int) and g < 2):
                    pool.wait_ge(scaled, g - 1)
                link.then(pool.tensor_tensor(variance[:], moments[:, b, :, 1], eps[:], ALU.add))
                link.then(pool.tensor_tensor(rstd[:, b], variance[:], power[:], ALU.pow))
                link.then(pool.tensor_tensor(product[:], moments[:, b, :, 0], rstd[:, b], ALU.mult))
                pool.tensor_tensor(shift[:, b], zero[:], product[:], ALU.subtract).then_inc(shift_done, 1)
                if not first:
                    affine(g - 1, 1 - b)
            pool.wait_ge(vec_in, 16 * 5)
            add_b2(0, 0)
            pairs(pool, step)
            affine(STEPS - 1, 1)

        @block.scalar
        def _(act):
            def first_part(g):
                act.wait_ge(turned_done, g + 1)
                act.activation(xT[0][:], turned[:], ACT.Copy).then_inc(xT_hi, 1)
            first_part(0)
            act.wait_ge(vec_in, 16 * 5)

            def step(g, b, first, last):
                for c in range(HC):
                    act.wait_ge(prod, g * HC + c + 1)
                    if c == 0 and not first:
                        act.wait_ge(out_done, g)
                    act.activation(a[:, c, :], wide[:, c, :], ACT.Relu, bias=b1[:, c:c + 1]).then_inc(act_out, 1)
                if not last:
                    first_part(g + 1)
            pairs(act, step)

        @block.vector
        def _(dve):
            link = Chain(dve, chain)

            def split_x(g):
                dve.wait_ge(xT_hi, g + 1)
                dve.tensor_tensor(xT[1][:], turned[:], xT[0][:].bitcast(F32), ALU.subtract).then_inc(xT_done, 1)
            dve.wait_ge(factors, 4)
            normalise(dve, s, xn[:, 0], 0, TT, normed)
            dve.wait_ge(w_in, 16)
            link.then(dve.tensor_copy(w1[0][:], raw1[:]))
            dve.tensor_tensor(w1[1][:], raw1[:], w1[0][:].bitcast(F32), ALU.subtract).then_inc(split, 1)
            split_x(0)
            dve.wait_ge(factors, 8)
            dve.wait_ge(vec_in, 16 * 5)
            before = link.base

            def make_x(g, b):
                if not (isinstance(g, int) and g < 2):
                    dve.wait_ge(turned_done, g - 1)
                    dve.wait_ge(xb_done, g - 1)
                normalise(dve, s, xn[:, b], g * TT, TT, normed)

            def make_z(g, b, meanwhile):
                dve.wait_ge(xb_done, g + 1)
                if not (isinstance(g, int) and g < 2):
                    dve.wait_ge(scaled, g - 1)
                dve.wait_ge(out_done, g + 1)
                dve.tensor_tensor(z[:, b], out[:, b], xb[:, b], ALU.add).then_inc(z_added, 1)
                dve.wait_ge(z_added, g + 1)
                for t in range(TT):
                    ins = dve.bn_stats(stats[:, t, :], z[:, b, t, :])
                link.then(ins)
                meanwhile()
                for t in range(TT):
                    ins = dve.bn_aggr(moments[:, b, t, :], stats[:, t, :])
                ins.then_inc(z_done, 1)

            def scale(g, b):
                dve.wait_ge(shift_done, g + 1)
                if not (isinstance(g, int) and g < 2):
                    dve.wait_ge(stored[b], (g - b) * 8)
                for t in range(TT):
                    ins = dve.tensor_scalar(y[:, b, t, :], z[:, b, t, :], rstd[:, b, t:t + 1],
                                            shift[:, b, t:t + 1], ALU.mult, ALU.add)
                ins.then_inc(scaled, 1)

            def add_x(g, b):
                dve.wait_ge(plus_beta, g + 1)
                dve.tensor_tensor(y[:, b], y[:, b], s.x[:, at(g * TT, TT), :], ALU.add).then_inc(y_done, 1)

            def step(g, b, first, last):
                if not last:
                    make_x(g + 1, 1 - b)
                link.start(before + (0 if first else g - 1))
                if not first:
                    make_z(g - 1, 1 - b, (lambda: None) if isinstance(g, int) and g == 1 else lambda: scale(g - 2, b))
                if not last:
                    split_x(g + 1)
                if not (isinstance(g, int) and g < 3):
                    add_x(g - 3, 1 - b)
            pairs(dve, step)
            add_x(STEPS - 3, 1)
            link.start(before + STEPS - 1)
            make_z(STEPS - 1, 1, lambda: scale(STEPS - 2, 0))
            add_x(STEPS - 2, 0)
            scale(STEPS - 1, 1)
            add_x(STEPS - 1, 1)
            dve.wait_ge(y_done, STEPS)

        @block.tensor
        def _(pe):
            def turn(g, b):
                pe.wait_ge(normed, (g + 1) * TT)
                for t in range(TT):
                    ins = pe.transpose(turned[:, t * P:(t + 1) * P], xn[:, b, t, :], s.ident[:])
                ins.then_inc(turned_done, 1)
            turn(0, 0)
            pe.wait_ge(split, 1)

            def step(g, b, first, last):
                pe.wait_ge(xT_done, g + 1)
                for c in range(HC):
                    if not first:
                        pe.wait_ge(act_out, (g - 1) * HC + c + 1)
                    for i, (p, q) in enumerate(PARTS):
                        ins = pe.matmul(wide[:, c, :], w1[p][:, c * P:(c + 1) * P], xT[q][:],
                                        start=(i == 0), stop=(i == 2))
                    ins.then_inc(prod, 1)
                if not last:
                    turn(g + 1, 1 - b)
                if first:
                    pe.wait_ge(vec_in, 16 * 5)
                if not (isinstance(g, int) and g < 2):
                    pe.wait_ge(z_done, g - 1)
                for t in range(TT):
                    for k in range(HC):
                        if t == 0:
                            pe.wait_ge(act_out, g * HC + k + 1)
                        ins = pe.matmul(out[:, b, t, :], a[:, k, t * P:(t + 1) * P], w2[:, k, :],
                                        start=(k == 0), stop=(k == HC - 1))
                ins.then_inc(out_done, 1)
            pairs(pe, step)


def attention_stack(nc, a, y):
    with ExitStack() as ctx:
        s = Stream(nc, ctx, a["x"].shape[0])
        load_stream(nc, s, a["x"])
        xattn_small(nc, s, a["x"], a["ctxT"], dict(q=a["q0_w"], qb=a["q0_b"], kv=a["kv0_w"], kb=a["k0_b"], vb=a["v0_b"],
                                                    o=a["o0_w"], ob=a["o0_b"]))
        ffn_gated(nc, s, dict(w1=a["w1"], w2=a["w2"], h1=a["h1"], h2=a["h2"], w3=a["w3"], w1s=a["w1_s"],
                              w2s=a["w2_s"], h1s=a["h1_s"], h2s=a["h2_s"], w3s=a["w3_s"]))
        xattn_large(nc, s, a["ctxT"], dict(q=a["q1_w"], k=a["k1_w"], v=a["v1_w"], o=a["o1_w"], ob=a["o1_b"]))
        ffn_expert(nc, s, dict(w1=a["e_w1"], b1=a["e_b1"], w2=a["e_w2"], b2=a["e_b2"], gamma=a["gamma"],
                               beta=a["beta"]), y)


def kernel(x, ctx_768, L0_xattn_q_w, L0_xattn_q_b, L0_xattn_kv_w, L0_xattn_kv_b, L0_xattn_proj_w, L0_xattn_proj_b,
           L0_ffn_w1_w, L0_ffn_w1_s, L0_ffn_w2_w, L0_ffn_w2_s, L0_ffn_h1_w, L0_ffn_h1_s, L0_ffn_h2_w, L0_ffn_h2_s,
           L0_ffn_w3_w, L0_ffn_w3_s, L1_xattn_w_q, L1_xattn_w_k, L1_xattn_w_v, L1_xattn_w_out, L1_xattn_b_out,
           L1_ffn_router_w, L1_ffn_router_b, L1_ffn_w1, L1_ffn_b1, L1_ffn_w2, L1_ffn_b2, L1_ffn_gamma,
           L1_ffn_beta):
    import numpy as np
    import concourse.bacc as bacc
    from concourse.bass_utils import run_bass_kernel_spmd

    def by_chunk(v):
        return np.asarray(v).reshape(-1, P).T

    batches, length, width = x.shape
    tokens = batches * length
    operands = {
        "x": np.asarray(x).reshape(tokens, width),
        "ctxT": np.asarray(ctx_768).reshape(tokens, -1).T,
        "q0_w": L0_xattn_q_w, "q0_b": by_chunk(L0_xattn_q_b), "kv0_w": L0_xattn_kv_w,
        "k0_b": by_chunk(np.asarray(L0_xattn_kv_b)[:width]), "v0_b": np.asarray(L0_xattn_kv_b)[width:],
        "o0_w": L0_xattn_proj_w, "o0_b": L0_xattn_proj_b,
        "w1": np.asarray(L0_ffn_w1_w).T, "w1_s": by_chunk(L0_ffn_w1_s),
        "w2": np.asarray(L0_ffn_w2_w).T, "w2_s": by_chunk(L0_ffn_w2_s),
        "h1": np.asarray(L0_ffn_h1_w).T, "h1_s": by_chunk(L0_ffn_h1_s),
        "h2": np.asarray(L0_ffn_h2_w).T, "h2_s": by_chunk(L0_ffn_h2_s),
        "w3": np.asarray(L0_ffn_w3_w).T, "w3_s": L0_ffn_w3_s,
        "q1_w": L1_xattn_w_q, "k1_w": L1_xattn_w_k, "v1_w": L1_xattn_w_v, "o1_w": L1_xattn_w_out,
        "o1_b": L1_xattn_b_out,
        "e_w1": np.asarray(L1_ffn_w1)[0], "e_b1": by_chunk(np.asarray(L1_ffn_b1)[0]),
        "e_w2": np.asarray(L1_ffn_w2)[0], "e_b2": np.asarray(L1_ffn_b2)[0],
        "gamma": L1_ffn_gamma, "beta": L1_ffn_beta,
    }
    nc = bacc.Bacc("TRN2", target_bir_lowering=False, num_devices=1)
    arrays, aps = {}, {}
    for name, a in operands.items():
        arrays[f"in_{name}"] = np.ascontiguousarray(a)
        aps[name] = nc.dram_tensor(f"in_{name}", list(arrays[f"in_{name}"].shape), F32, kind="ExternalInput").ap()
    y = nc.dram_tensor("out_y", [tokens, width], F32, kind="ExternalOutput").ap()
    attention_stack(nc, aps, y)
    result = run_bass_kernel_spmd(nc, [arrays], core_ids=[0])
    return result.results[0]["out_y"].reshape(batches, length, width)
```
